# Optimizing a Trainium2 kernel written in Bass

```python
import numpy as np
import jax
import jax.numpy as jnp

def _softmax(x, axis=-1):
    return jax.nn.softmax(x, axis=axis)

def _gelu(x):
    return jax.nn.gelu(x, approximate=True)

def _silu(x):
    return jax.nn.silu(x)

def _sigmoid(x):
    return jax.nn.sigmoid(x)

def _layernorm(x, axis=-1, eps=1e-05):
    m = jnp.mean(x, axis=axis, keepdims=True)
    v = jnp.var(x, axis=axis, keepdims=True)
    return (x - m) / jnp.sqrt(v + eps)

def _scatter_add(tgt, idx, src, axis=0):
    return tgt.at[idx].add(src)

def _segment_sum(src, seg, n):
    return jax.ops.segment_sum(src, seg, n)
kernel_name = 'mk_xattn_ffn_d2_seqx_r4_8c0225'

def setup_inputs(seed: int=0):
    np.random.seed(seed)
    _w = jnp.asarray

    def _rec_inputs():
        import jax
        import jax.numpy as jnp
        _rk = jax.random.key(seed)
        x = 7.22e-05 + 1 * jax.random.normal(jax.random.fold_in(_rk, 1), (8, 256, 512), jnp.float32)
        _lenS = 256 - jax.random.randint(jax.random.fold_in(_rk, 7), (8,), 0, max(1, 256 // 4) + 1, jnp.int32)
        _lenS2 = 256 - jax.random.randint(jax.random.fold_in(_rk, 8), (8,), 0, max(1, 256 // 4) + 1, jnp.int32)
        _ctx_512P = jax.random.normal(jax.random.fold_in(_rk, 11), (8, 16, 128), jnp.float32)
        _ctx_512c = jax.random.dirichlet(jax.random.fold_in(_rk, 511), 0.3 * jnp.ones((16,), jnp.float32), (8, 256))
        _ctx_512t = jnp.einsum('bsk,bkd->bsd', _ctx_512c, _ctx_512P)
        _ctx_512t = _ctx_512t * jax.lax.rsqrt(jnp.mean(jnp.square(_ctx_512t)) + 1e-12) * 0.953939
        ctx_512 = -0.000514642 + 1.00011 * (_ctx_512t + 0.3 * jax.random.normal(jax.random.fold_in(_rk, 611), (8, 256, 128), jnp.float32))
        return (x, ctx_512)
    x, ctx_512 = _rec_inputs()

    def _L0_xattn_setup():
        import jax, jax.numpy as jnp
        import numpy as np
        B, S, H, NH, L = (2, 512, 512, 16, 128)
        HD = H // NH
        key = jax.random.key(seed)
        k1, k2, k3, k4, k5 = jax.random.split(key, 5)
        scale = 0.02
        return {'q': jax.random.normal(k1, (B, S, H), dtype=jnp.float32), 'latent_kv': jax.random.normal(k2, (B, S, L), dtype=jnp.float32), 'Wq': jax.random.normal(k3, (H, H), dtype=jnp.float32) * scale, 'Wkv_expand': jax.random.normal(k4, (2 * H, L), dtype=jnp.float32) * scale, 'Wout': jax.random.normal(k5, (H, H), dtype=jnp.float32) * scale}
    _L0_xattn_all = _L0_xattn_setup()
    _L0_xattn_in = {k: v for k, v in _L0_xattn_all.items() if k in ('Wq', 'Wkv_expand', 'Wout')}
    del _L0_xattn_all

    def _L0_ffn_setup():
        import jax, jax.numpy as jnp
        import numpy as np
        D_MODEL = 512
        D_FF = 2048

        def _act_quant(x):
            scale = 127.0 / jnp.clip(jnp.max(jnp.abs(x), axis=-1, keepdims=True), 1e-05)
            xq = jnp.clip(jnp.round(x * scale), -128.0, 127.0) / scale
            return x + jax.lax.stop_gradient(xq - x)

        def _weight_quant(w):
            scale = 1.0 / jnp.clip(jnp.mean(jnp.abs(w)), 1e-05)
            wq = jnp.clip(jnp.round(w * scale), -1.0, 1.0) / scale
            return w + jax.lax.stop_gradient(wq - w)

        def _bitlinear(x, w):
            return jnp.einsum('bsd,fd->bsf', _act_quant(x), _weight_quant(w))
        key = jax.random.key(seed)
        k_x, k_w1, k_w2 = jax.random.split(key, 3)
        x = jax.random.normal(k_x, (4, 1024, D_MODEL), dtype=jnp.float32)
        W1 = jax.random.normal(k_w1, (D_FF, D_MODEL), dtype=jnp.float32) / np.sqrt(D_MODEL)
        W2 = jax.random.normal(k_w2, (D_MODEL, D_FF), dtype=jnp.float32) / np.sqrt(D_FF)
        return {'x': x, 'W1': W1, 'W2': W2}
    _L0_ffn_all = _L0_ffn_setup()
    _L0_ffn_in = {k: v for k, v in _L0_ffn_all.items() if k in ('W1', 'W2')}
    del _L0_ffn_all

    def _L1_xattn_setup():
        import jax, jax.numpy as jnp
        import numpy as np
        B, S, L = (2, 256, 256)
        DIM_Q, H, K, D_C, D_CQ, R = (512, 16, 128, 128, 384, 64)

        def _rope_tables(seq_len, dim, dtype):
            inv_freq = 1.0 / 10000.0 ** (jnp.arange(0, dim, 2, dtype=dtype) / dim)
            t = jnp.arange(seq_len, dtype=dtype)
            freqs = t[:, None] * inv_freq[None, :]
            sin = jnp.repeat(jnp.sin(freqs), 2, axis=-1)
            cos = jnp.repeat(jnp.cos(freqs), 2, axis=-1)
            return (sin, cos)

        def _rotate_half(x):
            h = x.shape[-1] // 2
            return jnp.concatenate([-x[..., h:], x[..., :h]], axis=-1)
        key = jax.random.key(seed)
        ks = jax.random.split(key, 8)
        s_in = 1.0 / np.sqrt(DIM_Q)
        s_k = 1.0 / np.sqrt(K)
        s_cq = 1.0 / np.sqrt(D_CQ)
        s_c = 1.0 / np.sqrt(D_C)
        return {'hidden_q': jax.random.normal(ks[0], (B, S, DIM_Q), jnp.float32), 'kv_c': jax.random.normal(ks[1], (B, L, D_C), jnp.float32), 'Wq': jax.random.normal(ks[2], (H * K, DIM_Q), jnp.float32) * s_in, 'w_kc_q': jax.random.normal(ks[3], (H, K, D_CQ), jnp.float32) * s_k, 'w_kc_kv': jax.random.normal(ks[4], (H, K, D_C), jnp.float32) * s_k, 'W_qr': jax.random.normal(ks[5], (H, D_CQ, R), jnp.float32) * s_cq / np.sqrt(R), 'W_kr': jax.random.normal(ks[6], (H, D_C, R), jnp.float32) * s_c, 'Wo': jax.random.normal(ks[7], (DIM_Q, H * K), jnp.float32) * s_k}
    _L1_xattn_all = _L1_xattn_setup()
    _L1_xattn_in = {k: v for k, v in _L1_xattn_all.items() if k in ('Wq', 'w_kc_q', 'w_kc_kv', 'W_qr', 'W_kr', 'Wo')}
    del _L1_xattn_all

    def _L1_ffn_setup():
        import jax, jax.numpy as jnp
        import numpy as np
        H = 512
        E = 8
        K = 2
        I = 16
        key = jax.random.key(seed)
        k1, k2, k3, k4 = jax.random.split(key, 4)
        B, T = (2, 1024)
        x = jax.random.normal(k1, (B, T, H), dtype=jnp.float32)
        router_w = jax.random.normal(k2, (E, H), dtype=jnp.float32) / np.sqrt(H)
        down_w = jax.random.normal(k3, (E, I, H), dtype=jnp.float32) / np.sqrt(H)
        up_w = jax.random.normal(k4, (E, H, I), dtype=jnp.float32) / np.sqrt(I)
        return {'x': x, 'router_w': router_w, 'down_w': down_w, 'up_w': up_w}
    _L1_ffn_all = _L1_ffn_setup()
    _L1_ffn_in = {k: v for k, v in _L1_ffn_all.items() if k in ('router_w', 'down_w', 'up_w')}
    del _L1_ffn_all
    return {'x': x, 'ctx_512': ctx_512, 'L0_xattn_Wq': _L0_xattn_in['Wq'], 'L0_xattn_Wkv_expand': _L0_xattn_in['Wkv_expand'], 'L0_xattn_Wout': _L0_xattn_in['Wout'], 'L0_ffn_W1': _L0_ffn_in['W1'], 'L0_ffn_W2': _L0_ffn_in['W2'], 'L1_xattn_Wq': _L1_xattn_in['Wq'], 'L1_xattn_w_kc_q': _L1_xattn_in['w_kc_q'], 'L1_xattn_w_kc_kv': _L1_xattn_in['w_kc_kv'], 'L1_xattn_W_qr': _L1_xattn_in['W_qr'], 'L1_xattn_W_kr': _L1_xattn_in['W_kr'], 'L1_xattn_Wo': _L1_xattn_in['Wo'], 'L1_ffn_router_w': _L1_ffn_in['router_w'], 'L1_ffn_down_w': _L1_ffn_in['down_w'], 'L1_ffn_up_w': _L1_ffn_in['up_w']}

def reference(x, ctx_512, L0_xattn_Wq, L0_xattn_Wkv_expand, L0_xattn_Wout, L0_ffn_W1, L0_ffn_W2, L1_xattn_Wq, L1_xattn_w_kc_q, L1_xattn_w_kc_kv, L1_xattn_W_qr, L1_xattn_W_kr, L1_xattn_Wo, L1_ffn_router_w, L1_ffn_down_w, L1_ffn_up_w):
    import jax
    import jax.numpy as jnp

    def _L0_xattn_ref(q, latent_kv, Wq, Wkv_expand, Wout):
        import jax, jax.numpy as jnp
        import numpy as np
        B, S, H, NH, L = (2, 512, 512, 16, 128)
        HD = H // NH
        b, sq, _ = q.shape
        sk = latent_kv.shape[1]
        qp = q @ Wq.T
        kv = latent_kv @ Wkv_expand.T
        k, v = jnp.split(kv, 2, axis=-1)
        qh = qp.reshape(b, sq, NH, HD).transpose(0, 2, 1, 3)
        kh = k.reshape(b, sk, NH, HD).transpose(0, 2, 1, 3)
        vh = v.reshape(b, sk, NH, HD).transpose(0, 2, 1, 3)
        inv_sqrt_d = 1.0 / jnp.sqrt(jnp.float32(HD))
        scores = jnp.einsum('bhqd,bhkd->bhqk', qh, kh) * inv_sqrt_d
        causal = jnp.tril(jnp.ones((sq, sk), dtype=bool))
        scores = jnp.where(causal, scores, jnp.finfo(scores.dtype).min)
        attn = jax.nn.softmax(scores, axis=-1)
        out = jnp.einsum('bhqk,bhkd->bhqd', attn, vh)
        out = out.transpose(0, 2, 1, 3).reshape(b, sq, H)
        return out @ Wout.T

    def _L0_ffn_ref(x, W1, W2):
        import jax, jax.numpy as jnp
        import numpy as np
        D_MODEL = 512
        D_FF = 2048

        def _act_quant(x):
            scale = 127.0 / jnp.clip(jnp.max(jnp.abs(x), axis=-1, keepdims=True), 1e-05)
            xq = jnp.clip(jnp.round(x * scale), -128.0, 127.0) / scale
            return x + jax.lax.stop_gradient(xq - x)

        def _weight_quant(w):
            scale = 1.0 / jnp.clip(jnp.mean(jnp.abs(w)), 1e-05)
            wq = jnp.clip(jnp.round(w * scale), -1.0, 1.0) / scale
            return w + jax.lax.stop_gradient(wq - w)

        def _bitlinear(x, w):
            return jnp.einsum('bsd,fd->bsf', _act_quant(x), _weight_quant(w))
        h = jax.nn.silu(_bitlinear(x, W1))
        return _bitlinear(h, W2)

    def _L1_xattn_ref(hidden_q, kv_c, Wq, w_kc_q, w_kc_kv, W_qr, W_kr, Wo):
        import jax, jax.numpy as jnp
        import numpy as np
        B, S, L = (2, 256, 256)
        DIM_Q, H, K, D_C, D_CQ, R = (512, 16, 128, 128, 384, 64)

        def _rope_tables(seq_len, dim, dtype):
            inv_freq = 1.0 / 10000.0 ** (jnp.arange(0, dim, 2, dtype=dtype) / dim)
            t = jnp.arange(seq_len, dtype=dtype)
            freqs = t[:, None] * inv_freq[None, :]
            sin = jnp.repeat(jnp.sin(freqs), 2, axis=-1)
            cos = jnp.repeat(jnp.cos(freqs), 2, axis=-1)
            return (sin, cos)

        def _rotate_half(x):
            h = x.shape[-1] // 2
            return jnp.concatenate([-x[..., h:], x[..., :h]], axis=-1)
        b, s, _ = hidden_q.shape
        l = kv_c.shape[1]
        q_hk = (hidden_q @ Wq.T).reshape(b, s, H, K)
        q_big = jnp.einsum('bshk,hkq->bshq', q_hk, w_kc_q)
        sin, cos = _rope_tables(l, D_C, kv_c.dtype)
        kv_rope = kv_c * cos[None] + _rotate_half(kv_c) * sin[None]
        q_r = jnp.einsum('bshq,hqr->bhsr', q_big, W_qr)
        k_r = jnp.einsum('bld,hdr->bhlr', kv_rope, W_kr)
        scores = jnp.einsum('bhsr,bhlr->bhsl', q_r, k_r)
        attn = jax.nn.softmax(scores, axis=-1)
        ctx_c = jnp.einsum('bhsl,bld->bhsd', attn, kv_rope)
        ctx_lat = jnp.einsum('bhsd,hkd->bshk', ctx_c, w_kc_kv)
        out = ctx_lat.reshape(b, s, H * K) @ Wo.T
        return out

    def _L1_ffn_ref(x, router_w, down_w, up_w):
        import jax, jax.numpy as jnp
        import numpy as np
        H = 512
        E = 8
        K = 2
        I = 16
        logits = jnp.einsum('bth,eh->bte', x, router_w)
        weights = jax.nn.softmax(logits, axis=-1)
        top_w, top_idx = jax.lax.top_k(weights, K)
        topk_mask = jnp.sum(jax.nn.one_hot(top_idx, E, dtype=x.dtype), axis=-2)
        gate = weights * topk_mask
        h = jnp.einsum('bth,eih->beti', x, down_w)
        a = jax.nn.silu(h)
        expert_out = jnp.einsum('beti,ehi->beth', a, up_w)
        out = jnp.einsum('beth,bte->bth', expert_out, gate)
        return out
    x = x + _L0_xattn_ref(_layernorm(x, axis=-1), ctx_512, L0_xattn_Wq, L0_xattn_Wkv_expand, L0_xattn_Wout)
    x = x + _L0_ffn_ref(_layernorm(x, axis=-1), L0_ffn_W1, L0_ffn_W2)
    x = x + _L1_xattn_ref(_layernorm(x, axis=-1), ctx_512, L1_xattn_Wq, L1_xattn_w_kc_q, L1_xattn_w_kc_kv, L1_xattn_W_qr, L1_xattn_W_kr, L1_xattn_Wo)
    x = x + _L1_ffn_ref(_layernorm(x, axis=-1), L1_ffn_router_w, L1_ffn_down_w, L1_ffn_up_w)
    return x

_drawn_inputs = setup_inputs


def setup_inputs(seed=0):
    import zlib

    import numpy as np

    out = dict(_drawn_inputs(seed))
    spreads = {}
    factors = {'L0_xattn_Wq': 26.167}
    for name, (base, spread) in spreads.items():
        noise = np.random.default_rng([zlib.crc32(name.encode()), seed]).standard_normal(out[name].shape)
        drawn = base * np.exp(spread * noise) if base else spread * noise
        out[name] = jnp.asarray(drawn.astype(out[name].dtype))
    for name, factor in factors.items():
        out[name] = (out[name] * factor).astype(out[name].dtype)
    return out
```

```python
from contextlib import ExitStack

import concourse.bass as bass
from concourse import mybir

F32 = mybir.dt.float32
F32R = mybir.dt.float32r
BF16 = mybir.dt.bfloat16
U32 = mybir.dt.uint32
ALU = mybir.AluOpType
ACT = mybir.ActivationFunctionType
AX = mybir.AxisListType

P = 128
B, S, D = 8, 256, 512
TPB = S // P
TILES = B * TPB
DC = D // P
CTX = 128
DMA = 16
EPS = 1e-5

H0, HD0 = 16, 32
GROUPS = H0 // 4
F = 2048
FC = F // P
MAGIC = 1.5 * 2.0 ** 23
H1, R1 = 16, 64
PAIRS = H1 // 2
E, EI = 8, 16


def products(pe, out, pairs, start=True, stop=True):
    last = None
    for n, (lh, ll, rh, rl) in enumerate(pairs):
        pe.matmul(out, ll, rh, start=start and n == 0, stop=False)
        pe.matmul(out, lh, rl, start=False, stop=False)
        last = pe.matmul(out, lh, rh, start=False, stop=stop and n == len(pairs) - 1)
    return last


def f32(ap):
    return ap.bitcast(F32)


class Memory:

    def __init__(self, nc, phase):
        self.nc, self.phase, self.stack = nc, phase, ExitStack()

    def __enter__(self):
        self.stack.__enter__()
        return self

    def __exit__(self, *a):
        return self.stack.__exit__(*a)

    def sb(self, name, shape, dt=F32):
        return self.stack.enter_context(self.nc.sbuf_tensor(f"{self.phase}_{name}", shape, dt))

    def ps(self, name, shape, dt=F32):
        return self.stack.enter_context(self.nc.psum_tensor(f"{self.phase}_{name}", shape, dt))

    def sem(self, name):
        return self.stack.enter_context(self.nc.semaphore(f"{self.phase}_{name}"))

    def block(self):
        return self.nc.Block()


def tile_stats(dve, x_tile, stats, mean_var):
    dve.bn_stats(stats, x_tile)
    dve.drain()
    return dve.bn_aggr(mean_var, stats)


def inverse_deviations(nc, phase, mv, rstd):
    with Memory(nc, phase) as m:
        var = m.sb("var", [P, TILES])
        dev = m.sb("dev", [P, TILES])
        sq = m.sb("sq", [P, TILES])
        var_ready, dev_ready = m.sem("var_ready"), m.sem("dev_ready")
        with m.block() as block:
            @block.vector
            def _(dve):
                dve.tensor_scalar(var[:, :], mv[:, :, 1], EPS, None, ALU.add).then_inc(var_ready, 1)
                dve.wait_ge(dev_ready, 1)
                dve.reciprocal(rstd[:, :], dev[:, :])
                dve.drain()
                dve.tensor_tensor(sq[:, :], rstd[:, :], rstd[:, :], ALU.mult)
                dve.drain()
                dve.tensor_tensor(sq[:, :], sq[:, :], var[:, :], ALU.mult)
                dve.drain()
                dve.tensor_scalar(sq[:, :], sq[:, :], -0.5, 1.5, ALU.mult, ALU.add)
                dve.drain()
                dve.tensor_tensor(rstd[:, :], rstd[:, :], sq[:, :], ALU.mult)

            @block.scalar
            def _(act):
                act.wait_ge(var_ready, 1)
                act.activation(dev[:, :], var[:, :], ACT.Sqrt).then_inc(dev_ready, 1)



FULL0 = ["S0", "lnt0", "lnt1", "proj0", "proj1",
         "S1", "T0", "proj2", "proj3", "pv0",
         "S2", "T1", "pv1",
         "S3", "T2", "pv2",
         "T3", "pv3", "v0", "v1", "out0", "out1"]
PREP0 = ["lnt0", "lnt1", "proj0", "proj1", "proj2", "proj3", "v0", "v1"]
LAST0 = [s for s in FULL0 if s not in PREP0]
SPLIT0 = ("lnt", "proj", "pv")


def pieces(steps):
    return [s for s in steps if s[0] not in "ST"]


def layer0_attention(nc, io, X, mv, rstd, ident, identb):
    with Memory(nc, "a") as m:
        wq_h, wq_l = m.sb("wq_h", [P, DC, D], F32R), m.sb("wq_l", [P, DC, D], F32R)
        wkv_h, wkv_l = m.sb("wkv_h", [P, 2 * D], F32R), m.sb("wkv_l", [P, 2 * D], F32R)
        wo_h, wo_l = m.sb("wo_h", [P, DC, D], F32R), m.sb("wo_l", [P, DC, D], F32R)
        maskb = m.sb("maskb", [P, P], BF16)

        with Memory(nc, "aw") as w:
            raw = w.sb("raw", [P, 5 * 1024])
            identf, maskf = ident, w.sb("maskf", [P, P])
            stats = w.sb("stats", [P, TILES, 6])
            raws = [raw[:, 0:2048].rearrange("p (c n) -> p c n", c=DC), raw[:, 2048:3072],
                    raw[:, 3072:5120].rearrange("p (c n) -> p c n", c=DC)]
            x_in, w_in, c_in = w.sem("x_in"), [w.sem(f"w_in{i}") for i in range(3)], w.sem("c_in")
            split_hi = w.sem("split_hi")
            XG = 4
            with w.block() as block:
                @block.sync
                def _(sp):
                    sp.dma_start(raws[0], io["wq0"].rearrange("(c p) n -> p c n", p=P)).then_inc(w_in[0], DMA)
                    sp.dma_start(raws[1], io["wkv0"]).then_inc(w_in[1], DMA)
                    sp.dma_start(raws[2], io["wo0"].rearrange("(c p) n -> p c n", p=P)).then_inc(w_in[2], DMA)
                    sp.dma_start(identf[:, :], io["ident"]).then_inc(c_in, DMA)
                    sp.dma_start(maskf[:, :], io["mask"]).then_inc(c_in, DMA)

                @block.gpsimd
                def _(pool):
                    pool.wait_ge(c_in, 2 * DMA)
                    pool.tensor_copy(identb[:, :], identf[:, :])
                    pool.tensor_copy(maskb[:, :], maskf[:, :])

                @block.scalar
                def _(act):
                    for g in range(TILES // XG):
                        act.dma_start(X[:, XG * g:XG * g + XG, :],
                                      io["x"].rearrange("(t p) d -> p t d", p=P)[:, XG * g:XG * g + XG, :]
                                      ).then_inc(x_in, DMA)
                    for i, hi in enumerate((wq_h, wkv_h, wo_h)):
                        act.wait_ge(w_in[i], DMA)
                        act.activation(hi[:], raws[i], ACT.Copy).then_inc(split_hi, 1)

                @block.vector
                def _(dve):
                    for i, (hi, lo) in enumerate(((wq_h, wq_l), (wkv_h, wkv_l), (wo_h, wo_l))):
                        dve.wait_ge(split_hi, i + 1)
                        dve.tensor_tensor(lo[:], raws[i], f32(hi[:]), ALU.subtract)
                    dve.wait_ge(x_in, TILES // XG * DMA)
                    for t in range(TILES):
                        dve.bn_stats(stats[:, t, :], X[:, t, :])
                    dve.drain()
                    for t in range(TILES):
                        dve.bn_aggr(mv[:, t, :], stats[:, t, :])

        inverse_deviations(nc, "as", mv, rstd)

        y = m.sb("y", [P, TPB, D])
        yT_h, yT_l = m.sb("yT_h", [P, DC, S], F32R), m.sb("yT_l", [P, DC, S], F32R)
        ctx_raw = m.sb("ctx_raw", [P, S])
        cT_h, cT_l = m.sb("cT_h", [P, S], F32R), m.sb("cT_l", [P, S], F32R)
        qk_h, qk_l = m.sb("qk_h", [P, 2, GROUPS, S], F32R), m.sb("qk_l", [P, 2, GROUPS, S], F32R)
        q_stack = m.sb("q_stack", [96, 4, GROUPS, S], F32R)
        k_stack = m.sb("k_stack", [96, 4, GROUPS, S], F32R)
        V = m.sb("V", [P, TPB, D])
        neg_max = m.sb("neg_max", [P, 8])
        sums, inv = m.sb("sums", [P, 8]), m.sb("inv", [P, 8])
        probs = [m.sb(f"probs{i}", [P, 4 * 3 * P]) for i in range(2)]
        pT = m.sb("pT", [P, 4, 3 * P])
        c_h, c_l = m.sb("c_h", [P, 4, S], F32R), m.sb("c_l", [P, 4, S], F32R)
        stats, new_mv = m.sb("stats", [P, TPB, 6]), m.sb("new_mv", [P, TPB, 2])

        s_q0, s_q1 = m.ps("s_q0", [P, 4, P]), m.ps("s_q1", [P, 4, S])
        t_k0, t_k1 = m.ps("t_k0", [P, 4, S]), m.ps("t_k1", [P, 4, P])
        work = [m.ps(f"work{i}", [P, D]) for i in range(2)]

        ctx_in, ctx_hi, ctx_split = m.sem("ctx_in"), m.sem("ctx_hi"), m.sem("ctx_split")
        y_ready = m.sem("y_ready")
        worked, work_hi, work_free = m.sem("worked"), m.sem("work_hi"), m.sem("work_free")
        stacked = [m.sem(f"stacked{j}") for j in range(4)]
        scored, maxed, exped, normed = m.sem("scored"), m.sem("maxed"), m.sem("exped"), m.sem("normed")
        turned, evac_act, evac_dve = m.sem("turned"), m.sem("evac_act"), m.sem("evac_dve")

        PER, PRO = len(pieces(FULL0)), len(pieces(PREP0))
        HI_PER = sum(s.rstrip("0123") in SPLIT0 for s in pieces(FULL0))
        HI_PRO = sum(s.rstrip("0123") in SPLIT0 for s in pieces(PREP0))
        SCALE = float(HD0) ** -0.5

        def piece_no(b, steps, name):
            n = pieces(steps).index(name)
            return n if steps is PREP0 else b * PER + PRO + n

        def hi_no(b, steps, name):
            n = [s for s in pieces(steps) if s.rstrip("0123") in SPLIT0].index(name)
            return n if steps is PREP0 else b * HI_PER + HI_PRO + n

        def rounds(eng, batch):
            batch(0, PREP0, 0)
            batch(0, FULL0, 1)
            with eng.Fori(1, B - 1) as b:
                batch(b, FULL0, b + 1)
            batch(B - 1, LAST0, None)

        with m.block() as block:
            @block.sync
            def _(sp):
                def batch(b, steps, nb):
                    if nb is None:
                        return
                    if steps is FULL0:
                        sp.wait_ge(ctx_split, nb)
                    sp.dma_start(ctx_raw[:, :], io["ctxT"][:, bass.ts(nb, S)]).then_inc(ctx_in, DMA)
                    sp.wait_ge(work_free, piece_no(b, steps, "proj3") + 1)
                    for j in range(4):
                        if steps is FULL0:
                            sp.wait_ge(scored, b * 4 + j + 1)
                        src = slice(32 * j, 32 * j + 32)
                        for r, (q, k) in enumerate(((qk_h, qk_h), (qk_l, qk_h), (qk_h, qk_l))):
                            dst = slice(32 * r, 32 * r + 32)
                            sp.dma_start(f32(q_stack[dst, j, :, :]), f32(q[src, 0, :, :])).then_inc(stacked[j], DMA)
                            sp.dma_start(f32(k_stack[dst, j, :, :]), f32(k[src, 1, :, :])).then_inc(stacked[j], DMA)
                rounds(sp, batch)

            @block.tensor
            def _(pe):
                def batch(b, steps, nb):
                    for step in steps:
                        kind, i = step[:-1], int(step[-1])
                        slot = b * 4 + i
                        if kind == "S":
                            pe.wait_ge(stacked[i], (b + 1) * 6 * DMA)
                            if steps is not FULL0 or not isinstance(b, int) or i > 0:
                                pe.wait_ge(exped, slot)
                            for h in range(4):
                                pe.matmul(s_q0[:, h, :], q_stack[:, i, h, 0:P], k_stack[:, i, h, 0:P],
                                          start=True, stop=False)
                                pe.matmul(s_q0[:, h, :], identb[:, :], maskb[:, :], start=False, stop=True)
                            for h in range(4):
                                pe.matmul(s_q1[:, h, :], q_stack[:, i, h, P:S], k_stack[:, i, h, :],
                                          start=True, stop=False)
                                last = pe.matmul(s_q1[:, h, P:S], identb[:, :], maskb[:, :],
                                                 start=False, stop=True)
                            last.then_inc(scored, 1)
                            continue
                        if kind == "T":
                            pe.wait_ge(normed, slot + 1)
                            if steps is not FULL0 or not isinstance(b, int) or i > 0:
                                pe.wait_ge(evac_act, slot)
                                pe.wait_ge(evac_dve, slot)
                            p0 = probs[i % 2][:, 0:4 * P].rearrange("p (h k) -> p h k", h=4)
                            p1 = probs[i % 2][:, 4 * P:12 * P].rearrange("p (h k) -> p h k", h=4)
                            for h in range(4):
                                pe.transpose(t_k0[:, h, 0:P], p0[:, h, :], ident[:, :])
                                pe.transpose(t_k0[:, h, P:S], p1[:, h, 0:P], ident[:, :])
                            for h in range(4):
                                last = pe.transpose(t_k1[:, h, :], p1[:, h, P:S], ident[:, :])
                            last.then_inc(turned, 1)
                            continue
                        n = piece_no(b, steps, step)
                        out = work[pieces(steps).index(step) % 2]
                        if not isinstance(n, int) or n >= 2:
                            pe.wait_ge(work_free, n - 1)
                        if kind == "lnt":
                            pe.wait_ge(y_ready, nb * TPB + i + 1)
                            for c in range(DC):
                                last = pe.transpose(out[:, c * P:(c + 1) * P], y[:, i, c * P:(c + 1) * P],
                                                    ident[:, :])
                        elif kind == "proj":
                            if i == 0:
                                pe.wait_ge(work_free, piece_no(b, steps, "lnt1") + 1)
                                pe.wait_ge(ctx_split, nb + 1)
                            cols = slice(i * P, (i + 1) * P)
                            products(pe, out[:, 0:S], [(wq_h[:, c, cols], wq_l[:, c, cols],
                                                        yT_h[:, c, :], yT_l[:, c, :]) for c in range(DC)])
                            last = products(pe, out[:, S:2 * S], [(wkv_h[:, cols], wkv_l[:, cols],
                                                                   cT_h[:, :], cT_l[:, :])])
                        elif kind == "v":
                            tok = slice(i * P, (i + 1) * P)
                            last = products(pe, out[:, :], [(cT_h[:, tok], cT_l[:, tok],
                                                             wkv_h[:, D:2 * D], wkv_l[:, D:2 * D])])
                        elif kind == "pv":
                            pe.wait_ge(evac_act, slot + 1)
                            pe.wait_ge(evac_dve, slot + 1)
                            if i == 0:
                                pe.wait_ge(work_free, piece_no(0, PREP0, "v1") + 1 if isinstance(b, int) and b == 0
                                           else piece_no(b - 1, FULL0, "v1") + 1)
                            for h in range(4):
                                head = slice((4 * h + i) * HD0, (4 * h + i + 1) * HD0)
                                rows = slice(32 * h, 32 * h + 32)
                                pe.matmul(out[rows, 0:S], V[:, 0, head], pT[:, h, 0:S], start=True, stop=False,
                                          tile_position=(0, 32 * h))
                            for h in range(4):
                                head = slice((4 * h + i) * HD0, (4 * h + i + 1) * HD0)
                                rows = slice(32 * h, 32 * h + 32)
                                last = pe.matmul(out[rows, P:S], V[:, 1, head], pT[:, h, S:S + P],
                                                 start=False, stop=True, tile_position=(0, 32 * h))
                        elif kind == "out":
                            if i == 0:
                                pe.wait_ge(work_free, piece_no(b, steps, "pv3") + 1)
                            tok = slice(i * P, (i + 1) * P)
                            last = products(pe, out[:, :], [(c_h[:, j, tok], c_l[:, j, tok],
                                                             wo_h[:, j, :], wo_l[:, j, :]) for j in range(4)])
                        last.then_inc(worked, 1)
                rounds(pe, batch)

            @block.scalar
            def _(act):
                def batch(b, steps, nb):
                    if nb is not None:
                        act.wait_ge(ctx_in, (nb + 1) * DMA)
                        if steps is FULL0:
                            act.wait_ge(worked, b * PER + PRO - 2 if not isinstance(b, int) or b > 0 else PRO)
                        act.activation(cT_h[:, :], ctx_raw[:, :], ACT.Copy).then_inc(ctx_hi, 1)
                    for step in steps:
                        kind, i = step[:-1], int(step[-1])
                        slot = b * 4 + i
                        if kind == "S":
                            act.wait_ge(maxed, slot + 1)
                            if not isinstance(slot, int) or slot >= 2:
                                act.wait_ge(turned, slot - 1)
                            pr = probs[i % 2]
                            for h in range(4):
                                act.activation(pr[:, h * P:(h + 1) * P], s_q0[:, h, :], ACT.Exp,
                                               bias=neg_max[:, h:h + 1], scale=SCALE, accum_out=sums[:, h:h + 1])
                            for h in range(4):
                                last = act.activation(pr[:, 4 * P + h * S:4 * P + (h + 1) * S], s_q1[:, h, :], ACT.Exp,
                                                      bias=neg_max[:, 4 + h:5 + h], scale=SCALE,
                                                      accum_out=sums[:, 4 + h:5 + h])
                            last.then_inc(exped, 1)
                        elif kind == "T":
                            act.wait_ge(turned, slot + 1)
                            act.activation(pT[:, :, 0:S], t_k0[:, :, :], ACT.Copy).then_inc(evac_act, 1)
                        elif kind in SPLIT0:
                            out = work[pieces(steps).index(step) % 2]
                            act.wait_ge(worked, piece_no(b, steps, step) + 1)
                            if kind == "lnt":
                                hi = act.activation(yT_h[:, :, i * P:(i + 1) * P],
                                                    out[:, :].rearrange("p (c t) -> p c t", c=DC), ACT.Copy)
                            elif kind == "proj":
                                if i == 0 and steps is FULL0:
                                    for s in stacked:
                                        act.wait_ge(s, nb * 6 * DMA)
                                hi = act.activation(qk_h[:, :, i, :], out[:, :].rearrange("p (a t) -> p a t", a=2),
                                                    ACT.Copy)
                            else:
                                hi = act.activation(c_h[:, i, :], out[:, 0:S], ACT.Copy)
                            hi.then_inc(work_hi, 1)
                rounds(act, batch)

            @block.vector
            def _(dve):
                def normalise(b, i):
                    dve.wait_ge(exped, b * 4 + i + 1)
                    dve.reciprocal(inv[:, :], sums[:, :])
                    dve.drain()
                    p0 = probs[i % 2][:, 0:4 * P].rearrange("p (h k) -> p h k", h=4)
                    p1 = probs[i % 2][:, 4 * P:12 * P].rearrange("p (h k) -> p h k", h=4)
                    for h in range(4):
                        dve.tensor_scalar(p0[:, h, :], p0[:, h, :], inv[:, h:h + 1], None, ALU.mult)
                    for h in range(4):
                        last = dve.tensor_scalar(p1[:, h, :], p1[:, h, :], inv[:, 4 + h:5 + h], None, ALU.mult)
                    last.then_inc(normed, 1)

                def batch(b, steps, nb):
                    if nb is not None:
                        if steps is FULL0:
                            dve.wait_ge(worked, 2 if isinstance(b, int) and b == 0 else (b - 1) * PER + PRO + 2)
                        for t in range(TPB):
                            tile = nb * TPB + t
                            dve.tensor_scalar(y[:, t, :], X[:, bass.ds(tile, 1), :].rearrange("p a d -> p (a d)"),
                                              mv[:, bass.ds(tile, 1), 0:1].rearrange("p a d -> p (a d)"),
                                              rstd[:, bass.ds(tile, 1)], ALU.subtract, ALU.mult).then_inc(y_ready, 1)
                        dve.wait_ge(ctx_hi, nb + 1)
                        dve.tensor_tensor(cT_l[:, :], ctx_raw[:, :], f32(cT_h[:, :]), ALU.subtract).then_inc(ctx_split, 1)
                    for step in steps:
                        kind, i = step[:-1], int(step[-1])
                        slot = b * 4 + i
                        if kind == "S":
                            if i > 0:
                                normalise(b, i - 1)
                            dve.wait_ge(scored, slot + 1)
                            dve.tensor_reduce(neg_max[:, 0:4], s_q0[:, :, :], AX.X, ALU.max, negate=True)
                            dve.tensor_reduce(neg_max[:, 4:8], s_q1[:, :, :], AX.X, ALU.max, negate=True)
                            dve.drain()
                            dve.tensor_scalar(neg_max[:, :], neg_max[:, :], SCALE, None, ALU.mult).then_inc(maxed, 1)
                            continue
                        if kind == "T":
                            if i == 3:
                                normalise(b, 3)
                            dve.wait_ge(turned, slot + 1)
                            dve.tensor_copy(pT[:, :, S:S + P], t_k1[:, :, :]).then_inc(evac_dve, 1)
                            continue
                        out = work[pieces(steps).index(step) % 2]
                        if kind in SPLIT0:
                            dve.wait_ge(work_hi, hi_no(b, steps, step) + 1)
                            if kind == "lnt":
                                hi = yT_h[:, :, i * P:(i + 1) * P]
                                lo, src = yT_l[:, :, i * P:(i + 1) * P], out[:, :].rearrange("p (c t) -> p c t", c=DC)
                            elif kind == "proj":
                                hi, lo = qk_h[:, :, i, :], qk_l[:, :, i, :]
                                src = out[:, :].rearrange("p (a t) -> p a t", a=2)
                            else:
                                hi, lo, src = c_h[:, i, :], c_l[:, i, :], out[:, 0:S]
                            dve.tensor_tensor(lo, src, f32(hi), ALU.subtract).then_inc(work_free, 1)
                            continue
                        dve.wait_ge(worked, piece_no(b, steps, step) + 1)
                        if kind == "v":
                            dve.tensor_copy(V[:, i, :], out[:, :]).then_inc(work_free, 1)
                        else:
                            tile = b * TPB + i
                            xt = X[:, bass.ds(tile, 1), :].rearrange("p a d -> p (a d)")
                            dve.tensor_tensor(xt, xt, out[:, :], ALU.add).then_inc(work_free, 1)
                            dve.drain()
                            dve.bn_stats(stats[:, i, :], xt)
                            dve.drain()
                            dve.bn_aggr(new_mv[:, i, :], stats[:, i, :])
                            dve.drain()
                            dve.tensor_copy(mv[:, bass.ds(tile, 1), :].rearrange("p a d -> p (a d)"), new_mv[:, i, :])
                rounds(dve, batch)



def layer0_feed_forward(nc, io, X, mv, rstd, ident, identb):
    with Memory(nc, "b") as m:
        w1, w2 = m.sb("w1", [P, DC, F], BF16), m.sb("w2", [P, FC, D], BF16)
        mean = m.sb("mean", [P, 2])

        with Memory(nc, "bw") as w:
            raw = [w.sb("raw1", [P, DC, F]), w.sb("raw2", [P, FC, D])]
            part, total = w.sb("part", [P, 2, FC]), w.sb("total", [P, 2])
            ones, scale = w.sb("ones", [P, P]), w.sb("scale", [P, 2])
            all_sums = w.ps("all_sums", [P, 2])
            w_in, ones_ready, summed, crossed, rounded = (
                [w.sem("w1_in"), w.sem("w2_in")], w.sem("ones_ready"), w.sem("summed"), w.sem("crossed"), w.sem("rounded"))
            with w.block() as block:
                @block.sync
                def _(sp):
                    sp.dma_start(raw[0][:], io["w1"].rearrange("(c p) n -> p c n", p=P)).then_inc(w_in[0], DMA)
                    sp.dma_start(raw[1][:], io["w2"].rearrange("(c p) n -> p c n", p=P)).then_inc(w_in[1], DMA)

                @block.gpsimd
                def _(pool):
                    pool.memset(ones[:, :], 1.0).then_inc(ones_ready, 1)

                @block.tensor
                def _(pe):
                    pe.wait_ge(ones_ready, 1)
                    pe.wait_ge(summed, 1)
                    pe.matmul(all_sums[:, :], ones[:, :], total[:, :], start=True, stop=True).then_inc(crossed, 1)

                @block.vector
                def _(dve):
                    for i in range(2):
                        dve.wait_ge(w_in[i], DMA)
                        dve.tensor_reduce(part[:, i, :], raw[i][:].rearrange("p c n -> p (c n)").rearrange(
                            "p (c n) -> p c n", c=FC), AX.X, ALU.add, apply_absolute_value=True)
                    dve.drain()
                    dve.tensor_reduce(total[:, :], part[:, :, :], AX.X, ALU.add).then_inc(summed, 1)
                    dve.wait_ge(crossed, 1)
                    dve.tensor_scalar(mean[:, :], all_sums[:, :], 1.0 / (F * D), 1e-5, ALU.mult, ALU.max)
                    dve.drain()
                    dve.reciprocal(scale[:, :], mean[:, :])
                    dve.drain()
                    for i in range(2):
                        dve.tensor_scalar(raw[i][:], raw[i][:], scale[:, i:i + 1], 1.0, ALU.mult, ALU.min)
                        dve.drain()
                        dve.tensor_scalar(raw[i][:], raw[i][:], -1.0, MAGIC, ALU.max, ALU.add).then_inc(rounded, 1)

                @block.scalar
                def _(act):
                    for i, q in enumerate((w1, w2)):
                        act.wait_ge(rounded, i + 1)
                        act.activation(q[:], raw[i][:], ACT.Copy, bias=-MAGIC)

        inverse_deviations(nc, "bs", mv, rstd)

        y, yr = m.sb("y", [P, D]), m.sb("yr", [P, D])
        xq = [m.sb(f"xq{i}", [P, D], BF16) for i in range(2)]
        xqT = m.sb("xqT", [P, DC, P], BF16)
        s1 = m.sb("s1", [P, 2])
        s2 = m.sb("s2", [P, 2])
        h = [m.sb(f"h{i}", [P, F]) for i in range(2)]
        hr, hq = m.sb("hr", [P, F]), m.sb("hq", [P, F], BF16)
        hqT = m.sb("hqT", [P, FC, P], BF16)
        amax, amax2, q_scale, q_scale2 = m.sb("amax", [P, 1]), m.sb("amax2", [P, 1]), m.sb("qs", [P, 1]), m.sb("qs2", [P, 1])
        stats, new_mv = m.sb("stats", [P, 6]), m.sb("new_mv", [P, 2])
        up = m.ps("up", [P, F])
        xT = m.ps("xT", [P, DC, P], BF16)
        hT = m.ps("hT", [P, FC, P], BF16)
        down = m.ps("down", [P, D])
        x_quant, x_turned, x_copied = m.sem("x_quant"), m.sem("x_turned"), m.sem("x_copied")
        upped, silued, h_quant = m.sem("upped"), m.sem("silued"), m.sem("h_quant")
        h_turned, h_act, h_dve, downed, added = m.sem("h_turned"), m.sem("h_act"), m.sem("h_dve"), m.sem("downed"), m.sem("added")

        def tiles(tile):
            with_loop = (TILES - 2) // 2
            return with_loop

        with m.block() as block:
            @block.tensor
            def _(pe):
                def front(t, par):
                    pe.wait_ge(x_quant, t + 1)
                    if not isinstance(t, int) or t > 0:
                        pe.wait_ge(x_copied, t)
                    for c in range(DC):
                        last = pe.transpose(xT[:, c, :], xq[par][:, c * P:(c + 1) * P], identb[:, :])
                    last.then_inc(x_turned, 1)
                    pe.wait_ge(x_copied, t + 1)
                    for n in range(4):
                        if n % 2 == 0 and (not isinstance(t, int) or t > 0):
                            pe.wait_ge(silued, 2 * t - 1 + n // 2)
                        for c in range(DC):
                            last = pe.matmul(up[:, n * D:(n + 1) * D], xqT[:, c, :], w1[:, c, n * D:(n + 1) * D],
                                             start=c == 0, stop=c == DC - 1)
                        if n % 2:
                            last.then_inc(upped, 1)

                def back(t):
                    pe.wait_ge(h_quant, t + 1)
                    if not isinstance(t, int) or t > 0:
                        pe.wait_ge(h_act, t)
                        pe.wait_ge(h_dve, t)
                        pe.wait_ge(added, t)
                    for c in range(FC):
                        last = pe.transpose(hT[:, c, :], hq[:, c * P:(c + 1) * P], identb[:, :])
                    last.then_inc(h_turned, 1)
                    for c in range(FC):
                        if c == 0:
                            pe.wait_ge(h_act, t + 1)
                        if c == FC // 2:
                            pe.wait_ge(h_dve, t + 1)
                        last = pe.matmul(down[:, :], hqT[:, c, :], w2[:, c, :], start=c == 0, stop=c == FC - 1)
                    last.then_inc(downed, 1)

                front(0, 0)
                with pe.Fori(0, TILES // 2 - 1) as r:
                    for par in range(2):
                        front(2 * r + par + 1, 1 - par)
                        back(2 * r + par)
                front(TILES - 1, 1)
                back(TILES - 2)
                back(TILES - 1)

            @block.scalar
            def _(act):
                def front(t, par):
                    act.wait_ge(x_turned, t + 1)
                    act.activation(xqT[:], xT[:], ACT.Copy).then_inc(x_copied, 1)
                    if not isinstance(t, int) or t >= 2:
                        act.wait_ge(h_quant, t - 1)
                    for n in range(2):
                        act.wait_ge(upped, 2 * t + n + 1)
                        cols = slice(n * F // 2, (n + 1) * F // 2)
                        act.activation(h[par][:, cols], up[:, cols], ACT.Silu, scale=s1[:, par:par + 1]
                                       ).then_inc(silued, 1)

                def back(t):
                    act.wait_ge(h_turned, t + 1)
                    act.activation(hqT[:, 0:FC // 2, :], hT[:, 0:FC // 2, :], ACT.Copy).then_inc(h_act, 1)

                front(0, 0)
                front(1, 1)
                back(0)
                with act.Fori(0, TILES // 2 - 1) as r:
                    for par in range(2):
                        front(2 * r + par + 2, par)
                        back(2 * r + par + 1)
                back(TILES - 1)

            @block.vector
            def _(dve):
                def quantise(src, rounded, dst, factor, scale):
                    dve.drain()
                    dve.tensor_scalar(factor, factor, 1e-5, None, ALU.max)
                    dve.drain()
                    dve.reciprocal(scale, factor)
                    dve.drain()
                    dve.tensor_scalar(scale, scale, 127.0, None, ALU.mult)
                    dve.drain()
                    dve.tensor_scalar(rounded, src, scale, MAGIC, ALU.mult, ALU.add)
                    dve.drain()
                    return dve.tensor_scalar(dst, rounded, -MAGIC, 127.0, ALU.add, ALU.min)

                def quantise_tokens(t, par):
                    if not isinstance(t, int) or t >= 2:
                        dve.wait_ge(x_turned, t - 1)
                    dve.tensor_scalar(y[:, :], X[:, bass.ds(t, 1), :].rearrange("p a d -> p (a d)"),
                                      mv[:, bass.ds(t, 1), 0:1].rearrange("p a d -> p (a d)"),
                                      rstd[:, bass.ds(t, 1)], ALU.subtract, ALU.mult)
                    dve.drain()
                    dve.tensor_reduce(amax[:, :], y[:, :], AX.X, ALU.max, apply_absolute_value=True)
                    quantise(y[:, :], yr[:, :], xq[par][:, :], amax[:, :], q_scale[:, :])
                    dve.tensor_scalar(s1[:, par:par + 1], amax[:, :], mean[:, 0:1], 1.0 / 127.0,
                                      ALU.mult, ALU.mult).then_inc(x_quant, 1)

                def quantise_hidden(t, par):
                    dve.wait_ge(silued, 2 * t + 2)
                    dve.tensor_reduce(amax2[:, :], h[par][:, :], AX.X, ALU.max, apply_absolute_value=True)
                    quantise(h[par][:, :], hr[:, :], hq[:, :], amax2[:, :], q_scale2[:, :])
                    dve.tensor_scalar(s2[:, par:par + 1], amax2[:, :], mean[:, 1:2], 1.0 / 127.0,
                                      ALU.mult, ALU.mult).then_inc(h_quant, 1)

                def finish(t, par):
                    dve.wait_ge(downed, t + 1)
                    xt = X[:, bass.ds(t, 1), :].rearrange("p a d -> p (a d)")
                    dve.scalar_tensor_tensor(xt, down[:, :], s2[:, par:par + 1], xt, ALU.mult, ALU.add
                                             ).then_inc(added, 1)
                    dve.drain()
                    tile_stats(dve, xt, stats[:, :], new_mv[:, :])
                    dve.drain()
                    dve.tensor_copy(mv[:, bass.ds(t, 1), :].rearrange("p a d -> p (a d)"), new_mv[:, :])

                def tile(t, par, more):
                    quantise_hidden(t, par)
                    dve.wait_ge(h_turned, t + 1)
                    dve.tensor_copy(hqT[:, FC // 2:FC, :], hT[:, FC // 2:FC, :]).then_inc(h_dve, 1)
                    if more:
                        quantise_tokens(t + 2, par)
                    finish(t, par)

                quantise_tokens(0, 0)
                quantise_tokens(1, 1)
                with dve.Fori(0, TILES // 2 - 1) as r:
                    for par in range(2):
                        tile(2 * r + par, par, True)
                tile(TILES - 2, 0, False)
                tile(TILES - 1, 1, False)



def score_weights(nc, io, A_h, A_l):
    with Memory(nc, "cw") as w:
        kcq = w.sb("kcq", [P, H1, 3, P])
        wqr = w.sb("wqr", [P, H1, 3, R1])
        wq = w.sb("wq", [P, H1, D])
        mid = w.sb("mid", [P, H1, R1])
        banks = [w.ps(f"bank{i}", [P, D]) for i in range(4)]
        w_in, made, moved, split_hi, split_lo = (
            [w.sem(f"w_in{i}") for i in range(3)], w.sem("made"), w.sem("moved"), w.sem("split_hi"), w.sem("split_lo"))
        HB = D // R1
        with w.block() as block:
            @block.sync
            def _(sp):
                sp.dma_start(kcq[:], io["kcq"].rearrange("h (c p) k -> p h c k", p=P)).then_inc(w_in[0], DMA)
                sp.dma_start(wqr[:], io["wqr"].rearrange("h (c p) r -> p h c r", p=P)).then_inc(w_in[1], DMA)
                sp.dma_start(wq[:], io["wq1"].rearrange("(h k) d -> k h d", k=P)).then_inc(w_in[2], DMA)

            @block.tensor
            def _(pe):
                pe.wait_ge(w_in[0], DMA)
                pe.wait_ge(w_in[1], DMA)
                for h in range(H1):
                    for c in range(3):
                        last = pe.matmul(banks[h // HB][:, h % HB * R1:(h % HB + 1) * R1], kcq[:, h, c, :], wqr[:, h, c, :],
                                         start=c == 0, stop=c == 2)
                    if h % HB == HB - 1:
                        last.then_inc(made, 1)
                pe.wait_ge(w_in[2], DMA)
                for g in range(2):
                    pe.wait_ge(moved, g + 1)
                    for c in range(DC):
                        n = g * DC + c
                        if n >= 2:
                            pe.wait_ge(split_lo, n - 1)
                        for i in range(HB):
                            h = g * HB + i
                            last = pe.matmul(banks[2 + n % 2][:, i * R1:(i + 1) * R1], wq[:, h, c * P:(c + 1) * P],
                                             mid[:, h, :], start=True, stop=True)
                        last.then_inc(made, 1)

            @block.scalar
            def _(act):
                for g in range(2):
                    act.wait_ge(made, g + 1)
                    act.activation(mid[:, g * HB:(g + 1) * HB, :], banks[g][:, :].rearrange("p (h r) -> p h r", h=HB),
                                   ACT.Copy).then_inc(moved, 1)
                for n in range(2 * DC):
                    act.wait_ge(made, n + 3)
                    act.activation(A_h[:, n % DC, n // DC * D:(n // DC + 1) * D], banks[2 + n % 2][:, :], ACT.Copy
                                   ).then_inc(split_hi, 1)

            @block.vector
            def _(dve):
                for n in range(2 * DC):
                    cols = slice(n // DC * D, (n // DC + 1) * D)
                    dve.wait_ge(split_hi, n + 1)
                    dve.tensor_tensor(A_l[:, n % DC, cols], banks[2 + n % 2][:, :], f32(A_h[:, n % DC, cols]),
                                      ALU.subtract).then_inc(split_lo, 1)


def value_weights(nc, io, kr_h, kr_l, VO_h, VO_l):
    with Memory(nc, "cv") as w:
        kckv, wo, kr = w.sb("kckv", [P, H1, CTX]), w.sb("wo", [P, H1, D]), w.sb("kr", [P, H1 * R1])
        banks = [w.ps(f"bank{i}", [P, D]) for i in range(4)]
        w_in, made, split_hi, split_lo, kr_hi = (
            [w.sem(f"w_in{i}") for i in range(3)], w.sem("made"), w.sem("split_hi"), w.sem("split_lo"), w.sem("kr_hi"))
        with w.block() as block:
            @block.sync
            def _(sp):
                sp.dma_start(kckv[:], io["kckv"].rearrange("h k d -> k h d")).then_inc(w_in[0], DMA)
                sp.dma_start(wo[:], io["wo1"].rearrange("(h k) n -> k h n", k=P)).then_inc(w_in[1], DMA)
                sp.dma_start(kr[:], io["kr"]).then_inc(w_in[2], DMA)

            @block.tensor
            def _(pe):
                pe.wait_ge(w_in[0], DMA)
                pe.wait_ge(w_in[1], DMA)
                for h in range(H1):
                    if h >= 4:
                        pe.wait_ge(split_lo, h - 3)
                    pe.matmul(banks[h % 4][:, :], kckv[:, h, :], wo[:, h, :], start=True, stop=True).then_inc(made, 1)

            @block.scalar
            def _(act):
                act.wait_ge(w_in[2], DMA)
                act.activation(kr_h[:, :], kr[:, :], ACT.Copy).then_inc(kr_hi, 1)
                for h in range(H1):
                    act.wait_ge(made, h + 1)
                    act.activation(VO_h[:, h, :], banks[h % 4][:, :], ACT.Copy).then_inc(split_hi, 1)

            @block.vector
            def _(dve):
                dve.wait_ge(kr_hi, 1)
                dve.tensor_tensor(kr_l[:, :], kr[:, :], f32(kr_h[:, :]), ALU.subtract)
                for h in range(H1):
                    dve.wait_ge(split_hi, h + 1)
                    dve.tensor_tensor(VO_l[:, h, :], banks[h % 4][:, :], f32(VO_h[:, h, :]), ALU.subtract
                                      ).then_inc(split_lo, 1)


def layer1_attention(nc, io, X, mv, rstd, ident):
    with Memory(nc, "c") as m:
        A_h, A_l = m.sb("A_h", [P, DC, H1 * R1], F32R), m.sb("A_l", [P, DC, H1 * R1], F32R)
        score_weights(nc, io, A_h, A_l)
        kr_h, kr_l = m.sb("kr_h", [P, H1 * R1], F32R), m.sb("kr_l", [P, H1 * R1], F32R)
        VO_h, VO_l = m.sb("VO_h", [P, H1, D], F32R), m.sb("VO_l", [P, H1, D], F32R)
        value_weights(nc, io, kr_h, kr_l, VO_h, VO_l)
        inverse_deviations(nc, "cs", mv, rstd)

        table = m.sb("table", [P, 4, S])
        ctx_raw = m.sb("ctx_raw", [P, 4, S])
        ctx_sum = m.sb("ctx_sum", [P, 2, S])
        kv_h = [m.sb(f"kv_h{i}", [P, 2, S], F32R) for i in range(2)]
        kv_l = [m.sb(f"kv_l{i}", [P, 2, S], F32R) for i in range(2)]
        y = m.sb("y", [P, TPB, D])
        yT_h, yT_l = m.sb("yT_h", [P, DC, S], F32R), m.sb("yT_l", [P, DC, S], F32R)
        qk_h, qk_l = m.sb("qk_h", [P, 2 * S], F32R), m.sb("qk_l", [P, 2 * S], F32R)
        neg_max, sums, inv = m.sb("neg_max", [P, 4]), m.sb("sums", [P, 4]), m.sb("inv", [P, 4])
        probs = [m.sb(f"probs{i}", [P, 4, S]) for i in range(2)]
        pT_h, pT_l = m.sb("pT_h", [P, 2, 2 * S], F32R), m.sb("pT_l", [P, 2, 2 * S], F32R)
        c_h, c_l = m.sb("c_h", [P, 2 * S], F32R), m.sb("c_l", [P, 2 * S], F32R)
        stats, new_mv = m.sb("stats", [P, TPB, 6]), m.sb("new_mv", [P, TPB, 2])

        score = [m.ps(f"score{i}", [P, 2, S]) for i in range(2)]
        turn = [m.ps(f"turn{i}", [P, 2 * S]) for i in range(2)]
        bank_a, bank_b = m.ps("bank_a", [P, D]), m.ps("bank_b", [P, D])
        acc = [m.ps(f"acc{i}", [P, D]) for i in range(TPB)]

        table_in, ctx_in, kv_ready = m.sem("table_in"), m.sem("ctx_in"), m.sem("kv_ready")
        y_ready = m.sem("y_ready")
        a_made, a_hi, a_free = m.sem("a_made"), m.sem("a_hi"), m.sem("a_free")
        b_made, b_hi, b_free = m.sem("b_made"), m.sem("b_hi"), m.sem("b_free")
        scored, maxed, exped, normed = m.sem("scored"), m.sem("maxed"), m.sem("exped"), m.sem("normed")
        turned, turn_hi, turn_lo = m.sem("turned"), m.sem("turn_hi"), m.sem("turn_lo")
        outed, added = m.sem("outed"), m.sem("added")
        LASTP = PAIRS - 1

        def a_no(b, slot, what):
            if slot == -1:
                return ("lnt", "proj").index(what)
            return b * 9 + 2 + slot + (1 if slot == LASTP and what == "proj" else 0)

        def b_no(b, slot, what, last=False):
            if slot == -1:
                return 0
            return b * 9 + slot + (1 if slot == LASTP and what == "pv" and not last else 0)

        def first(n):
            return isinstance(n, int) and n <= 0

        def all_slots(slots):
            def run(eng):
                slots(0, 0, True, False)
                with eng.Fori(0, (B - 2) // 2) as r:
                    slots(2 * r + 1, 1, False, False)
                    slots(2 * r + 2, 0, False, False)
                slots(B - 1, (B - 1) % 2, False, True)
            return run

        with m.block() as block:
            @block.sync
            def _(sp):
                sp.dma_start(table[:], io["table"]).then_inc(table_in, DMA)
                sp.dma_start(ctx_raw[:], io["ctx1"][0:1, :, :, :].rearrange("b p a s -> p (b a) s")).then_inc(ctx_in, DMA)
                with sp.Fori(1, B) as b:
                    sp.wait_ge(kv_ready, b)
                    sp.dma_start(ctx_raw[:], io["ctx1"][bass.ds(b, 1), :, :, :].rearrange("b p a s -> p (b a) s")
                                 ).then_inc(ctx_in, DMA)

            @block.gpsimd
            def _(pool):
                def rope(b, par):
                    pool.wait_ge(ctx_in, (b + 1) * DMA)
                    if not isinstance(b, int) or b >= 2:
                        pool.wait_ge(b_made, b_no(b - 1, 0, "pv") + 1)
                    pool.tensor_tensor(ctx_raw[:], ctx_raw[:], table[:], ALU.mult)
                    pool.drain()
                    pool.tensor_tensor(ctx_sum[:], ctx_raw[:, 0:2, :], ctx_raw[:, 2:4, :], ALU.add)
                    pool.drain()
                    pool.tensor_copy(kv_h[par][:], ctx_sum[:])
                    pool.drain()
                    pool.tensor_tensor(kv_l[par][:], ctx_sum[:], f32(kv_h[par][:]), ALU.subtract).then_inc(kv_ready, 1)

                pool.wait_ge(table_in, DMA)
                rope(0, 0)
                rope(1, 1)
                with pool.Fori(1, B // 2) as r:
                    rope(2 * r, 0)
                    rope(2 * r + 1, 1)

            @block.tensor
            def _(pe):
                def transpose_y(b, t):
                    bank, free, n, made = ((bank_a, a_free, None, a_made), (bank_b, b_free, None, b_made))[t]
                    pe.wait_ge(y_ready, b * TPB + t + 1)
                    for c in range(DC):
                        last = pe.transpose(bank[:, c * P:(c + 1) * P], y[:, t, c * P:(c + 1) * P], ident[:, :])
                    last.then_inc(made, 1)

                def project(b, par, p, n):
                    pe.wait_ge(a_free, n)
                    cols = slice(p * P, (p + 1) * P)
                    products(pe, bank_a[:, 0:S], [(A_h[:, c, cols], A_l[:, c, cols], yT_h[:, c, :], yT_l[:, c, :])
                                                  for c in range(DC)])
                    products(pe, bank_a[:, S:2 * S], [(kr_h[:, cols], kr_l[:, cols], kv_h[par][:, 1, :], kv_l[par][:, 1, :])]
                             ).then_inc(a_made, 1)

                def scores(b, p, n_proj):
                    pe.wait_ge(a_free, n_proj + 1)
                    if not first(b * PAIRS + p):
                        pe.wait_ge(exped, b * PAIRS + p)
                    for h in range(2):
                        rows = slice(h * R1, (h + 1) * R1)
                        for t in range(TPB):
                            q = slice(t * P, (t + 1) * P)
                            products(pe, score[h][:, t, :], [(qk_h[rows, q], qk_l[rows, q], qk_h[rows, S:2 * S], qk_l[rows, S:2 * S])]
                                     ).then_inc(scored, 1)

                def transpose_probs(s, p):
                    pe.wait_ge(normed, s + 1)
                    for k in range(2):
                        if not first(s):
                            pe.wait_ge(turn_lo, 2 * s - 1 + k)
                        for hq in range(4):
                            last = pe.transpose(turn[k][:, hq * P:(hq + 1) * P], probs[p % 2][:, hq, k * P:(k + 1) * P], ident[:, :])
                        last.then_inc(turned, 1)

                def attend(s, par, n):
                    pe.wait_ge(b_free, n)
                    for k in range(2):
                        pe.wait_ge(turn_lo, 2 * s + k + 1)
                        kv = slice(k * P, (k + 1) * P)
                        pe.matmul(bank_b[:, :], kv_l[par][:, 0, kv], pT_h[:, k, :], start=k == 0, stop=False)
                        pe.matmul(bank_b[:, :], kv_h[par][:, 0, kv], pT_l[:, k, :], start=False, stop=False)
                        last = pe.matmul(bank_b[:, :], kv_h[par][:, 0, kv], pT_h[:, k, :], start=False, stop=k == 1)
                    last.then_inc(b_made, 1)

                def project_out(b, p, n_pv):
                    pe.wait_ge(b_free, n_pv + 1)
                    if p == 0 and not first(b):
                        pe.wait_ge(added, b * TPB)
                    for t in range(TPB):
                        last = products(pe, acc[t][:, :], [(c_h[:, h * S + t * P:h * S + (t + 1) * P],
                                                            c_l[:, h * S + t * P:h * S + (t + 1) * P],
                                                            VO_h[:, 2 * p + h, :], VO_l[:, 2 * p + h, :]) for h in range(2)],
                                        start=p == 0, stop=p == LASTP)
                        if p == LASTP:
                            last.then_inc(outed, 1)

                def slots(b, par, is_first, is_last):
                    for p in range(PAIRS):
                        s = b * PAIRS + p
                        n_proj = a_no(b, p - 1, "proj") if p > 0 else (1 if is_first else a_no(b - 1, LASTP, "proj"))
                        scores(b, p, n_proj)
                        if p == LASTP and not is_last:
                            pe.wait_ge(a_free, a_no(b, p, "lnt"))
                            transpose_y(b + 1, 0)
                            pe.wait_ge(b_free, b_no(b, p, "lnt"))
                            transpose_y(b + 1, 1)
                        if p > 0 or not is_first:
                            transpose_probs(s - 1, (p - 1) % 2)
                        if p < LASTP:
                            project(b, par, p + 1, a_no(b, p, "proj"))
                        if p >= 2:
                            project_out(b, p - 2, b_no(b, p - 1, "pv"))
                        elif not is_first:
                            project_out(b - 1, PAIRS - 2 + p, b_no(b - 1, LASTP, "pv") if p == 0 else b_no(b, 0, "pv"))
                        if p == LASTP and not is_last:
                            pe.wait_ge(b_free, b_no(b, p, "lnt") + 1)
                            pe.wait_ge(kv_ready, b + 2)
                            project(b + 1, 1 - par, 0, a_no(b, p, "proj"))
                        if p > 0 or not is_first:
                            attend(s - 1, par if p > 0 else 1 - par, b_no(b, p, "pv", is_last))

                transpose_y(0, 0)
                transpose_y(0, 1)
                pe.wait_ge(b_free, 1)
                pe.wait_ge(kv_ready, 1)
                project(0, 0, 0, 1)
                all_slots(slots)(pe)
                end = B - 1
                transpose_probs(B * PAIRS - 1, LASTP % 2)
                project_out(end, LASTP - 1, b_no(end, LASTP, "pv", True))
                attend(B * PAIRS - 1, end % 2, b_no(end, LASTP, "pv", True) + 1)
                project_out(end, LASTP, b_no(end, LASTP, "pv", True) + 1)

            @block.scalar
            def _(act):
                def split_y(t, n):
                    bank, made, hi = ((bank_a, a_made, a_hi), (bank_b, b_made, b_hi))[t]
                    act.wait_ge(made, n + 1)
                    act.activation(yT_h[:, :, t * P:(t + 1) * P], bank[:, :].rearrange("p (c t) -> p c t", c=DC), ACT.Copy
                                   ).then_inc(hi, 1)

                def split_proj(n):
                    act.wait_ge(a_made, n + 1)
                    act.activation(qk_h[:, :], bank_a[:, :], ACT.Copy).then_inc(a_hi, 1)

                def split_context(n):
                    act.wait_ge(b_made, n + 1)
                    act.activation(c_h[:, :], bank_b[:, :], ACT.Copy).then_inc(b_hi, 1)

                def split_probs(s):
                    for k in range(2):
                        act.wait_ge(turned, 2 * s + k + 1)
                        act.activation(pT_h[:, k, :], turn[k][:, :], ACT.Copy).then_inc(turn_hi, 1)

                def exponentials(s, p):
                    if not isinstance(s, int) or s >= 2:
                        act.wait_ge(turned, 2 * s - 2)
                    for h in range(2):
                        act.wait_ge(maxed, 2 * s + h + 1)
                        for t in range(TPB):
                            i = 2 * h + t
                            last = act.activation(probs[p % 2][:, i, :], score[h][:, t, :], ACT.Exp, bias=neg_max[:, i:i + 1],
                                                  accum_out=sums[:, i:i + 1])
                    last.then_inc(exped, 1)

                def slots(b, par, is_first, is_last):
                    for p in range(PAIRS):
                        s = b * PAIRS + p
                        if p == LASTP and not is_last:
                            split_y(0, a_no(b, p, "lnt"))
                            split_y(1, b_no(b, p, "lnt"))
                        if p > 0 or not is_first:
                            split_probs(s - 1)
                        exponentials(s, p)
                        if p < LASTP or not is_last:
                            split_proj(a_no(b, p, "proj"))
                        if p > 0 or not is_first:
                            split_context(b_no(b, p, "pv", is_last))

                split_y(0, 0)
                split_y(1, 0)
                split_proj(1)
                all_slots(slots)(act)
                split_probs(B * PAIRS - 1)
                split_context(b_no(B - 1, LASTP, "pv", True) + 1)

            @block.vector
            def _(dve):
                def normalise_y(b):
                    for t in range(TPB):
                        tile = b * TPB + t
                        dve.tensor_scalar(y[:, t, :], X[:, bass.ds(tile, 1), :].rearrange("p a d -> p (a d)"),
                                          mv[:, bass.ds(tile, 1), 0:1].rearrange("p a d -> p (a d)"),
                                          rstd[:, bass.ds(tile, 1)], ALU.subtract, ALU.mult).then_inc(y_ready, 1)

                def split_y(t, n):
                    bank, hi, free = ((bank_a, a_hi, a_free), (bank_b, b_hi, b_free))[t]
                    dve.wait_ge(hi, n + 1)
                    cols = slice(t * P, (t + 1) * P)
                    dve.tensor_tensor(yT_l[:, :, cols], bank[:, :].rearrange("p (c t) -> p c t", c=DC), f32(yT_h[:, :, cols]),
                                      ALU.subtract).then_inc(free, 1)

                def split_proj(n):
                    dve.wait_ge(a_hi, n + 1)
                    dve.tensor_tensor(qk_l[:, :], bank_a[:, :], f32(qk_h[:, :]), ALU.subtract).then_inc(a_free, 1)

                def split_context(n):
                    dve.wait_ge(b_hi, n + 1)
                    dve.tensor_tensor(c_l[:, :], bank_b[:, :], f32(c_h[:, :]), ALU.subtract).then_inc(b_free, 1)

                def split_probs(s):
                    for k in range(2):
                        dve.wait_ge(turn_hi, 2 * s + k + 1)
                        dve.tensor_tensor(pT_l[:, k, :], turn[k][:, :], f32(pT_h[:, k, :]), ALU.subtract).then_inc(turn_lo, 1)

                def maxima(s):
                    for h in range(2):
                        dve.wait_ge(scored, 4 * s + 2 * h + 2)
                        dve.tensor_reduce(neg_max[:, 2 * h:2 * h + 2], score[h][:, :, :], AX.X, ALU.max, negate=True
                                          ).then_inc(maxed, 1)

                def normalise(s, p):
                    dve.wait_ge(exped, s + 1)
                    dve.reciprocal(inv[:, :], sums[:, :])
                    dve.drain()
                    for i in range(4):
                        last = dve.tensor_scalar(probs[p % 2][:, i, :], probs[p % 2][:, i, :], inv[:, i:i + 1], None, ALU.mult)
                    last.then_inc(normed, 1)

                def add_output(b):
                    for t in range(TPB):
                        tile = b * TPB + t
                        xt = X[:, bass.ds(tile, 1), :].rearrange("p a d -> p (a d)")
                        dve.wait_ge(outed, b * TPB + t + 1)
                        dve.tensor_tensor(xt, xt, acc[t][:, :], ALU.add).then_inc(added, 1)
                        dve.drain()
                        tile_stats(dve, xt, stats[:, t, :], new_mv[:, t, :])
                        dve.drain()
                        dve.tensor_copy(mv[:, bass.ds(tile, 1), :].rearrange("p a d -> p (a d)"), new_mv[:, t, :])

                def slots(b, par, is_first, is_last):
                    for p in range(PAIRS):
                        s = b * PAIRS + p
                        maxima(s)
                        if p == LASTP and not is_last:
                            split_y(0, a_no(b, p, "lnt"))
                            split_y(1, b_no(b, p, "lnt"))
                        if p > 0 or not is_first:
                            split_probs(s - 1)
                        normalise(s, p)
                        if p < LASTP or not is_last:
                            split_proj(a_no(b, p, "proj"))
                        if p == LASTP - 1 and not is_last:
                            normalise_y(b + 1)
                        if p > 0 or not is_first:
                            split_context(b_no(b, p, "pv", is_last))
                        if p == 1 and not is_first:
                            add_output(b - 1)

                normalise_y(0)
                split_y(0, 0)
                split_y(1, 0)
                split_proj(1)
                all_slots(slots)(dve)
                split_probs(B * PAIRS - 1)
                split_context(b_no(B - 1, LASTP, "pv", True) + 1)
                add_output(B - 1)



def layer1_experts(nc, io, out_dram, X, mv, rstd, ident):
    G = E * EI
    GE = G + E
    with Memory(nc, "d") as m:
        wd_h, wd_l = m.sb("wd_h", [P, DC, GE], F32R), m.sb("wd_l", [P, DC, GE], F32R)
        wu_h, wu_l = m.sb("wu_h", [P, D], F32R), m.sb("wu_l", [P, D], F32R)
        iota = m.sb("iota", [P, E])
        with Memory(nc, "dw") as w:
            wd, wu = w.sb("wd", [P, DC, GE]), w.sb("wu", [P, D])
            w_in, split_hi = w.sem("w_in"), w.sem("split_hi")
            with w.block() as block:
                @block.sync
                def _(sp):
                    sp.dma_start(wd[:], io["wd"].rearrange("(c p) n -> p c n", p=P)).then_inc(w_in, DMA)
                    sp.dma_start(wu[:], io["wu"]).then_inc(w_in, DMA)
                    sp.dma_start(iota[:], io["iota"]).then_inc(w_in, DMA)

                @block.scalar
                def _(act):
                    act.wait_ge(w_in, 3 * DMA)
                    act.activation(wd_h[:], wd[:], ACT.Copy).then_inc(split_hi, 1)
                    act.activation(wu_h[:], wu[:], ACT.Copy).then_inc(split_hi, 1)

                @block.vector
                def _(dve):
                    dve.wait_ge(split_hi, 2)
                    dve.tensor_tensor(wd_l[:], wd[:], f32(wd_h[:]), ALU.subtract)
                    dve.tensor_tensor(wu_l[:], wu[:], f32(wu_h[:]), ALU.subtract)

        inverse_deviations(nc, "ds", mv, rstd)

        y = m.sb("y", [P, TPB, D])
        yT_h, yT_l = m.sb("yT_h", [P, TPB, DC, P], F32R), m.sb("yT_l", [P, TPB, DC, P], F32R)
        neg_max, sums = m.sb("neg_max", [P, TPB]), m.sb("sums", [P, TPB])
        weight, top, index = m.sb("weight", [P, TPB, E]), m.sb("top", [P, TPB, 8]), m.sb("index", [P, TPB, 8], U32)
        index_f, mask, gate = m.sb("index_f", [P, TPB, 8]), m.sb("mask", [P, TPB, E]), m.sb("gate", [P, TPB, E])
        sig, act_h = m.sb("sig", [P, TPB, G]), m.sb("act_h", [P, TPB, G])
        g_h, g_l = m.sb("g_h", [P, TPB * P], F32R), m.sb("g_l", [P, TPB * P], F32R)
        turn = m.ps("turn", [P, TPB, DC, P])
        hidden = m.ps("hidden", [P, TPB, S])
        turn_g = m.ps("turn_g", [P, 4 * P])
        up = m.ps("up", [P, TPB, D])
        y_ready, turned, y_hi, y_lo = m.sem("y_ready"), m.sem("turned"), m.sem("y_hi"), m.sem("y_lo")
        hid, maxed, exped, acted = m.sem("hid"), m.sem("maxed"), m.sem("exped"), m.sem("acted")
        g_ready, g_turned, g_hi, g_lo = m.sem("g_ready"), m.sem("g_turned"), m.sem("g_hi"), m.sem("g_lo")
        upped, added, stored = m.sem("upped"), m.sem("added"), m.sem("stored")

        def after(eng, sem, n):
            if not isinstance(n, int) or n > 0:
                eng.wait_ge(sem, n)

        with m.block() as block:
            @block.sync
            def _(sp):
                dst = out_dram.rearrange("(t p) d -> p t d", p=P)
                with sp.Fori(0, B) as b:
                    sp.wait_ge(added, b * TPB + TPB)
                    sp.dma_start(dst[:, bass.ds(b * TPB, TPB), :], X[:, bass.ds(b * TPB, TPB), :]).then_inc(stored, DMA)
                sp.wait_ge(stored, B * DMA)

            @block.tensor
            def _(pe):
                def front(b):
                    pe.wait_ge(y_ready, b + 1)
                    after(pe, y_lo, b)
                    for t in range(TPB):
                        for c in range(DC):
                            last = pe.transpose(turn[:, t, c, :], y[:, t, c * P:(c + 1) * P], ident[:, :])
                    last.then_inc(turned, 1)
                    pe.wait_ge(y_lo, b + 1)
                    after(pe, acted, b)
                    for t in range(TPB):
                        last = products(pe, hidden[:, t, 0:GE], [(yT_h[:, t, c, :], yT_l[:, t, c, :], wd_h[:, c, :], wd_l[:, c, :])
                                                                 for c in range(DC)])
                    last.then_inc(hid, 1)

                def back(b):
                    pe.wait_ge(g_ready, b + 1)
                    after(pe, g_lo, b)
                    for t in range(TPB):
                        last = pe.transpose(turn_g[:, t * P:(t + 1) * P], act_h[:, t, :], ident[:, :])
                    last.then_inc(g_turned, 1)
                    pe.wait_ge(g_lo, b + 1)
                    after(pe, added, b * TPB)
                    for t in range(TPB):
                        tok = slice(t * P, (t + 1) * P)
                        last = products(pe, up[:, t, :], [(g_h[:, tok], g_l[:, tok], wu_h[:, :], wu_l[:, :])])
                    last.then_inc(upped, 1)

                front(0)
                front(1)
                back(0)
                with pe.Fori(1, B - 1) as b:
                    front(b + 1)
                    back(b)
                back(B - 1)

            @block.scalar
            def _(act):
                def split_y(b):
                    act.wait_ge(turned, b + 1)
                    act.activation(yT_h[:], turn[:], ACT.Copy).then_inc(y_hi, 1)

                def gates(b):
                    act.wait_ge(hid, b + 1)
                    act.activation(sig[:], hidden[:, :, 0:G], ACT.Exp, scale=-1.0).then_inc(exped, 1)
                    act.wait_ge(maxed, b + 1)
                    for t in range(TPB):
                        last = act.activation(weight[:, t, :], hidden[:, t, G:GE], ACT.Exp, bias=neg_max[:, t:t + 1],
                                              accum_out=sums[:, t:t + 1])
                    last.then_inc(exped, 1)

                def split_g(b):
                    act.wait_ge(g_turned, b + 1)
                    act.activation(g_h[:, :], turn_g[:, 0:TPB * P], ACT.Copy).then_inc(g_hi, 1)

                split_y(0)
                gates(0)
                split_y(1)
                split_g(0)
                with act.Fori(1, B - 1) as b:
                    gates(b)
                    split_y(b + 1)
                    split_g(b)
                gates(B - 1)
                split_g(B - 1)

            @block.vector
            def _(dve):
                def normalise_y(b):
                    after(dve, turned, b)
                    for t in range(TPB):
                        tile = b * TPB + t
                        last = dve.tensor_scalar(y[:, t, :], X[:, bass.ds(tile, 1), :].rearrange("p a d -> p (a d)"),
                                                 mv[:, bass.ds(tile, 1), 0:1].rearrange("p a d -> p (a d)"),
                                                 rstd[:, bass.ds(tile, 1)], ALU.subtract, ALU.mult)
                    last.then_inc(y_ready, 1)

                def split_y(b):
                    dve.wait_ge(y_hi, b + 1)
                    dve.tensor_tensor(yT_l[:], turn[:], f32(yT_h[:]), ALU.subtract).then_inc(y_lo, 1)

                def router_max(b):
                    dve.wait_ge(exped, 2 * b + 1)
                    dve.tensor_reduce(neg_max[:, :], hidden[:, :, G:GE], AX.X, ALU.max, negate=True).then_inc(maxed, 1)

                def gates(b):
                    dve.tensor_scalar(sig[:], sig[:], 1.0, None, ALU.add)
                    dve.wait_ge(exped, 2 * b + 2)
                    dve.reciprocal(sums[:, :], sums[:, :])
                    dve.drain()
                    dve.reciprocal(sig[:], sig[:])
                    for t in range(TPB):
                        dve.tensor_scalar(weight[:, t, :], weight[:, t, :], sums[:, t:t + 1], None, ALU.mult)
                    dve.drain()
                    for t in range(TPB):
                        dve.max(top[:, t, :], weight[:, t, :])
                    dve.drain()
                    for t in range(TPB):
                        dve.max_index(index[:, t, :], top[:, t, :], weight[:, t, :])
                    dve.drain()
                    dve.tensor_copy(index_f[:], index[:])
                    dve.tensor_tensor(act_h[:], hidden[:, :, 0:G], sig[:], ALU.mult).then_inc(acted, 1)
                    dve.drain()
                    for t in range(TPB):
                        dve.tensor_scalar(mask[:, t, :], iota[:, :], index_f[:, t, 0:1], None, ALU.is_equal)
                    dve.drain()
                    for t in range(TPB):
                        dve.scalar_tensor_tensor(mask[:, t, :], iota[:, :], index_f[:, t, 1:2], mask[:, t, :],
                                                 ALU.is_equal, ALU.add)
                    dve.drain()
                    dve.tensor_tensor(gate[:], mask[:], weight[:], ALU.mult)
                    dve.drain()
                    units = act_h[:].rearrange("p t (e i) -> p (t e) i", e=E)
                    dve.tensor_tensor(units, units, gate[:].rearrange("p t e -> p (t e)").unsqueeze(2).broadcast_to([P, TPB * E, EI]),
                                      ALU.mult).then_inc(g_ready, 1)

                def split_g(b):
                    dve.wait_ge(g_hi, b + 1)
                    dve.tensor_tensor(g_l[:, :], turn_g[:, 0:TPB * P], f32(g_h[:, :]), ALU.subtract).then_inc(g_lo, 1)

                def add_output(b):
                    dve.wait_ge(upped, b + 1)
                    for t in range(TPB):
                        xt = X[:, bass.ds(b * TPB + t, 1), :].rearrange("p a d -> p (a d)")
                        dve.tensor_tensor(xt, xt, up[:, t, :], ALU.add).then_inc(added, 1)

                normalise_y(0)
                split_y(0)
                normalise_y(1)
                router_max(0)
                gates(0)
                split_y(1)
                split_g(0)
                with dve.Fori(1, B - 1) as b:
                    normalise_y(b + 1)
                    router_max(b)
                    gates(b)
                    split_y(b + 1)
                    split_g(b)
                    add_output(b - 1)
                router_max(B - 1)
                gates(B - 1)
                split_g(B - 1)
                add_output(B - 2)
                add_output(B - 1)


def program(nc, io, out, until=9):
    with Memory(nc, "g") as g:
        X = g.sb("x", [P, TILES, D])
        mv = g.sb("mean_var", [P, TILES, 2])
        rstd = g.sb("rstd", [P, TILES])
        ident = g.sb("ident", [P, P])
        identb = g.sb("identb", [P, P], BF16)
        layer0_attention(nc, io, X, mv, rstd, ident, identb)
        if until >= 2:
            layer0_feed_forward(nc, io, X, mv, rstd, ident, identb)
        if until >= 3:
            layer1_attention(nc, io, X, mv, rstd, ident)
        if until >= 4:
            layer1_experts(nc, io, out, X, mv, rstd, ident)
            return
        done = g.sem("done")
        with g.block() as block:
            @block.sync
            def _(sp):
                sp.dma_start(out.rearrange("(t p) d -> p t d", p=P), X[:, :, :]).then_inc(done, DMA)
                sp.wait_ge(done, DMA)



def arrays(x, ctx_512, L0_xattn_Wq, L0_xattn_Wkv_expand, L0_xattn_Wout, L0_ffn_W1, L0_ffn_W2, L1_xattn_Wq, L1_xattn_w_kc_q,
           L1_xattn_w_kc_kv, L1_xattn_W_qr, L1_xattn_W_kr, L1_xattn_Wo, L1_ffn_router_w, L1_ffn_down_w, L1_ffn_up_w):
    import numpy as np

    c = np.ascontiguousarray
    x, ctx = np.asarray(x), np.asarray(ctx_512)

    def tokens(a):
        return a.reshape(TPB, P, CTX).transpose(1, 0, 2).reshape(P, S)

    wo0 = np.asarray(L0_xattn_Wout).T.reshape(GROUPS, 4, HD0, D).transpose(1, 0, 2, 3).reshape(D, D)
    swapped = np.concatenate([ctx[..., CTX // 2:], ctx[..., :CTX // 2]], -1)
    ctx1 = np.stack([np.stack([tokens(ctx[b]), ctx[b].T, tokens(swapped[b]), swapped[b].T], 1) for b in range(B)])
    inv_freq = np.float32(1.0) / np.float32(10000.0) ** (np.arange(0, CTX, 2, dtype=np.float32) / np.float32(CTX))
    freqs = np.arange(S, dtype=np.float32)[:, None] * inv_freq[None, :]
    sin, cos = np.repeat(np.sin(freqs), 2, axis=-1), np.repeat(np.cos(freqs), 2, axis=-1)
    sin = sin * np.where(np.arange(CTX) < CTX // 2, -1, 1).astype(np.float32)
    table = np.stack([tokens(cos), cos.T, tokens(sin), sin.T], 1).astype(np.float32)
    causal = np.arange(P)[None, :] <= np.arange(P)[:, None]
    return {
        "x": c(x.reshape(B * S, D)),
        "ctxT": c(ctx.reshape(B * S, CTX).T),
        "wq0": c(np.asarray(L0_xattn_Wq).T),
        "wkv0": c(np.asarray(L0_xattn_Wkv_expand).T),
        "wo0": c(wo0),
        "ident": np.eye(P, dtype=np.float32),
        "mask": np.where(causal, 0.0, -2.0 ** 127).astype(np.float32),
        "w1": c(np.asarray(L0_ffn_W1).T),
        "w2": c(np.asarray(L0_ffn_W2).T),
        "kcq": c(np.asarray(L1_xattn_w_kc_q).transpose(0, 2, 1)),
        "wqr": c(L1_xattn_W_qr),
        "wq1": c(L1_xattn_Wq),
        "kckv": c(L1_xattn_w_kc_kv),
        "wo1": c(np.asarray(L1_xattn_Wo).T),
        "kr": c(np.asarray(L1_xattn_W_kr).transpose(1, 0, 2).reshape(CTX, H1 * R1)),
        "table": c(table),
        "ctx1": c(ctx1),
        "wd": c(np.concatenate([np.asarray(L1_ffn_down_w).reshape(E * EI, D).T, np.asarray(L1_ffn_router_w).T], 1)),
        "wu": c(np.asarray(L1_ffn_up_w).transpose(0, 2, 1).reshape(E * EI, D)),
        "iota": np.tile(np.arange(E, dtype=np.float32), (P, 1)),
    }


def kernel(**inputs):
    import concourse.bacc as bacc
    import numpy as np
    from concourse.bass_utils import run_bass_kernel_spmd

    nc = bacc.Bacc("TRN2", target_bir_lowering=False, num_devices=1)
    placed = arrays(**inputs)
    io = {n: nc.dram_tensor(f"in_{n}", a.shape, mybir.dt.from_np(a.dtype), kind="ExternalInput").ap()
          for n, a in placed.items()}
    out = nc.dram_tensor("out", (B * S, D), F32, kind="ExternalOutput").ap()
    program(nc, io, out)
    r = run_bass_kernel_spmd(nc, [{f"in_{n}": a for n, a in placed.items()}], core_ids=[0])
    return np.asarray(r.results[0]["out"]).reshape(B, S, D)
```

```python
from contextlib import ExitStack

import concourse.bass as bass
from concourse import mybir

F32 = mybir.dt.float32
F32R = mybir.dt.float32r
BF16 = mybir.dt.bfloat16
U32 = mybir.dt.uint32
ALU = mybir.AluOpType
ACT = mybir.ActivationFunctionType
AX = mybir.AxisListType

P = 128
B, S, D = 8, 256, 512
TPB = S // P
TILES = B * TPB
DC = D // P
CTX = 128
DMA = 16
EPS = 1e-5

H0, HD0 = 16, 32
GROUPS = H0 // 4
F = 2048
FC = F // P
MAGIC = 1.5 * 2.0 ** 23
H1, R1 = 16, 64
PAIRS = H1 // 2
E, EI = 8, 16


def products(pe, out, pairs, start=True, stop=True):
    last = None
    for n, (lh, ll, rh, rl) in enumerate(pairs):
        pe.matmul(out, ll, rh, start=start and n == 0, stop=False)
        pe.matmul(out, lh, rl, start=False, stop=False)
        last = pe.matmul(out, lh, rh, start=False, stop=stop and n == len(pairs) - 1)
    return last


def f32(ap):
    return ap.bitcast(F32)


class Memory:

    def __init__(self, nc, phase):
        self.nc, self.phase, self.stack = nc, phase, ExitStack()

    def __enter__(self):
        self.stack.__enter__()
        return self

    def __exit__(self, *a):
        return self.stack.__exit__(*a)

    def sb(self, name, shape, dt=F32):
        return self.stack.enter_context(self.nc.sbuf_tensor(f"{self.phase}_{name}", shape, dt))

    def ps(self, name, shape, dt=F32):
        return self.stack.enter_context(self.nc.psum_tensor(f"{self.phase}_{name}", shape, dt))

    def sem(self, name):
        return self.stack.enter_context(self.nc.semaphore(f"{self.phase}_{name}"))

    def block(self):
        return self.nc.Block()


class Store:
    UNIT = 4 * 1024

    def __init__(self, nc, memory, units):
        self.nc, self.offset = nc, -(-nc.sbuf_base // 32) * 32
        memory.sb("store", [P, units * self.UNIT // 4])

    def place(self, name, start, shape, dt=F32):
        return self.nc.alloc_sbuf_tensor_at(name, shape, dt, offset=self.offset + start * self.UNIT)[:]


def tile_stats(dve, x_tile, stats, mean_var):
    dve.bn_stats(stats, x_tile)
    dve.drain()
    return dve.bn_aggr(mean_var, stats)


def inverse_deviations(nc, phase, mv, rstd):
    with Memory(nc, phase) as m:
        var = m.sb("var", [P, TILES])
        dev = m.sb("dev", [P, TILES])
        sq = m.sb("sq", [P, TILES])
        var_ready, dev_ready = m.sem("var_ready"), m.sem("dev_ready")
        with m.block() as block:
            @block.vector
            def _(dve):
                dve.tensor_scalar(var[:, :], mv[:, :, 1], EPS, None, ALU.add).then_inc(var_ready, 1)
                dve.wait_ge(dev_ready, 1)
                dve.reciprocal(rstd[:, :], dev[:, :])
                dve.drain()
                dve.tensor_tensor(sq[:, :], rstd[:, :], rstd[:, :], ALU.mult)
                dve.drain()
                dve.tensor_tensor(sq[:, :], sq[:, :], var[:, :], ALU.mult)
                dve.drain()
                dve.tensor_scalar(sq[:, :], sq[:, :], -0.5, 1.5, ALU.mult, ALU.add)
                dve.drain()
                dve.tensor_tensor(rstd[:, :], rstd[:, :], sq[:, :], ALU.mult)

            @block.scalar
            def _(act):
                act.wait_ge(var_ready, 1)
                act.activation(dev[:, :], var[:, :], ACT.Sqrt).then_inc(dev_ready, 1)



SLOTS0 = [["proj0", "T3'", "proj1", "pv3'"],
          ["out0'", "T0", "out1'", "proj2", "pv0"],
          ["proj3", "T1", "v0", "pv1"],
          ["v1", "T2", "lnt0", "lnt1", "pv2"]]
BEGIN0 = ["lnt0", "lnt1", "proj0", "proj1", "proj2", "proj3", "v0", "v1", "lnt0", "lnt1"]
END0 = ["T3'", "pv3'", "out0'", "out1'"]
SPLIT0 = ("lnt", "proj", "pv")


def kind_of(step):
    return step.rstrip("'0123")


def slots_of(is_first=False, prepares=True, turns=True):
    left_out = ([x for slot in SLOTS0 for x in slot if "'" in x] if is_first else []) + (
        [] if prepares else ["proj0", "proj1", "proj2", "proj3", "v0", "v1"]) + ([] if turns else ["lnt0", "lnt1"])
    return [[x for x in slot if x not in left_out] for slot in SLOTS0]


class Numbering:

    def __init__(self):
        full = [x for slot in slots_of() for x in slot if x[0] != "T"]
        first = [x for slot in slots_of(is_first=True) for x in slot if x[0] != "T"]
        self.per = len(full)
        self.per_hi = sum(kind_of(x) in SPLIT0 for x in full)
        self.at0 = len(BEGIN0) - (self.per - len(first))
        self.hi0 = sum(kind_of(x) in SPLIT0 for x in BEGIN0) - (
            self.per_hi - sum(kind_of(x) in SPLIT0 for x in first))

    def begin(self, b, slots, skipped=0, skipped_hi=0):
        out = {}
        n, hi = self.at0 - skipped, self.hi0 - skipped_hi
        if isinstance(b, int) and b == 0:
            n, hi = len(BEGIN0), sum(kind_of(x) in SPLIT0 for x in BEGIN0)
        for slot in slots:
            for x in slot:
                if x[0] == "T":
                    continue
                out[x] = (b * self.per + n, b * self.per_hi + hi, n % 2 if self.per % 2 == 0 else None)
                n += 1
                hi += kind_of(x) in SPLIT0
        return out


def layer0_attention(nc, io, X, mv, rstd, ident, identb, store, w1_raw, w1_in):
    with Memory(nc, "a") as m:
        wq_h, wq_l, wo_h, wo_l = (store.place(name, at, [P, DC, D], F32R)
                                  for name, at in (("wq0_h", 8), ("wq0_l", 10), ("wo0_h", 14), ("wo0_l", 16)))
        wkv_h, wkv_l = store.place("wkv0_h", 12, [P, 2 * D], F32R), store.place("wkv0_l", 13, [P, 2 * D], F32R)
        maskb = m.sb("maskb", [P, P], BF16)

        with Memory(nc, "aw") as w:
            raw = w.sb("raw", [P, 5 * 1024])
            identf, maskf = ident, w.sb("maskf", [P, P])
            stats = w.sb("stats", [P, TILES, 6])
            raws = [raw[:, 0:2048].rearrange("p (c n) -> p c n", c=DC), raw[:, 2048:3072],
                    raw[:, 3072:5120].rearrange("p (c n) -> p c n", c=DC)]
            x_in, w_in, c_in = w.sem("x_in"), [w.sem(f"w_in{i}") for i in range(3)], w.sem("c_in")
            split_hi = w.sem("split_hi")
            XG = 4
            with w.block() as block:
                @block.sync
                def _(sp):
                    sp.dma_start(raws[0], io["wq0"].rearrange("(c p) n -> p c n", p=P)).then_inc(w_in[0], DMA)
                    sp.dma_start(raws[1], io["wkv0"]).then_inc(w_in[1], DMA)
                    sp.dma_start(raws[2], io["wo0"].rearrange("(c p) n -> p c n", p=P)).then_inc(w_in[2], DMA)
                    sp.dma_start(identf[:, :], io["ident"]).then_inc(c_in, DMA)
                    sp.dma_start(maskf[:, :], io["mask"]).then_inc(c_in, DMA)

                @block.gpsimd
                def _(pool):
                    pool.wait_ge(c_in, 2 * DMA)
                    pool.tensor_copy(identb[:, :], identf[:, :])
                    pool.tensor_copy(maskb[:, :], maskf[:, :])

                @block.scalar
                def _(act):
                    for g in range(TILES // XG):
                        act.dma_start(X[:, XG * g:XG * g + XG, :],
                                      io["x"].rearrange("(t p) d -> p t d", p=P)[:, XG * g:XG * g + XG, :]
                                      ).then_inc(x_in, DMA)
                    for i, hi in enumerate((wq_h, wkv_h, wo_h)):
                        act.wait_ge(w_in[i], DMA)
                        act.activation(hi[:], raws[i], ACT.Copy).then_inc(split_hi, 1)

                @block.vector
                def _(dve):
                    for i, (hi, lo) in enumerate(((wq_h, wq_l), (wkv_h, wkv_l), (wo_h, wo_l))):
                        dve.wait_ge(split_hi, i + 1)
                        dve.tensor_tensor(lo[:], raws[i], f32(hi[:]), ALU.subtract)
                    dve.wait_ge(x_in, TILES // XG * DMA)
                    for t in range(TILES):
                        dve.bn_stats(stats[:, t, :], X[:, t, :])
                    dve.drain()
                    for t in range(TILES):
                        dve.bn_aggr(mv[:, t, :], stats[:, t, :])

        inverse_deviations(nc, "as", mv, rstd)

        y = store.place("y0", 26, [P, TPB, D])
        yT_h, yT_l = m.sb("yT_h", [P, DC, S], F32R), m.sb("yT_l", [P, DC, S], F32R)
        ctx_raw = m.sb("ctx_raw", [P, S])
        cT_h, cT_l = m.sb("cT_h", [P, S], F32R), m.sb("cT_l", [P, S], F32R)
        qk_h, qk_l = m.sb("qk_h", [P, 2, GROUPS, S], F32R), m.sb("qk_l", [P, 2, GROUPS, S], F32R)
        q_stack, k_stack = (store.place(name, at, [96, 4, GROUPS, S], F32R)
                            for name, at in (("q_stack", 18), ("k_stack", 22)))
        V, next_V = m.sb("V", [P, TPB, D]), m.sb("next_V", [P, TPB, D])
        neg_max = m.sb("neg_max", [P, 8])
        sums, inv = m.sb("sums", [P, 8]), m.sb("inv", [P, 8])
        probs = [m.sb(f"probs{i}", [P, 4 * 3 * P]) for i in range(2)]
        pT = m.sb("pT", [P, 4, 3 * P])
        c_h, c_l = m.sb("c_h", [P, 4, S], F32R), m.sb("c_l", [P, 4, S], F32R)
        stats, new_mv = m.sb("stats", [P, TPB, 6]), m.sb("new_mv", [P, TPB, 2])

        s_q0, s_q1 = m.ps("s_q0", [P, 4, P]), m.ps("s_q1", [P, 4, S])
        t_k0, t_k1 = m.ps("t_k0", [P, 4, S]), m.ps("t_k1", [P, 4, P])
        work = [m.ps(f"work{i}", [P, D]) for i in range(2)]

        ctx_in, ctx_hi, ctx_split = m.sem("ctx_in"), m.sem("ctx_hi"), m.sem("ctx_split")
        y_ready, v_ready, v_moved = m.sem("y_ready"), m.sem("v_ready"), m.sem("v_moved")
        worked, work_hi, work_free = m.sem("worked"), m.sem("work_hi"), m.sem("work_free")
        stacked = [m.sem(f"stacked{j}") for j in range(4)]
        scored, maxed, exped, normed = m.sem("scored"), m.sem("maxed"), m.sem("exped"), m.sem("normed")
        turned, evac_act, evac_dve = m.sem("turned"), m.sem("evac_act"), m.sem("evac_dve")

        SCALE = float(HD0) ** -0.5
        numbers = Numbering()
        in_begin = {}
        for n, x in enumerate(BEGIN0):
            in_begin[x, n // 8] = (n, sum(kind_of(z) in SPLIT0 for z in BEGIN0[:n]), n % 2)
        L = B - 1
        count = lambda slots: (sum(x[0] != "T" for s in slots for x in s),
                               sum(kind_of(x) in SPLIT0 for s in slots for x in s))
        short = tuple(a - c for a, c in zip(count(slots_of()), count(slots_of(turns=False))))

        def all_batches(eng, begin, slots, end):
            begin()
            slots(0, slots_of(is_first=True), numbers.begin(0, slots_of(is_first=True)))
            with eng.Fori(1, B - 2) as b:
                slots(b, slots_of(), numbers.begin(b, slots_of()))
            slots(L - 1, slots_of(turns=False), numbers.begin(L - 1, slots_of(turns=False)))
            last = slots_of(prepares=False, turns=False)
            at = numbers.begin(L, last, *short)
            slots(L, last, at)
            n, hi = max(v[0] for v in at.values()) + 1, max(v[1] for v in at.values()) + 1
            end({"pv3'": (n, hi, n % 2), "out0'": (n + 1, None, (n + 1) % 2), "out1'": (n + 2, None, n % 2)})

        with m.block() as block:
            @block.sync
            def _(sp):
                def load_context(nb):
                    if not isinstance(nb, int) or nb > 0:
                        sp.wait_ge(ctx_split, nb)
                    sp.dma_start(ctx_raw[:, :], io["ctxT"][:, bass.ts(nb, S)]).then_inc(ctx_in, DMA)

                def stack(b, n_proj3, is_begin=False):
                    sp.wait_ge(work_free, n_proj3 + 1)
                    for j in range(4):
                        if not is_begin:
                            sp.wait_ge(scored, (b * 4 + j) * 2 + 2)
                        src = slice(32 * j, 32 * j + 32)
                        for r, (q, k) in enumerate(((qk_h, qk_h), (qk_l, qk_h), (qk_h, qk_l))):
                            dst = slice(32 * r, 32 * r + 32)
                            sp.dma_start(f32(q_stack[dst, j, :, :]), f32(q[src, 0, :, :])).then_inc(stacked[j], DMA)
                            sp.dma_start(f32(k_stack[dst, j, :, :]), f32(k[src, 1, :, :])).then_inc(stacked[j], DMA)

                def begin():
                    load_context(0)
                    stack(0, in_begin["proj3", 0][0], True)
                    load_context(1)

                def slots(b, steps, at):
                    if "lnt0" in at:
                        load_context(b + 2)
                    if "proj3" in at:
                        stack(b, at["proj3"][0])
                all_batches(sp, begin, slots, lambda at: None)

            @block.tensor
            def _(pe):
                def scores(b, i):
                    slot = b * 4 + i
                    pe.wait_ge(stacked[i], (b + 1) * 6 * DMA)
                    if not isinstance(slot, int) or slot > 0:
                        pe.wait_ge(exped, 2 * slot - 1)
                    for h in range(4):
                        pe.matmul(s_q0[:, h, :], q_stack[:, i, h, 0:P], k_stack[:, i, h, 0:P], start=True, stop=False)
                        last = pe.matmul(s_q0[:, h, :], identb[:, :], maskb[:, :], start=False, stop=True)
                    last.then_inc(scored, 1)
                    if not isinstance(slot, int) or slot > 0:
                        pe.wait_ge(exped, 2 * slot)
                    for h in range(4):
                        pe.matmul(s_q1[:, h, :], q_stack[:, i, h, P:S], k_stack[:, i, h, :], start=True, stop=False)
                        last = pe.matmul(s_q1[:, h, P:S], identb[:, :], maskb[:, :], start=False, stop=True)
                    last.then_inc(scored, 1)

                def transpose_probs(slot, i):
                    pe.wait_ge(normed, slot + 1)
                    if not isinstance(slot, int) or slot > 0:
                        pe.wait_ge(evac_act, slot)
                        pe.wait_ge(evac_dve, slot)
                    p0 = probs[i % 2][:, 0:4 * P].rearrange("p (h k) -> p h k", h=4)
                    p1 = probs[i % 2][:, 4 * P:12 * P].rearrange("p (h k) -> p h k", h=4)
                    for h in range(4):
                        pe.transpose(t_k0[:, h, 0:P], p0[:, h, :], ident[:, :])
                        last = pe.transpose(t_k0[:, h, P:S], p1[:, h, 0:P], ident[:, :])
                    last.then_inc(turned, 1)
                    for h in range(4):
                        last = pe.transpose(t_k1[:, h, :], p1[:, h, P:S], ident[:, :])
                    last.then_inc(turned, 1)

                def piece(step, n, bank, slot, nb, ready):
                    kind, i = kind_of(step), int(step.strip("'")[-1])
                    out = work[bank]
                    if not isinstance(n, int) or n >= 2:
                        pe.wait_ge(work_free, n - 1)
                    if kind == "lnt":
                        pe.wait_ge(y_ready, nb * TPB + i + 1)
                        for c in range(DC):
                            last = pe.transpose(out[:, c * P:(c + 1) * P], y[:, i, c * P:(c + 1) * P], ident[:, :])
                    elif kind == "proj":
                        if i == 0:
                            pe.wait_ge(work_free, ready)
                            pe.wait_ge(ctx_split, nb + 1)
                        cols = slice(i * P, (i + 1) * P)
                        products(pe, out[:, 0:S], [(wq_h[:, c, cols], wq_l[:, c, cols], yT_h[:, c, :], yT_l[:, c, :])
                                                   for c in range(DC)])
                        last = products(pe, out[:, S:2 * S], [(wkv_h[:, cols], wkv_l[:, cols], cT_h[:, :], cT_l[:, :])])
                    elif kind == "v":
                        tok = slice(i * P, (i + 1) * P)
                        last = products(pe, out[:, :], [(cT_h[:, tok], cT_l[:, tok], wkv_h[:, D:2 * D], wkv_l[:, D:2 * D])])
                    elif kind == "pv":
                        pe.wait_ge(evac_act, slot + 1)
                        if i == 0:
                            pe.wait_ge(v_moved, nb)
                        for h in range(4):
                            head = slice((4 * h + i) * HD0, (4 * h + i + 1) * HD0)
                            rows = slice(32 * h, 32 * h + 32)
                            pe.matmul(out[rows, 0:S], V[:, 0, head], pT[:, h, 0:S], start=True, stop=False,
                                      tile_position=(0, 32 * h))
                        pe.wait_ge(evac_dve, slot + 1)
                        for h in range(4):
                            head = slice((4 * h + i) * HD0, (4 * h + i + 1) * HD0)
                            rows = slice(32 * h, 32 * h + 32)
                            last = pe.matmul(out[rows, P:S], V[:, 1, head], pT[:, h, S:S + P], start=False, stop=True,
                                             tile_position=(0, 32 * h))
                    elif kind == "out":
                        if i == 0:
                            pe.wait_ge(work_free, ready)
                        tok = slice(i * P, (i + 1) * P)
                        last = products(pe, out[:, :], [(c_h[:, j, tok], c_l[:, j, tok], wo_h[:, j, :], wo_l[:, j, :])
                                                        for j in range(4)])
                    last.then_inc(worked, 1)

                def begin():
                    for n, x in enumerate(BEGIN0):
                        piece(x, n, n % 2, None, n // 8, in_begin["lnt1", 0][0] + 1)

                def slots(b, steps, at):
                    for i, slot_steps in enumerate(steps):
                        scores(b, i)
                        for x in slot_steps:
                            slot = b * 4 + i - 1
                            if x[0] == "T":
                                transpose_probs(slot, (i - 1) % 4)
                                continue
                            if kind_of(x) == "proj":
                                nb = b + 1
                                ready = in_begin["lnt1", 1][0] + 1 if isinstance(b, int) and b == 0 else (
                                    next(iter(at.values()))[0] - 1)
                            elif kind_of(x) == "lnt":
                                nb, ready = b + 2, None
                            elif kind_of(x) == "out":
                                nb, ready = b - 1, at["pv3'"][0] + 1
                            else:
                                nb, ready = b + 1, None
                            piece(x, at[x][0], at[x][2], slot, nb, ready)

                def end(at):
                    transpose_probs(B * 4 - 1, 3)
                    for x in at:
                        piece(x, at[x][0], at[x][2], B * 4 - 1, B, at["pv3'"][0] + 1)
                all_batches(pe, begin, slots, end)

            @block.scalar
            def _(act):
                act.dma_start(w1_raw, io["w1"].rearrange("(c p) n -> p c n", p=P)).then_inc(w1_in, DMA)

                def split_context(nb, n_v1):
                    act.wait_ge(ctx_in, (nb + 1) * DMA)
                    if n_v1 is not None:
                        act.wait_ge(worked, n_v1 + 1)
                    act.activation(cT_h[:, :], ctx_raw[:, :], ACT.Copy).then_inc(ctx_hi, 1)

                def exponentials(slot, i, part):
                    act.wait_ge(maxed, 2 * slot + part + 1)
                    if part == 0 and (not isinstance(slot, int) or slot >= 2):
                        act.wait_ge(turned, 2 * slot - 2)
                    src, width = ((s_q0, P), (s_q1, S))[part]
                    for h in range(4):
                        at = part * 4 * P + h * width
                        m_at = part * 4 + h
                        last = act.activation(probs[i % 2][:, at:at + width], src[:, h, :], ACT.Exp,
                                              bias=neg_max[:, m_at:m_at + 1], scale=SCALE,
                                              accum_out=sums[:, m_at:m_at + 1])
                    last.then_inc(exped, 1)

                def copy_probs(slot):
                    act.wait_ge(turned, 2 * slot + 1)
                    act.activation(pT[:, :, 0:S], t_k0[:, :, :], ACT.Copy).then_inc(evac_act, 1)

                def split(step, n, bank, nb):
                    kind, i, out = kind_of(step), int(step.strip("'")[-1]), work[bank]
                    act.wait_ge(worked, n + 1)
                    if kind == "lnt":
                        hi = act.activation(yT_h[:, :, i * P:(i + 1) * P], out[:, :].rearrange("p (c t) -> p c t", c=DC),
                                            ACT.Copy)
                    elif kind == "proj":
                        if i == 0 and nb is not None:
                            for s in stacked:
                                act.wait_ge(s, nb * 6 * DMA)
                        hi = act.activation(qk_h[:, :, i, :], out[:, :].rearrange("p (a t) -> p a t", a=2), ACT.Copy)
                    else:
                        hi = act.activation(c_h[:, i, :], out[:, 0:S], ACT.Copy)
                    hi.then_inc(work_hi, 1)

                def move_values(nb):
                    act.wait_ge(v_ready, 2 * (nb + 1))
                    act.activation(V[:], next_V[:], ACT.Copy).then_inc(v_moved, 1)

                def begin():
                    split_context(0, None)
                    for n, x in enumerate(BEGIN0):
                        if n == 8:
                            split_context(1, in_begin["v1", 0][0])
                        if kind_of(x) in SPLIT0:
                            split(x, n, n % 2, None)

                def slots(b, steps, at):
                    for i, slot_steps in enumerate(steps):
                        slot = b * 4 + i
                        todo = [x for x in slot_steps if kind_of(x) in SPLIT0]
                        turned = any(x[0] == "T" for x in slot_steps)
                        early = [x for x in todo if not turned or slot_steps.index(x) == 0]
                        exponentials(slot, i, 0)
                        for x in early:
                            split(x, at[x][0], at[x][2], b + 1)
                        exponentials(slot, i, 1)
                        if turned:
                            copy_probs(slot - 1)
                        for x in todo[len(early):]:
                            split(x, at[x][0], at[x][2], b + 1)
                        if i == 0:
                            move_values(b)
                        if i == 3 and "lnt0" in at:
                            split_context(b + 2, at["v1"][0])

                def end(at):
                    copy_probs(B * 4 - 1)
                    split("pv3'", at["pv3'"][0], at["pv3'"][2], None)
                all_batches(act, begin, slots, end)

            @block.vector
            def _(dve):
                def normalise_y(nb):
                    for t in range(TPB):
                        tile = nb * TPB + t
                        dve.tensor_scalar(y[:, t, :], X[:, bass.ds(tile, 1), :].rearrange("p a d -> p (a d)"),
                                          mv[:, bass.ds(tile, 1), 0:1].rearrange("p a d -> p (a d)"),
                                          rstd[:, bass.ds(tile, 1)], ALU.subtract, ALU.mult).then_inc(y_ready, 1)

                def split_context(nb):
                    dve.wait_ge(ctx_hi, nb + 1)
                    dve.tensor_tensor(cT_l[:, :], ctx_raw[:, :], f32(cT_h[:, :]), ALU.subtract).then_inc(ctx_split, 1)

                def maxima(slot):
                    for part, src in enumerate((s_q0, s_q1)):
                        cols = neg_max[:, 4 * part:4 * part + 4]
                        dve.wait_ge(scored, 2 * slot + part + 1)
                        dve.tensor_reduce(cols, src[:, :, :], AX.X, ALU.max, negate=True)
                        dve.drain()
                        dve.tensor_scalar(cols, cols, SCALE, None, ALU.mult).then_inc(maxed, 1)

                def normalise(slot, i):
                    dve.wait_ge(exped, 2 * slot + 2)
                    dve.reciprocal(inv[:, :], sums[:, :])
                    dve.drain()
                    p0 = probs[i % 2][:, 0:4 * P].rearrange("p (h k) -> p h k", h=4)
                    p1 = probs[i % 2][:, 4 * P:12 * P].rearrange("p (h k) -> p h k", h=4)
                    for h in range(4):
                        dve.tensor_scalar(p0[:, h, :], p0[:, h, :], inv[:, h:h + 1], None, ALU.mult)
                    for h in range(4):
                        last = dve.tensor_scalar(p1[:, h, :], p1[:, h, :], inv[:, 4 + h:5 + h], None, ALU.mult)
                    last.then_inc(normed, 1)

                def copy_probs(slot):
                    dve.wait_ge(turned, 2 * slot + 2)
                    dve.tensor_copy(pT[:, :, S:S + P], t_k1[:, :, :]).then_inc(evac_dve, 1)

                def piece(step, n, n_hi, bank, nb):
                    kind, i, out = kind_of(step), int(step.strip("'")[-1]), work[bank]
                    if kind in SPLIT0:
                        dve.wait_ge(work_hi, n_hi + 1)
                        if kind == "lnt":
                            hi = yT_h[:, :, i * P:(i + 1) * P]
                            lo, src = yT_l[:, :, i * P:(i + 1) * P], out[:, :].rearrange("p (c t) -> p c t", c=DC)
                        elif kind == "proj":
                            hi, lo = qk_h[:, :, i, :], qk_l[:, :, i, :]
                            src = out[:, :].rearrange("p (a t) -> p a t", a=2)
                        else:
                            hi, lo, src = c_h[:, i, :], c_l[:, i, :], out[:, 0:S]
                        dve.tensor_tensor(lo, src, f32(hi), ALU.subtract).then_inc(work_free, 1)
                        return
                    dve.wait_ge(worked, n + 1)
                    if kind == "v":
                        if i == 0 and nb is not None:
                            dve.wait_ge(v_moved, nb)
                        dve.tensor_copy(next_V[:, i, :], out[:, :]).then_inc(work_free, 1)
                        dve.drain().then_inc(v_ready, 1)
                    else:
                        tile = nb * TPB + i
                        xt = X[:, bass.ds(tile, 1), :].rearrange("p a d -> p (a d)")
                        dve.tensor_tensor(xt, xt, out[:, :], ALU.add).then_inc(work_free, 1)

                def new_stats(nb):
                    for i in range(TPB):
                        xt = X[:, bass.ds(nb * TPB + i, 1), :].rearrange("p a d -> p (a d)")
                        dve.bn_stats(stats[:, i, :], xt)
                    dve.drain()
                    for i in range(TPB):
                        dve.bn_aggr(new_mv[:, i, :], stats[:, i, :])
                    dve.drain()
                    dve.tensor_copy(mv[:, bass.ds(nb * TPB, TPB), :], new_mv[:, :, :])

                def begin():
                    normalise_y(0)
                    split_context(0)
                    for n, x in enumerate(BEGIN0):
                        if n == 2:
                            normalise_y(1)
                        if n == 8:
                            split_context(1)
                        piece(x, n, in_begin[x, n // 8][1], n % 2, None)

                def slots(b, steps, at):
                    for i, slot_steps in enumerate(steps):
                        slot = b * 4 + i
                        maxima(slot)
                        for n_step, x in enumerate(slot_steps):
                            if n_step == 2:
                                normalise(slot, i)
                            if x[0] == "T":
                                copy_probs(slot - 1)
                            else:
                                piece(x, *at[x], b - 1 if "'" in x else b + 1)
                        if len(slot_steps) <= 2:
                            normalise(slot, i)
                        if i == 3 and any("'" in x for x in at):
                            new_stats(b - 1)
                        if i == 2 and "lnt0" in at:
                            normalise_y(b + 2)
                        if i == 3 and "lnt0" in at:
                            split_context(b + 2)

                def end(at):
                    copy_probs(B * 4 - 1)
                    for x in at:
                        piece(x, *at[x], B - 1)
                    dve.drain()
                    new_stats(B - 1)
                all_batches(dve, begin, slots, end)



def quantise_weights(nc, io, w1_raw, w2_raw, w1, w2, mean, w1_in):
    CH = 4
    with Memory(nc, "bw") as w:
        raw, dst = ([a.rearrange("p c n -> p (c n)").rearrange("p (c n) -> p c n", c=CH) for a in pair]
                    for pair in ((w1_raw, w2_raw), (w1, w2)))
        part, total = w.sb("part", [P, 2, CH]), w.sb("total", [P, 2])
        ones, scale = w.sb("ones", [P, P]), w.sb("scale", [P, 2])
        all_sums = w.ps("all_sums", [P, 2])
        w2_in, ones_ready = w.sem("w2_in"), w.sem("ones_ready")
        act_summed, summed, crossed, rounded = w.sem("act_summed"), w.sem("summed"), w.sem("crossed"), w.sem("rounded")
        with w.block() as block:
            @block.sync
            def _(sp):
                for c in range(CH):
                    sp.dma_start(w2_raw[:, c * FC // CH:(c + 1) * FC // CH, :],
                                 io["w2"].rearrange("(k c p) n -> k p c n", p=P, k=CH)[c]).then_inc(w2_in, DMA)

            @block.gpsimd
            def _(pool):
                pool.memset(ones[:, :], 1.0).then_inc(ones_ready, 1)

            def arrived(eng, i):
                if i == 0:
                    eng.wait_ge(w1_in, DMA)
                else:
                    eng.wait_ge(w2_in, CH * DMA)

            @block.tensor
            def _(pe):
                pe.wait_ge(ones_ready, 1)
                for i in range(2):
                    pe.wait_ge(summed, i + 1)
                    pe.matmul(all_sums[:, i:i + 1], ones[:, :], total[:, i:i + 1], start=True, stop=True).then_inc(crossed, 1)

            @block.vector
            def _(dve):
                def sums(i):
                    arrived(dve, i)
                    for c in range(CH // 2):
                        dve.tensor_reduce(part[:, i, c:c + 1], raw[i][:, c, :], AX.X, ALU.add, apply_absolute_value=True)
                    dve.drain()
                    dve.wait_ge(act_summed, i + 1)
                    dve.tensor_reduce(total[:, i:i + 1], part[:, i, :], AX.X, ALU.add).then_inc(summed, 1)
                    dve.wait_ge(crossed, i + 1)
                    dve.tensor_scalar(mean[:, i:i + 1], all_sums[:, i:i + 1], 1.0 / (F * D), 1e-5, ALU.mult, ALU.max)
                    dve.drain()
                    dve.reciprocal(scale[:, i:i + 1], mean[:, i:i + 1])
                    dve.drain()

                for i in range(2):
                    sums(i)
                    for c in range(CH):
                        dve.tensor_scalar(raw[i][:, c, :], raw[i][:, c, :], scale[:, i:i + 1], 1.0, ALU.mult, ALU.min)
                        dve.drain()
                        dve.tensor_scalar(raw[i][:, c, :], raw[i][:, c, :], -1.0, MAGIC, ALU.max, ALU.add).then_inc(rounded, 1)

            @block.scalar
            def _(act):
                for i in range(2):
                    arrived(act, i)
                    for c in range(CH // 2, CH):
                        last = act.activation(dst[i][:, c, :], raw[i][:, c, :], ACT.Abs, accum_out=part[:, i, c:c + 1])
                    last.then_inc(act_summed, 1)
                    for c in range(CH):
                        act.wait_ge(rounded, i * CH + c + 1)
                        act.activation(dst[i][:, c, :], raw[i][:, c, :], ACT.Copy, bias=-MAGIC)


def layer0_feed_forward(nc, io, X, mv, rstd, ident, identb, store, w1_raw, w1_in, ahead, ahead_in):
    with Memory(nc, "b") as m:
        w2_raw = store.place("w2_raw", 8, [P, FC, D])
        w1, w2 = store.place("w1", 18, [P, DC, F], BF16), store.place("w2", 22, [P, FC, D], BF16)
        mean = m.sb("mean", [P, 2])
        quantise_weights(nc, io, w1_raw, w2_raw, w1, w2, mean, w1_in)
        inverse_deviations(nc, "bs", mv, rstd)

        y, yr = m.sb("y", [P, D]), m.sb("yr", [P, D])
        xq = [m.sb(f"xq{i}", [P, D], BF16) for i in range(2)]
        xqT = m.sb("xqT", [P, DC, P], BF16)
        s1, s2 = m.sb("s1", [P, 2]), m.sb("s2", [P, 2])
        h = [m.sb(f"h{i}", [P, F]) for i in range(2)]
        hr, hq = m.sb("hr", [P, F]), m.sb("hq", [P, F], BF16)
        hqT = m.sb("hqT", [P, FC, P], BF16)
        amax, unit, q_scale = m.sb("amax", [P, 2]), m.sb("unit", [P, 2]), m.sb("q_scale", [P, 2])
        stats, new_mv = m.sb("stats", [P, 6]), m.sb("new_mv", [P, 2])
        up = m.ps("up", [P, F])
        xT = m.ps("xT", [P, DC, P], BF16)
        hT = m.ps("hT", [P, FC, P], BF16)
        down = m.ps("down", [P, D])
        x_quant, x_turned, x_copied = m.sem("x_quant"), m.sem("x_turned"), m.sem("x_copied")
        upped, silued = m.sem("upped"), m.sem("silued")
        h_scaled, h_rounded, h_quant = m.sem("h_scaled"), m.sem("h_rounded"), m.sem("h_quant")
        h_turned, h_copied, downed, added = m.sem("h_turned"), m.sem("h_copied"), m.sem("downed"), m.sem("added")
        HALF = FC // 2

        def all_steps(eng, step):
            for t in range(-3, 1):
                step(t, t % 2, t)
            with eng.Fori(0, (TILES - 4) // 2) as r:
                step(2 * r + 1, 1, None)
                step(2 * r + 2, 0, None)
            for t in range(TILES - 3, TILES):
                step(t, t % 2, t)

        def has(t, ahead):
            return t is None or 0 <= t + ahead < TILES

        def after(eng, sem, n):
            if not isinstance(n, int) or n > 0:
                eng.wait_ge(sem, n)

        with m.block() as block:
            @block.sync
            def _(sp):
                wq, kcq, wqr, kckv = ahead
                sp.dma_start(kcq, io["kcq"].rearrange("h (c p) k -> p h c k", p=P)).then_inc(ahead_in, DMA)
                sp.dma_start(wqr, io["wqr"].rearrange("h (c p) r -> p h c r", p=P)).then_inc(ahead_in, DMA)
                sp.dma_start(wq, io["wq1"].rearrange("(h k) d -> k h d", k=P)).then_inc(ahead_in, DMA)
                sp.dma_start(kckv, io["kckv"].rearrange("h k d -> k h d")).then_inc(ahead_in, DMA)

            @block.tensor
            def _(pe):
                def step(t, par, at):
                    if has(at, 0):
                        pe.wait_ge(h_quant, t + 1)
                        after(pe, h_copied, 2 * t)
                        for c in range(FC):
                            last = pe.transpose(hT[:, c, :], hq[:, c * P:(c + 1) * P], identb[:, :])
                            if c == HALF - 1:
                                last.then_inc(h_turned, 1)
                        last.then_inc(h_turned, 1)
                    if has(at, 2):
                        pe.wait_ge(x_copied, t + 3)
                        for n in range(4):
                            if n % 2 == 0:
                                after(pe, silued, 2 * t + 3 + n // 2)
                            for c in range(DC):
                                last = pe.matmul(up[:, n * D:(n + 1) * D], xqT[:, c, :], w1[:, c, n * D:(n + 1) * D],
                                                 start=c == 0, stop=c == DC - 1)
                            if n % 2:
                                last.then_inc(upped, 1)
                    if has(at, 0):
                        after(pe, added, t)
                        for c in range(FC):
                            if c % HALF == 0:
                                pe.wait_ge(h_copied, 2 * t + 1 + c // HALF)
                            last = pe.matmul(down[:, :], hqT[:, c, :], w2[:, c, :], start=c == 0, stop=c == FC - 1)
                        last.then_inc(downed, 1)
                    if has(at, 3):
                        pe.wait_ge(x_quant, t + 4)
                        after(pe, x_copied, t + 3)
                        for c in range(DC):
                            last = pe.transpose(xT[:, c, :], xq[1 - par][:, c * P:(c + 1) * P], identb[:, :])
                        last.then_inc(x_turned, 1)
                all_steps(pe, step)

            @block.scalar
            def _(act):
                def step(t, par, at):
                    if has(at, 0):
                        for i in range(2):
                            act.wait_ge(h_turned, 2 * t + i + 1)
                            act.activation(hqT[:, i * HALF:(i + 1) * HALF, :], hT[:, i * HALF:(i + 1) * HALF, :], ACT.Copy
                                           ).then_inc(h_copied, 1)
                    if has(at, 1):
                        act.wait_ge(h_scaled, t + 2)
                        after(act, h_quant, t + 1)
                        act.activation(hr[:, :], h[1 - par][:, :], ACT.Copy, scale=q_scale[:, 1:2], bias=MAGIC
                                       ).then_inc(h_rounded, 1)
                    if has(at, 2):
                        for n in range(2):
                            act.wait_ge(upped, 2 * t + n + 5)
                            cols = slice(n * F // 2, (n + 1) * F // 2)
                            act.activation(h[par][:, cols], up[:, cols], ACT.Silu, scale=s1[:, par:par + 1]
                                           ).then_inc(silued, 1)
                    if has(at, 3):
                        act.wait_ge(x_turned, t + 4)
                        act.activation(xqT[:], xT[:], ACT.Copy).then_inc(x_copied, 1)
                all_steps(act, step)

            @block.vector
            def _(dve):
                def scales(i):
                    dve.drain()
                    dve.tensor_scalar(unit[:, i:i + 1], amax[:, i:i + 1], 1e-5, 1.0 / 127.0, ALU.max, ALU.mult)
                    dve.drain()
                    return dve.reciprocal(q_scale[:, i:i + 1], unit[:, i:i + 1])

                def add_output(t, par):
                    dve.wait_ge(downed, t + 1)
                    xt = X[:, bass.ds(t, 1), :].rearrange("p a d -> p (a d)")
                    dve.scalar_tensor_tensor(xt, down[:, :], s2[:, par:par + 1], xt, ALU.mult, ALU.add
                                             ).then_inc(added, 1)

                def scale_hidden(t, par):
                    dve.wait_ge(silued, 2 * t + 2)
                    dve.tensor_reduce(amax[:, 1:2], h[par][:, :], AX.X, ALU.max, apply_absolute_value=True)
                    scales(1).then_inc(h_scaled, 1)
                    dve.tensor_scalar(s2[:, par:par + 1], unit[:, 1:2], mean[:, 1:2], None, ALU.mult)

                def quantise_tokens(t, par):
                    after(dve, x_turned, t - 1)
                    dve.tensor_scalar(y[:, :], X[:, bass.ds(t, 1), :].rearrange("p a d -> p (a d)"),
                                      mv[:, bass.ds(t, 1), 0:1].rearrange("p a d -> p (a d)"),
                                      rstd[:, bass.ds(t, 1)], ALU.subtract, ALU.mult)
                    dve.drain()
                    dve.tensor_reduce(amax[:, 0:1], y[:, :], AX.X, ALU.max, apply_absolute_value=True)
                    scales(0)
                    dve.tensor_scalar(s1[:, par:par + 1], unit[:, 0:1], mean[:, 0:1], None, ALU.mult)
                    dve.drain()
                    dve.tensor_scalar(yr[:, :], y[:, :], q_scale[:, 0:1], MAGIC, ALU.mult, ALU.add)
                    dve.drain()
                    dve.tensor_scalar(xq[par][:, :], yr[:, :], -MAGIC, 127.0, ALU.add, ALU.min).then_inc(x_quant, 1)

                def quantise_hidden(t):
                    dve.wait_ge(h_rounded, t + 1)
                    after(dve, h_turned, 2 * t)
                    dve.tensor_scalar(hq[:, :], hr[:, :], -MAGIC, 127.0, ALU.add, ALU.min).then_inc(h_quant, 1)

                def new_stats(t):
                    xt = X[:, bass.ds(t, 1), :].rearrange("p a d -> p (a d)")
                    tile_stats(dve, xt, stats[:, :], new_mv[:, :])
                    dve.drain()
                    dve.tensor_copy(mv[:, bass.ds(t, 1), :].rearrange("p a d -> p (a d)"), new_mv[:, :])

                def step(t, par, at):
                    if has(at, -1):
                        add_output(t - 1, 1 - par)
                    if has(at, 1):
                        scale_hidden(t + 1, 1 - par)
                    if has(at, 3):
                        quantise_tokens(t + 3, 1 - par)
                    if has(at, 1):
                        quantise_hidden(t + 1)
                    else:
                        dve.drain()
                    if has(at, -1):
                        new_stats(t - 1)
                all_steps(dve, step)
                add_output(TILES - 1, (TILES - 1) % 2)
                dve.drain()
                new_stats(TILES - 1)



def score_weights(nc, io, A_h, A_l, ahead, ahead_in, wo, wo_in):
    with Memory(nc, "cw") as w:
        wq, kcq, wqr, _ = ahead
        mid = w.sb("mid", [P, H1, R1])
        banks = [w.ps(f"bank{i}", [P, D]) for i in range(4)]
        made, moved, split_hi, split_lo = w.sem("made"), w.sem("moved"), w.sem("split_hi"), w.sem("split_lo")
        HB = D // R1
        with w.block() as block:
            @block.sync
            def _(sp):
                sp.wait_ge(made, 2)
                sp.dma_start(wo, io["wo1"].rearrange("(h k) n -> k h n", k=P)).then_inc(wo_in, DMA)

            @block.tensor
            def _(pe):
                pe.wait_ge(ahead_in, 4 * DMA)
                for h in range(H1):
                    for c in range(3):
                        last = pe.matmul(banks[h // HB][:, h % HB * R1:(h % HB + 1) * R1], kcq[:, h, c, :], wqr[:, h, c, :],
                                         start=c == 0, stop=c == 2)
                    if h % HB == HB - 1:
                        last.then_inc(made, 1)
                for g in range(2):
                    pe.wait_ge(moved, g + 1)
                    for c in range(DC):
                        n = g * DC + c
                        if n >= 2:
                            pe.wait_ge(split_lo, n - 1)
                        for i in range(HB):
                            h = g * HB + i
                            last = pe.matmul(banks[2 + n % 2][:, i * R1:(i + 1) * R1], wq[:, h, c * P:(c + 1) * P],
                                             mid[:, h, :], start=True, stop=True)
                        last.then_inc(made, 1)

            @block.scalar
            def _(act):
                for g in range(2):
                    act.wait_ge(made, g + 1)
                    act.activation(mid[:, g * HB:(g + 1) * HB, :], banks[g][:, :].rearrange("p (h r) -> p h r", h=HB),
                                   ACT.Copy).then_inc(moved, 1)
                for n in range(2 * DC):
                    act.wait_ge(made, n + 3)
                    act.activation(A_h[:, n % DC, n // DC * D:(n // DC + 1) * D], banks[2 + n % 2][:, :], ACT.Copy
                                   ).then_inc(split_hi, 1)

            @block.vector
            def _(dve):
                for n in range(2 * DC):
                    cols = slice(n // DC * D, (n // DC + 1) * D)
                    dve.wait_ge(split_hi, n + 1)
                    dve.tensor_tensor(A_l[:, n % DC, cols], banks[2 + n % 2][:, :], f32(A_h[:, n % DC, cols]),
                                      ALU.subtract).then_inc(split_lo, 1)


def value_weights(nc, io, kr_h, kr_l, VO_h, VO_l, kckv, wo, wo_in):
    with Memory(nc, "cv") as w:
        kr = w.sb("kr", [P, H1 * R1])
        banks = [w.ps(f"bank{i}", [P, D]) for i in range(4)]
        kr_in, made, split_hi, split_lo, kr_hi = (
            w.sem("kr_in"), w.sem("made"), w.sem("split_hi"), w.sem("split_lo"), w.sem("kr_hi"))
        with w.block() as block:
            @block.sync
            def _(sp):
                sp.dma_start(kr[:], io["kr"]).then_inc(kr_in, DMA)

            @block.tensor
            def _(pe):
                pe.wait_ge(wo_in, DMA)
                for h in range(H1):
                    if h >= 4:
                        pe.wait_ge(split_lo, h - 3)
                    pe.matmul(banks[h % 4][:, :], kckv[:, h, :], wo[:, h, :], start=True, stop=True).then_inc(made, 1)

            @block.scalar
            def _(act):
                act.wait_ge(kr_in, DMA)
                act.activation(kr_h[:, :], kr[:, :], ACT.Copy).then_inc(kr_hi, 1)
                for h in range(H1):
                    act.wait_ge(made, h + 1)
                    act.activation(VO_h[:, h, :], banks[h % 4][:, :], ACT.Copy).then_inc(split_hi, 1)

            @block.vector
            def _(dve):
                dve.wait_ge(kr_hi, 1)
                dve.tensor_tensor(kr_l[:, :], kr[:, :], f32(kr_h[:, :]), ALU.subtract)
                for h in range(H1):
                    dve.wait_ge(split_hi, h + 1)
                    dve.tensor_tensor(VO_l[:, h, :], banks[h % 4][:, :], f32(VO_h[:, h, :]), ALU.subtract
                                      ).then_inc(split_lo, 1)


def layer1_attention(nc, io, X, mv, rstd, ident, store, ahead, ahead_in):
    with Memory(nc, "c") as m:
        A_h, A_l = (store.place(name, at, [P, DC, H1 * R1], F32R) for name, at in (("A_h", 18), ("A_l", 22)))
        VO_h, VO_l = (store.place(name, at, [P, H1, D], F32R) for name, at in (("VO_h", 0), ("VO_l", 8)))
        wo, wo_in = store.place("wo1", 8, [P, H1, D]), m.sem("wo_in")
        score_weights(nc, io, A_h, A_l, ahead, ahead_in, wo, wo_in)
        kr_h, kr_l = m.sb("kr_h", [P, H1 * R1], F32R), m.sb("kr_l", [P, H1 * R1], F32R)
        value_weights(nc, io, kr_h, kr_l, VO_h, VO_l, ahead[3], wo, wo_in)
        inverse_deviations(nc, "cs", mv, rstd)

        table = m.sb("table", [P, 4, S])
        ctx_raw = m.sb("ctx_raw", [P, 4, S])
        ctx_sum = m.sb("ctx_sum", [P, 2, S])
        kv_h = [m.sb(f"kv_h{i}", [P, 2, S], F32R) for i in range(2)]
        kv_l = [m.sb(f"kv_l{i}", [P, 2, S], F32R) for i in range(2)]
        y = m.sb("y", [P, TPB, D])
        yT_h, yT_l = m.sb("yT_h", [P, DC, S], F32R), m.sb("yT_l", [P, DC, S], F32R)
        qk_h, qk_l = m.sb("qk_h", [P, 2 * S], F32R), m.sb("qk_l", [P, 2 * S], F32R)
        neg_max, sums, inv = m.sb("neg_max", [P, 4]), m.sb("sums", [P, 4]), m.sb("inv", [P, 4])
        probs = [m.sb(f"probs{i}", [P, 4, S]) for i in range(2)]
        pT_h, pT_l = m.sb("pT_h", [P, 2, 2 * S], F32R), m.sb("pT_l", [P, 2, 2 * S], F32R)
        c_h, c_l = m.sb("c_h", [P, 2 * S], F32R), m.sb("c_l", [P, 2 * S], F32R)
        stats, new_mv = m.sb("stats", [P, TPB, 6]), m.sb("new_mv", [P, TPB, 2])

        score = [m.ps(f"score{i}", [P, 2, S]) for i in range(2)]
        turn = [m.ps(f"turn{i}", [P, 2 * S]) for i in range(2)]
        bank_a, bank_b = m.ps("bank_a", [P, D]), m.ps("bank_b", [P, D])
        acc = [m.ps(f"acc{i}", [P, D]) for i in range(TPB)]

        table_in, ctx_in, kv_ready = m.sem("table_in"), m.sem("ctx_in"), m.sem("kv_ready")
        y_ready = m.sem("y_ready")
        a_made, a_hi, a_free = m.sem("a_made"), m.sem("a_hi"), m.sem("a_free")
        b_made, b_hi, b_free = m.sem("b_made"), m.sem("b_hi"), m.sem("b_free")
        scored, maxed, exped, normed = m.sem("scored"), m.sem("maxed"), m.sem("exped"), m.sem("normed")
        turned, turn_hi, turn_lo = m.sem("turned"), m.sem("turn_hi"), m.sem("turn_lo")
        outed, added = m.sem("outed"), m.sem("added")
        LASTP = PAIRS - 1

        def a_no(b, slot, what):
            if slot == -1:
                return ("lnt", "proj").index(what)
            return b * 9 + 2 + slot + (1 if slot == LASTP and what == "proj" else 0)

        def b_no(b, slot, what, last=False):
            if slot == -1:
                return 0
            return b * 9 + slot + (1 if slot == LASTP and what == "pv" and not last else 0)

        def first(n):
            return isinstance(n, int) and n <= 0

        def all_slots(slots):
            def run(eng):
                slots(0, 0, True, False)
                with eng.Fori(0, (B - 2) // 2) as r:
                    slots(2 * r + 1, 1, False, False)
                    slots(2 * r + 2, 0, False, False)
                slots(B - 1, (B - 1) % 2, False, True)
            return run

        with m.block() as block:
            @block.sync
            def _(sp):
                sp.dma_start(table[:], io["table"]).then_inc(table_in, DMA)
                sp.dma_start(ctx_raw[:], io["ctx1"][0:1, :, :, :].rearrange("b p a s -> p (b a) s")).then_inc(ctx_in, DMA)
                with sp.Fori(1, B) as b:
                    sp.wait_ge(kv_ready, b)
                    sp.dma_start(ctx_raw[:], io["ctx1"][bass.ds(b, 1), :, :, :].rearrange("b p a s -> p (b a) s")
                                 ).then_inc(ctx_in, DMA)

            @block.gpsimd
            def _(pool):
                def rope(b, par):
                    pool.wait_ge(ctx_in, (b + 1) * DMA)
                    if not isinstance(b, int) or b >= 2:
                        pool.wait_ge(b_made, b_no(b - 1, 0, "pv") + 1)
                    pool.tensor_tensor(ctx_raw[:], ctx_raw[:], table[:], ALU.mult)
                    pool.drain()
                    pool.tensor_tensor(ctx_sum[:], ctx_raw[:, 0:2, :], ctx_raw[:, 2:4, :], ALU.add)
                    pool.drain()
                    pool.tensor_copy(kv_h[par][:], ctx_sum[:])
                    pool.drain()
                    pool.tensor_tensor(kv_l[par][:], ctx_sum[:], f32(kv_h[par][:]), ALU.subtract).then_inc(kv_ready, 1)

                pool.wait_ge(table_in, DMA)
                rope(0, 0)
                rope(1, 1)
                with pool.Fori(1, B // 2) as r:
                    rope(2 * r, 0)
                    rope(2 * r + 1, 1)

            @block.tensor
            def _(pe):
                def transpose_y(b, t):
                    bank, free, n, made = ((bank_a, a_free, None, a_made), (bank_b, b_free, None, b_made))[t]
                    pe.wait_ge(y_ready, b * TPB + t + 1)
                    for c in range(DC):
                        last = pe.transpose(bank[:, c * P:(c + 1) * P], y[:, t, c * P:(c + 1) * P], ident[:, :])
                    last.then_inc(made, 1)

                def project(b, par, p, n):
                    pe.wait_ge(a_free, n)
                    cols = slice(p * P, (p + 1) * P)
                    products(pe, bank_a[:, 0:S], [(A_h[:, c, cols], A_l[:, c, cols], yT_h[:, c, :], yT_l[:, c, :])
                                                  for c in range(DC)])
                    products(pe, bank_a[:, S:2 * S], [(kr_h[:, cols], kr_l[:, cols], kv_h[par][:, 1, :], kv_l[par][:, 1, :])]
                             ).then_inc(a_made, 1)

                def scores(b, p, n_proj):
                    pe.wait_ge(a_free, n_proj + 1)
                    if not first(b * PAIRS + p):
                        pe.wait_ge(exped, b * PAIRS + p)
                    for h in range(2):
                        rows = slice(h * R1, (h + 1) * R1)
                        for t in range(TPB):
                            q = slice(t * P, (t + 1) * P)
                            products(pe, score[h][:, t, :], [(qk_h[rows, q], qk_l[rows, q], qk_h[rows, S:2 * S], qk_l[rows, S:2 * S])]
                                     ).then_inc(scored, 1)

                def transpose_probs(s, p):
                    pe.wait_ge(normed, s + 1)
                    for k in range(2):
                        if not first(s):
                            pe.wait_ge(turn_lo, 2 * s - 1 + k)
                        for hq in range(4):
                            last = pe.transpose(turn[k][:, hq * P:(hq + 1) * P], probs[p % 2][:, hq, k * P:(k + 1) * P], ident[:, :])
                        last.then_inc(turned, 1)

                def attend(s, par, n):
                    pe.wait_ge(b_free, n)
                    for k in range(2):
                        pe.wait_ge(turn_lo, 2 * s + k + 1)
                        kv = slice(k * P, (k + 1) * P)
                        pe.matmul(bank_b[:, :], kv_l[par][:, 0, kv], pT_h[:, k, :], start=k == 0, stop=False)
                        pe.matmul(bank_b[:, :], kv_h[par][:, 0, kv], pT_l[:, k, :], start=False, stop=False)
                        last = pe.matmul(bank_b[:, :], kv_h[par][:, 0, kv], pT_h[:, k, :], start=False, stop=k == 1)
                    last.then_inc(b_made, 1)

                def project_out(b, p, n_pv):
                    pe.wait_ge(b_free, n_pv + 1)
                    if p == 0 and not first(b):
                        pe.wait_ge(added, b * TPB)
                    for t in range(TPB):
                        last = products(pe, acc[t][:, :], [(c_h[:, h * S + t * P:h * S + (t + 1) * P],
                                                            c_l[:, h * S + t * P:h * S + (t + 1) * P],
                                                            VO_h[:, 2 * p + h, :], VO_l[:, 2 * p + h, :]) for h in range(2)],
                                        start=p == 0, stop=p == LASTP)
                        if p == LASTP:
                            last.then_inc(outed, 1)

                def slots(b, par, is_first, is_last):
                    for p in range(PAIRS):
                        s = b * PAIRS + p
                        n_proj = a_no(b, p - 1, "proj") if p > 0 else (1 if is_first else a_no(b - 1, LASTP, "proj"))
                        scores(b, p, n_proj)
                        if p == LASTP and not is_last:
                            pe.wait_ge(a_free, a_no(b, p, "lnt"))
                            transpose_y(b + 1, 0)
                            pe.wait_ge(b_free, b_no(b, p, "lnt"))
                            transpose_y(b + 1, 1)
                        if p > 0 or not is_first:
                            transpose_probs(s - 1, (p - 1) % 2)
                        if p < LASTP:
                            project(b, par, p + 1, a_no(b, p, "proj"))
                        if p >= 2:
                            project_out(b, p - 2, b_no(b, p - 1, "pv"))
                        elif not is_first:
                            project_out(b - 1, PAIRS - 2 + p, b_no(b - 1, LASTP, "pv") if p == 0 else b_no(b, 0, "pv"))
                        if p == LASTP and not is_last:
                            pe.wait_ge(b_free, b_no(b, p, "lnt") + 1)
                            pe.wait_ge(kv_ready, b + 2)
                            project(b + 1, 1 - par, 0, a_no(b, p, "proj"))
                        if p > 0 or not is_first:
                            attend(s - 1, par if p > 0 else 1 - par, b_no(b, p, "pv", is_last))

                transpose_y(0, 0)
                transpose_y(0, 1)
                pe.wait_ge(b_free, 1)
                pe.wait_ge(kv_ready, 1)
                project(0, 0, 0, 1)
                all_slots(slots)(pe)
                end = B - 1
                transpose_probs(B * PAIRS - 1, LASTP % 2)
                project_out(end, LASTP - 1, b_no(end, LASTP, "pv", True))
                attend(B * PAIRS - 1, end % 2, b_no(end, LASTP, "pv", True) + 1)
                project_out(end, LASTP, b_no(end, LASTP, "pv", True) + 1)

            @block.scalar
            def _(act):
                def split_y(t, n):
                    bank, made, hi = ((bank_a, a_made, a_hi), (bank_b, b_made, b_hi))[t]
                    act.wait_ge(made, n + 1)
                    act.activation(yT_h[:, :, t * P:(t + 1) * P], bank[:, :].rearrange("p (c t) -> p c t", c=DC), ACT.Copy
                                   ).then_inc(hi, 1)

                def split_proj(n):
                    act.wait_ge(a_made, n + 1)
                    act.activation(qk_h[:, :], bank_a[:, :], ACT.Copy).then_inc(a_hi, 1)

                def split_context(n):
                    act.wait_ge(b_made, n + 1)
                    act.activation(c_h[:, :], bank_b[:, :], ACT.Copy).then_inc(b_hi, 1)

                def split_probs(s):
                    for k in range(2):
                        act.wait_ge(turned, 2 * s + k + 1)
                        act.activation(pT_h[:, k, :], turn[k][:, :], ACT.Copy).then_inc(turn_hi, 1)

                def exponentials(s, p):
                    if not isinstance(s, int) or s >= 2:
                        act.wait_ge(turned, 2 * s - 2)
                    for h in range(2):
                        act.wait_ge(maxed, 2 * s + h + 1)
                        for t in range(TPB):
                            i = 2 * h + t
                            last = act.activation(probs[p % 2][:, i, :], score[h][:, t, :], ACT.Exp, bias=neg_max[:, i:i + 1],
                                                  accum_out=sums[:, i:i + 1])
                    last.then_inc(exped, 1)

                def slots(b, par, is_first, is_last):
                    for p in range(PAIRS):
                        s = b * PAIRS + p
                        if p == LASTP and not is_last:
                            split_y(0, a_no(b, p, "lnt"))
                            split_y(1, b_no(b, p, "lnt"))
                        if p > 0 or not is_first:
                            split_probs(s - 1)
                        exponentials(s, p)
                        if p < LASTP or not is_last:
                            split_proj(a_no(b, p, "proj"))
                        if p > 0 or not is_first:
                            split_context(b_no(b, p, "pv", is_last))

                split_y(0, 0)
                split_y(1, 0)
                split_proj(1)
                all_slots(slots)(act)
                split_probs(B * PAIRS - 1)
                split_context(b_no(B - 1, LASTP, "pv", True) + 1)

            @block.vector
            def _(dve):
                def normalise_y(b):
                    for t in range(TPB):
                        tile = b * TPB + t
                        dve.tensor_scalar(y[:, t, :], X[:, bass.ds(tile, 1), :].rearrange("p a d -> p (a d)"),
                                          mv[:, bass.ds(tile, 1), 0:1].rearrange("p a d -> p (a d)"),
                                          rstd[:, bass.ds(tile, 1)], ALU.subtract, ALU.mult).then_inc(y_ready, 1)

                def split_y(t, n):
                    bank, hi, free = ((bank_a, a_hi, a_free), (bank_b, b_hi, b_free))[t]
                    dve.wait_ge(hi, n + 1)
                    cols = slice(t * P, (t + 1) * P)
                    dve.tensor_tensor(yT_l[:, :, cols], bank[:, :].rearrange("p (c t) -> p c t", c=DC), f32(yT_h[:, :, cols]),
                                      ALU.subtract).then_inc(free, 1)

                def split_proj(n):
                    dve.wait_ge(a_hi, n + 1)
                    dve.tensor_tensor(qk_l[:, :], bank_a[:, :], f32(qk_h[:, :]), ALU.subtract).then_inc(a_free, 1)

                def split_context(n):
                    dve.wait_ge(b_hi, n + 1)
                    dve.tensor_tensor(c_l[:, :], bank_b[:, :], f32(c_h[:, :]), ALU.subtract).then_inc(b_free, 1)

                def split_probs(s):
                    for k in range(2):
                        dve.wait_ge(turn_hi, 2 * s + k + 1)
                        dve.tensor_tensor(pT_l[:, k, :], turn[k][:, :], f32(pT_h[:, k, :]), ALU.subtract).then_inc(turn_lo, 1)

                def maxima(s):
                    for h in range(2):
                        dve.wait_ge(scored, 4 * s + 2 * h + 2)
                        dve.tensor_reduce(neg_max[:, 2 * h:2 * h + 2], score[h][:, :, :], AX.X, ALU.max, negate=True
                                          ).then_inc(maxed, 1)

                def normalise(s, p):
                    dve.wait_ge(exped, s + 1)
                    dve.reciprocal(inv[:, :], sums[:, :])
                    dve.drain()
                    for i in range(4):
                        last = dve.tensor_scalar(probs[p % 2][:, i, :], probs[p % 2][:, i, :], inv[:, i:i + 1], None, ALU.mult)
                    last.then_inc(normed, 1)

                def add_output(b):
                    for t in range(TPB):
                        tile = b * TPB + t
                        xt = X[:, bass.ds(tile, 1), :].rearrange("p a d -> p (a d)")
                        dve.wait_ge(outed, b * TPB + t + 1)
                        dve.tensor_tensor(xt, xt, acc[t][:, :], ALU.add).then_inc(added, 1)
                        dve.drain()
                        tile_stats(dve, xt, stats[:, t, :], new_mv[:, t, :])
                        dve.drain()
                        dve.tensor_copy(mv[:, bass.ds(tile, 1), :].rearrange("p a d -> p (a d)"), new_mv[:, t, :])

                def slots(b, par, is_first, is_last):
                    for p in range(PAIRS):
                        s = b * PAIRS + p
                        maxima(s)
                        if p == LASTP and not is_last:
                            split_y(0, a_no(b, p, "lnt"))
                            split_y(1, b_no(b, p, "lnt"))
                        if p > 0 or not is_first:
                            split_probs(s - 1)
                        normalise(s, p)
                        if p < LASTP or not is_last:
                            split_proj(a_no(b, p, "proj"))
                        if p == LASTP - 1 and not is_last:
                            normalise_y(b + 1)
                        if p > 0 or not is_first:
                            split_context(b_no(b, p, "pv", is_last))
                        if p == 1 and not is_first:
                            add_output(b - 1)

                normalise_y(0)
                split_y(0, 0)
                split_y(1, 0)
                split_proj(1)
                all_slots(slots)(dve)
                split_probs(B * PAIRS - 1)
                split_context(b_no(B - 1, LASTP, "pv", True) + 1)
                add_output(B - 1)



def layer1_experts(nc, io, out_dram, X, mv, rstd, ident):
    G = E * EI
    GE = G + E
    with Memory(nc, "d") as m:
        wd_h, wd_l = m.sb("wd_h", [P, DC, GE], F32R), m.sb("wd_l", [P, DC, GE], F32R)
        wu_h, wu_l = m.sb("wu_h", [P, D], F32R), m.sb("wu_l", [P, D], F32R)
        iota = m.sb("iota", [P, E])
        with Memory(nc, "dw") as w:
            wd, wu = w.sb("wd", [P, DC, GE]), w.sb("wu", [P, D])
            w_in, split_hi = w.sem("w_in"), w.sem("split_hi")
            with w.block() as block:
                @block.sync
                def _(sp):
                    sp.dma_start(wd[:], io["wd"].rearrange("(c p) n -> p c n", p=P)).then_inc(w_in, DMA)
                    sp.dma_start(wu[:], io["wu"]).then_inc(w_in, DMA)
                    sp.dma_start(iota[:], io["iota"]).then_inc(w_in, DMA)

                @block.scalar
                def _(act):
                    act.wait_ge(w_in, 3 * DMA)
                    act.activation(wd_h[:], wd[:], ACT.Copy).then_inc(split_hi, 1)
                    act.activation(wu_h[:], wu[:], ACT.Copy).then_inc(split_hi, 1)

                @block.vector
                def _(dve):
                    dve.wait_ge(split_hi, 2)
                    dve.tensor_tensor(wd_l[:], wd[:], f32(wd_h[:]), ALU.subtract)
                    dve.tensor_tensor(wu_l[:], wu[:], f32(wu_h[:]), ALU.subtract)

        inverse_deviations(nc, "ds", mv, rstd)

        y = m.sb("y", [P, TPB, D])
        yT_h, yT_l = m.sb("yT_h", [P, TPB, DC, P], F32R), m.sb("yT_l", [P, TPB, DC, P], F32R)
        neg_max, sums = m.sb("neg_max", [P, TPB]), m.sb("sums", [P, TPB])
        weight, top, index = m.sb("weight", [P, TPB, E]), m.sb("top", [P, TPB, 8]), m.sb("index", [P, TPB, 8], U32)
        index_f, mask, gate = m.sb("index_f", [P, TPB, 8]), m.sb("mask", [P, TPB, E]), m.sb("gate", [P, TPB, E])
        act_h = m.sb("act_h", [P, TPB, G])
        g_h, g_l = m.sb("g_h", [P, TPB * P], F32R), m.sb("g_l", [P, TPB * P], F32R)
        turn = m.ps("turn", [P, TPB, DC, P])
        hidden = [m.ps(f"hidden{i}", [P, TPB, S]) for i in range(2)]
        turn_g = m.ps("turn_g", [P, 4 * P])
        up = m.ps("up", [P, TPB, D])
        y_ready, turned, y_hi, y_lo = m.sem("y_ready"), m.sem("turned"), m.sem("y_hi"), m.sem("y_lo")
        hid, acted, maxed, exped = m.sem("hid"), m.sem("acted"), m.sem("maxed"), m.sem("exped")
        g_ready, g_turned, g_hi, g_lo = m.sem("g_ready"), m.sem("g_turned"), m.sem("g_hi"), m.sem("g_lo")
        upped, added, stored = m.sem("upped"), m.sem("added"), m.sem("stored")

        def after(eng, sem, n):
            if not isinstance(n, int) or n > 0:
                eng.wait_ge(sem, n)

        def all_steps(eng, step):
            for b in range(-3, 1):
                step(b, b % 2, b)
            with eng.Fori(0, (B - 4) // 2) as r:
                step(2 * r + 1, 1, None)
                step(2 * r + 2, 0, None)
            for b in range(B - 3, B + 1):
                step(b, b % 2, b)

        def has(at, ahead):
            return at is None or 0 <= at + ahead < B

        with m.block() as block:
            @block.sync
            def _(sp):
                dst = out_dram.rearrange("(t p) d -> p t d", p=P)
                with sp.Fori(0, B) as b:
                    sp.wait_ge(added, b * TPB + TPB)
                    sp.dma_start(dst[:, bass.ds(b * TPB, TPB), :], X[:, bass.ds(b * TPB, TPB), :]).then_inc(stored, DMA)
                sp.wait_ge(stored, B * DMA)

            @block.tensor
            def _(pe):
                def step(b, par, at):
                    if has(at, 1):
                        pe.wait_ge(y_lo, b + 2)
                        after(pe, acted, b)
                        for t in range(TPB):
                            last = products(pe, hidden[1 - par][:, t, 0:GE], [(yT_h[:, t, c, :], yT_l[:, t, c, :], wd_h[:, c, :], wd_l[:, c, :])
                                                                     for c in range(DC)])
                        last.then_inc(hid, 1)
                    if has(at, 2):
                        pe.wait_ge(y_ready, b + 3)
                        for t in range(TPB):
                            for c in range(DC):
                                last = pe.transpose(turn[:, t, c, :], y[:, t, c * P:(c + 1) * P], ident[:, :])
                        last.then_inc(turned, 1)
                    if has(at, -1):
                        pe.wait_ge(g_lo, b)
                        after(pe, added, (b - 1) * TPB)
                        for t in range(TPB):
                            tok = slice(t * P, (t + 1) * P)
                            last = products(pe, up[:, t, :], [(g_h[:, tok], g_l[:, tok], wu_h[:, :], wu_l[:, :])])
                        last.then_inc(upped, 1)
                    if has(at, 0):
                        pe.wait_ge(g_ready, b + 1)
                        after(pe, g_lo, b)
                        for t in range(TPB):
                            last = pe.transpose(turn_g[:, t * P:(t + 1) * P], act_h[:, t, :], ident[:, :])
                        last.then_inc(g_turned, 1)
                all_steps(pe, step)

            @block.scalar
            def _(act):
                def step(b, par, at):
                    if has(at, 2):
                        act.wait_ge(turned, b + 3)
                        act.activation(yT_h[:], turn[:], ACT.Copy).then_inc(y_hi, 1)
                    if has(at, 0):
                        act.wait_ge(g_turned, b + 1)
                        act.activation(g_h[:, :], turn_g[:, 0:TPB * P], ACT.Copy).then_inc(g_hi, 1)
                    if has(at, 1):
                        act.wait_ge(maxed, b + 2)
                        for t in range(TPB):
                            act.activation(weight[:, t, :], hidden[1 - par][:, t, G:GE], ACT.Exp, bias=neg_max[:, t:t + 1],
                                           accum_out=sums[:, t:t + 1])
                        act.drain().then_inc(exped, 1)
                        act.activation(act_h[:], hidden[1 - par][:, :, 0:G], ACT.Silu).then_inc(acted, 1)
                all_steps(act, step)

            @block.vector
            def _(dve):
                def normalise_y(b):
                    after(dve, turned, b)
                    for t in range(TPB):
                        tile = b * TPB + t
                        last = dve.tensor_scalar(y[:, t, :], X[:, bass.ds(tile, 1), :].rearrange("p a d -> p (a d)"),
                                                 mv[:, bass.ds(tile, 1), 0:1].rearrange("p a d -> p (a d)"),
                                                 rstd[:, bass.ds(tile, 1)], ALU.subtract, ALU.mult)
                    last.then_inc(y_ready, 1)

                def gates(b):
                    dve.wait_ge(exped, b + 1)
                    dve.reciprocal(sums[:, :], sums[:, :])
                    dve.drain()
                    for t in range(TPB):
                        dve.tensor_scalar(weight[:, t, :], weight[:, t, :], sums[:, t:t + 1], None, ALU.mult)
                    dve.drain()
                    for t in range(TPB):
                        dve.max(top[:, t, :], weight[:, t, :])
                    dve.drain()
                    for t in range(TPB):
                        dve.max_index(index[:, t, :], top[:, t, :], weight[:, t, :])
                    dve.drain()
                    dve.tensor_copy(index_f[:], index[:])
                    dve.drain()
                    for t in range(TPB):
                        dve.tensor_scalar(mask[:, t, :], iota[:, :], index_f[:, t, 0:1], None, ALU.is_equal)
                    dve.drain()
                    for t in range(TPB):
                        dve.scalar_tensor_tensor(mask[:, t, :], iota[:, :], index_f[:, t, 1:2], mask[:, t, :],
                                                 ALU.is_equal, ALU.add)
                    dve.drain()
                    dve.tensor_tensor(gate[:], mask[:], weight[:], ALU.mult)
                    dve.drain()
                    dve.wait_ge(acted, b + 1)
                    units = act_h[:].rearrange("p t (e i) -> p (t e) i", e=E)
                    dve.tensor_tensor(units, units, gate[:].rearrange("p t e -> p (t e)").unsqueeze(2).broadcast_to([P, TPB * E, EI]),
                                      ALU.mult).then_inc(g_ready, 1)

                def step(b, par, at):
                    if has(at, 1):
                        dve.wait_ge(hid, b + 2)
                        dve.tensor_reduce(neg_max[:, :], hidden[1 - par][:, :, G:GE], AX.X, ALU.max, negate=True).then_inc(maxed, 1)
                    if has(at, 2):
                        dve.wait_ge(y_hi, b + 3)
                        dve.tensor_tensor(yT_l[:], turn[:], f32(yT_h[:]), ALU.subtract).then_inc(y_lo, 1)
                    if has(at, 0):
                        dve.wait_ge(g_hi, b + 1)
                        dve.tensor_tensor(g_l[:, :], turn_g[:, 0:TPB * P], f32(g_h[:, :]), ALU.subtract).then_inc(g_lo, 1)
                    if has(at, 1):
                        gates(b + 1)
                    if has(at, 3):
                        normalise_y(b + 3)
                    if has(at, -1):
                        dve.wait_ge(upped, b)
                        for t in range(TPB):
                            xt = X[:, bass.ds((b - 1) * TPB + t, 1), :].rearrange("p a d -> p (a d)")
                            dve.tensor_tensor(xt, xt, up[:, t, :], ALU.add).then_inc(added, 1)
                all_steps(dve, step)


def program(nc, io, out, until=9):
    with Memory(nc, "g") as g:
        X = g.sb("x", [P, TILES, D])
        mv = g.sb("mean_var", [P, TILES, 2])
        rstd = g.sb("rstd", [P, TILES])
        ident = g.sb("ident", [P, P])
        identb = g.sb("identb", [P, P], BF16)
        store = Store(nc, g, 28)
        w1_raw = store.place("w1_raw", 0, [P, DC, F])
        ahead = (store.place("wq1", 0, [P, H1, D]), store.place("kcq", 8, [P, H1, 3, P]),
                 store.place("wqr", 14, [P, H1, 3, R1]), store.place("kckv", 26, [P, H1, CTX]))
        w1_in, ahead_in = g.sem("w1_in"), g.sem("ahead_in")
        layer0_attention(nc, io, X, mv, rstd, ident, identb, store, w1_raw, w1_in)
        if until >= 2:
            layer0_feed_forward(nc, io, X, mv, rstd, ident, identb, store, w1_raw, w1_in, ahead, ahead_in)
        if until >= 3:
            layer1_attention(nc, io, X, mv, rstd, ident, store, ahead, ahead_in)
        if until >= 4:
            layer1_experts(nc, io, out, X, mv, rstd, ident)
            return
        done = g.sem("done")
        with g.block() as block:
            @block.sync
            def _(sp):
                sp.dma_start(out.rearrange("(t p) d -> p t d", p=P), X[:, :, :]).then_inc(done, DMA)
                sp.wait_ge(done, DMA)
                sp.wait_ge(w1_in if until < 2 else ahead_in, DMA if until < 2 else 4 * DMA)



def arrays(x, ctx_512, L0_xattn_Wq, L0_xattn_Wkv_expand, L0_xattn_Wout, L0_ffn_W1, L0_ffn_W2, L1_xattn_Wq, L1_xattn_w_kc_q,
           L1_xattn_w_kc_kv, L1_xattn_W_qr, L1_xattn_W_kr, L1_xattn_Wo, L1_ffn_router_w, L1_ffn_down_w, L1_ffn_up_w):
    import numpy as np

    c = np.ascontiguousarray
    x, ctx = np.asarray(x), np.asarray(ctx_512)

    def tokens(a):
        return a.reshape(TPB, P, CTX).transpose(1, 0, 2).reshape(P, S)

    wo0 = np.asarray(L0_xattn_Wout).T.reshape(GROUPS, 4, HD0, D).transpose(1, 0, 2, 3).reshape(D, D)
    swapped = np.concatenate([ctx[..., CTX // 2:], ctx[..., :CTX // 2]], -1)
    ctx1 = np.stack([np.stack([tokens(ctx[b]), ctx[b].T, tokens(swapped[b]), swapped[b].T], 1) for b in range(B)])
    inv_freq = np.float32(1.0) / np.float32(10000.0) ** (np.arange(0, CTX, 2, dtype=np.float32) / np.float32(CTX))
    freqs = np.arange(S, dtype=np.float32)[:, None] * inv_freq[None, :]
    sin, cos = np.repeat(np.sin(freqs), 2, axis=-1), np.repeat(np.cos(freqs), 2, axis=-1)
    sin = sin * np.where(np.arange(CTX) < CTX // 2, -1, 1).astype(np.float32)
    table = np.stack([tokens(cos), cos.T, tokens(sin), sin.T], 1).astype(np.float32)
    causal = np.arange(P)[None, :] <= np.arange(P)[:, None]
    return {
        "x": c(x.reshape(B * S, D)),
        "ctxT": c(ctx.reshape(B * S, CTX).T),
        "wq0": c(np.asarray(L0_xattn_Wq).T),
        "wkv0": c(np.asarray(L0_xattn_Wkv_expand).T),
        "wo0": c(wo0),
        "ident": np.eye(P, dtype=np.float32),
        "mask": np.where(causal, 0.0, -2.0 ** 127).astype(np.float32),
        "w1": c(np.asarray(L0_ffn_W1).T),
        "w2": c(np.asarray(L0_ffn_W2).T),
        "kcq": c(np.asarray(L1_xattn_w_kc_q).transpose(0, 2, 1)),
        "wqr": c(L1_xattn_W_qr),
        "wq1": c(L1_xattn_Wq),
        "kckv": c(L1_xattn_w_kc_kv),
        "wo1": c(np.asarray(L1_xattn_Wo).T),
        "kr": c(np.asarray(L1_xattn_W_kr).transpose(1, 0, 2).reshape(CTX, H1 * R1)),
        "table": c(table),
        "ctx1": c(ctx1),
        "wd": c(np.concatenate([np.asarray(L1_ffn_down_w).reshape(E * EI, D).T, np.asarray(L1_ffn_router_w).T], 1)),
        "wu": c(np.asarray(L1_ffn_up_w).transpose(0, 2, 1).reshape(E * EI, D)),
        "iota": np.tile(np.arange(E, dtype=np.float32), (P, 1)),
    }


def kernel(**inputs):
    import concourse.bacc as bacc
    import numpy as np
    from concourse.bass_utils import run_bass_kernel_spmd

    nc = bacc.Bacc("TRN2", target_bir_lowering=False, num_devices=1)
    placed = arrays(**inputs)
    io = {n: nc.dram_tensor(f"in_{n}", a.shape, mybir.dt.from_np(a.dtype), kind="ExternalInput").ap()
          for n, a in placed.items()}
    out = nc.dram_tensor("out", (B * S, D), F32, kind="ExternalOutput").ap()
    program(nc, io, out)
    r = run_bass_kernel_spmd(nc, [{f"in_{n}": a for n, a in placed.items()}], core_ids=[0])
    return np.asarray(r.results[0]["out"]).reshape(B, S, D)
```

```python
from contextlib import ExitStack

import concourse.bass as bass
from concourse import mybir

F32 = mybir.dt.float32
F32R = mybir.dt.float32r
BF16 = mybir.dt.bfloat16
U32 = mybir.dt.uint32
ALU = mybir.AluOpType
ACT = mybir.ActivationFunctionType
AX = mybir.AxisListType

P = 128
B, S, D = 8, 256, 512
TPB = S // P
TILES = B * TPB
DC = D // P
CTX = 128
DMA = 16
EPS = 1e-5

H0, HD0 = 16, 32
GROUPS = H0 // 4
F = 2048
FC = F // P
MAGIC = 1.5 * 2.0 ** 23
H1, R1 = 16, 64
PAIRS = H1 // 2
E, EI = 8, 16
G = E * EI


def products(pe, out, pairs, start=True, stop=True):
    last = None
    for n, (lh, ll, rh, rl) in enumerate(pairs):
        pe.matmul(out, ll, rh, start=start and n == 0, stop=False)
        pe.matmul(out, lh, rl, start=False, stop=False)
        last = pe.matmul(out, lh, rh, start=False, stop=stop and n == len(pairs) - 1)
    return last


def f32(ap):
    return ap.bitcast(F32)


class Memory:

    def __init__(self, nc, phase):
        self.nc, self.phase, self.stack = nc, phase, ExitStack()

    def __enter__(self):
        self.stack.__enter__()
        return self

    def __exit__(self, *a):
        return self.stack.__exit__(*a)

    def sb(self, name, shape, dt=F32):
        return self.stack.enter_context(self.nc.sbuf_tensor(f"{self.phase}_{name}", shape, dt))

    def ps(self, name, shape, dt=F32):
        return self.stack.enter_context(self.nc.psum_tensor(f"{self.phase}_{name}", shape, dt))

    def sem(self, name):
        return self.stack.enter_context(self.nc.semaphore(f"{self.phase}_{name}"))

    def block(self):
        return self.nc.Block()


class Store:
    UNIT = 4 * 1024

    def __init__(self, nc, memory, units):
        self.nc, self.offset = nc, -(-nc.sbuf_base // 32) * 32
        memory.sb("store", [P, units * self.UNIT // 4])

    def place(self, name, start, shape, dt=F32):
        return self.nc.alloc_sbuf_tensor_at(name, shape, dt, offset=self.offset + start * self.UNIT)[:]


def tile_stats(dve, x_tile, stats, mean_var):
    dve.bn_stats(stats, x_tile)
    dve.drain()
    return dve.bn_aggr(mean_var, stats)


def inverse_deviations(nc, phase, mv, rstd, loads=()):
    with Memory(nc, phase) as m:
        var = m.sb("var", [P, TILES])
        dev = m.sb("dev", [P, TILES])
        sq = m.sb("sq", [P, TILES])
        var_ready, dev_ready = m.sem("var_ready"), m.sem("dev_ready")
        with m.block() as block:
            @block.sync
            def _(sp):
                for dst, src, arrived in loads:
                    sp.dma_start(dst, src).then_inc(arrived, DMA)

            @block.vector
            def _(dve):
                dve.tensor_scalar(var[:, :], mv[:, :, 1], EPS, None, ALU.add).then_inc(var_ready, 1)
                dve.wait_ge(dev_ready, 1)
                dve.reciprocal(rstd[:, :], dev[:, :])
                dve.drain()
                dve.tensor_tensor(sq[:, :], rstd[:, :], rstd[:, :], ALU.mult)
                dve.drain()
                dve.tensor_tensor(sq[:, :], sq[:, :], var[:, :], ALU.mult)
                dve.drain()
                dve.tensor_scalar(sq[:, :], sq[:, :], -0.5, 1.5, ALU.mult, ALU.add)
                dve.drain()
                dve.tensor_tensor(rstd[:, :], rstd[:, :], sq[:, :], ALU.mult)

            @block.scalar
            def _(act):
                act.wait_ge(var_ready, 1)
                act.activation(dev[:, :], var[:, :], ACT.Sqrt).then_inc(dev_ready, 1)



SLOTS0 = [["proj0", "T3'", "proj1", "pv3'"],
          ["out0'", "T0", "out1'", "proj2", "pv0"],
          ["proj3", "T1", "v0", "pv1"],
          ["v1", "T2", "lnt0", "lnt1", "pv2"]]
BEGIN0 = ["lnt0", "lnt1", "proj0", "proj1", "proj2", "proj3", "v0", "v1", "lnt0", "lnt1"]
SPLIT0 = ("lnt", "proj", "pv")


def kind_of(step):
    return step.rstrip("'0123")


def slots_of(is_first=False, prepares=True, turns=True):
    left_out = ([x for slot in SLOTS0 for x in slot if "'" in x] if is_first else []) + (
        [] if prepares else ["proj0", "proj1", "proj2", "proj3", "v0", "v1"]) + ([] if turns else ["lnt0", "lnt1"])
    return [[x for x in slot if x not in left_out] for slot in SLOTS0]


class Numbering:

    def __init__(self):
        full = [x for slot in slots_of() for x in slot if x[0] != "T"]
        first = [x for slot in slots_of(is_first=True) for x in slot if x[0] != "T"]
        self.per = len(full)
        self.per_hi = sum(kind_of(x) in SPLIT0 for x in full)
        self.at0 = len(BEGIN0) - (self.per - len(first))
        self.hi0 = sum(kind_of(x) in SPLIT0 for x in BEGIN0) - (
            self.per_hi - sum(kind_of(x) in SPLIT0 for x in first))

    def begin(self, b, slots, skipped=0, skipped_hi=0):
        out = {}
        n, hi = self.at0 - skipped, self.hi0 - skipped_hi
        if isinstance(b, int) and b == 0:
            n, hi = len(BEGIN0), sum(kind_of(x) in SPLIT0 for x in BEGIN0)
        for slot in slots:
            for x in slot:
                if x[0] == "T":
                    continue
                out[x] = (b * self.per + n, b * self.per_hi + hi, n % 2 if self.per % 2 == 0 else None)
                n += 1
                hi += kind_of(x) in SPLIT0
        return out


def layer0_attention(nc, io, X, mv, rstd, ident, identb, store, w1_raw, w1_in):
    with Memory(nc, "a") as m:
        wq_h, wq_l, wo_h, wo_l = (store.place(name, at, [P, DC, D], F32R)
                                  for name, at in (("wq0_h", 8), ("wq0_l", 10), ("wo0_h", 14), ("wo0_l", 16)))
        wkv_h, wkv_l = store.place("wkv0_h", 12, [P, 2 * D], F32R), store.place("wkv0_l", 13, [P, 2 * D], F32R)
        maskb = m.sb("maskb", [P, P], BF16)

        with Memory(nc, "aw") as w:
            raw = w.sb("raw", [P, 5 * 1024])
            identf, maskf = ident, w.sb("maskf", [P, P])
            stats = w.sb("stats", [P, TILES, 6])
            raws = [raw[:, 0:2048].rearrange("p (c n) -> p c n", c=DC), raw[:, 2048:3072],
                    raw[:, 3072:5120].rearrange("p (c n) -> p c n", c=DC)]
            x_in, w_in, c_in = [w.sem(f"x_in{g}") for g in range(TILES // 4)], [w.sem(f"w_in{i}") for i in range(3)], w.sem("c_in")
            split_hi = w.sem("split_hi")
            XG = 4
            with w.block() as block:
                @block.sync
                def _(sp):
                    sp.dma_start(raws[0], io["wq0"].rearrange("(c p) n -> p c n", p=P)).then_inc(w_in[0], DMA)
                    sp.dma_start(raws[1], io["wkv0"]).then_inc(w_in[1], DMA)
                    sp.dma_start(raws[2], io["wo0"].rearrange("(c p) n -> p c n", p=P)).then_inc(w_in[2], DMA)
                    sp.dma_start(identf[:, :], io["ident"]).then_inc(c_in, DMA)
                    sp.dma_start(maskf[:, :], io["mask"]).then_inc(c_in, DMA)

                @block.gpsimd
                def _(pool):
                    pool.wait_ge(c_in, 2 * DMA)
                    pool.tensor_copy(identb[:, :], identf[:, :])
                    pool.tensor_copy(maskb[:, :], maskf[:, :])

                @block.scalar
                def _(act):
                    for g in range(TILES // XG):
                        act.dma_start(X[:, XG * g:XG * g + XG, :],
                                      io["x"].rearrange("(t p) d -> p t d", p=P)[:, XG * g:XG * g + XG, :]
                                      ).then_inc(x_in[g], DMA)
                    for i, hi in enumerate((wq_h, wkv_h, wo_h)):
                        act.wait_ge(w_in[i], DMA)
                        act.activation(hi[:], raws[i], ACT.Copy).then_inc(split_hi, 1)

                @block.vector
                def _(dve):
                    los = ((wq_h, wq_l), (wkv_h, wkv_l), (wo_h, wo_l))
                    for g in range(TILES // XG):
                        dve.wait_ge(x_in[g], DMA)
                        for t in range(XG * g, XG * g + XG):
                            dve.bn_stats(stats[:, t, :], X[:, t, :])
                        if g < len(los):
                            hi, lo = los[g]
                            dve.wait_ge(split_hi, g + 1)
                            dve.tensor_tensor(lo[:], raws[g], f32(hi[:]), ALU.subtract)
                    dve.drain()
                    for t in range(TILES):
                        dve.bn_aggr(mv[:, t, :], stats[:, t, :])

        inverse_deviations(nc, "as", mv, rstd)

        y = store.place("y0", 26, [P, TPB, D])
        yT_h, yT_l = m.sb("yT_h", [P, DC, S], F32R), m.sb("yT_l", [P, DC, S], F32R)
        ctx_raw = m.sb("ctx_raw", [P, S])
        cT_h, cT_l = m.sb("cT_h", [P, S], F32R), m.sb("cT_l", [P, S], F32R)
        qk_h, qk_l = m.sb("qk_h", [P, 2, GROUPS, S], F32R), m.sb("qk_l", [P, 2, GROUPS, S], F32R)
        q_stack, k_stack = (store.place(name, at, [96, 4, GROUPS, S], F32R)
                            for name, at in (("q_stack", 18), ("k_stack", 22)))
        V, next_V = store.place("V0", 27, [P, TPB, D]), m.sb("next_V", [P, TPB, D])
        neg_max = m.sb("neg_max", [P, 8])
        sums, inv0, inv1 = m.sb("sums", [P, 8]), m.sb("inv0", [P, 4]), m.sb("inv1", [P, 4])
        probs = [m.sb(f"probs{i}", [P, 4 * 3 * P]) for i in range(2)]
        pT = m.sb("pT", [P, 4, 3 * P])
        c_h, c_l = m.sb("c_h", [P, 4, S], F32R), m.sb("c_l", [P, 4, S], F32R)
        stats, new_mv = m.sb("stats", [P, TPB, 6]), m.sb("new_mv", [P, TPB, 2])

        s_q0, s_q1 = m.ps("s_q0", [P, 4, P]), m.ps("s_q1", [P, 4, S])
        t_k0, t_k1 = m.ps("t_k0", [P, 4, S]), m.ps("t_k1", [P, 4, P])
        work = [m.ps(f"work{i}", [P, D]) for i in range(2)]

        ctx_in, ctx_hi, ctx_split = m.sem("ctx_in"), m.sem("ctx_hi"), m.sem("ctx_split")
        y_ready, v_ready, v_moved = m.sem("y_ready"), m.sem("v_ready"), m.sem("v_moved")
        worked, work_hi, work_free = m.sem("worked"), m.sem("work_hi"), m.sem("work_free")
        stacked = [m.sem(f"stacked{j}") for j in range(4)]
        scored, maxed, exped, normed = m.sem("scored"), m.sem("maxed"), m.sem("exped"), m.sem("normed")
        inverted, normed_pool = m.sem("inverted"), m.sem("normed_pool")
        turned, evac_act, evac_dve = m.sem("turned"), m.sem("evac_act"), m.sem("evac_dve")

        SCALE = float(HD0) ** -0.5
        numbers = Numbering()
        in_begin = {}
        for n, x in enumerate(BEGIN0):
            in_begin[x, n // 8] = (n, sum(kind_of(z) in SPLIT0 for z in BEGIN0[:n]), n % 2)
        L = B - 1
        count = lambda slots: (sum(x[0] != "T" for s in slots for x in s),
                               sum(kind_of(x) in SPLIT0 for s in slots for x in s))
        short = tuple(a - c for a, c in zip(count(slots_of()), count(slots_of(turns=False))))

        def all_batches(eng, begin, slots, end):
            begin()
            slots(0, slots_of(is_first=True), numbers.begin(0, slots_of(is_first=True)))
            with eng.Fori(1, B - 2) as b:
                slots(b, slots_of(), numbers.begin(b, slots_of()))
            slots(L - 1, slots_of(turns=False), numbers.begin(L - 1, slots_of(turns=False)))
            last = slots_of(prepares=False, turns=False)
            at = numbers.begin(L, last, *short)
            slots(L, last, at)
            n, hi = max(v[0] for v in at.values()) + 1, max(v[1] for v in at.values()) + 1
            end({"pv3'": (n, hi, n % 2), "out0'": (n + 1, None, (n + 1) % 2), "out1'": (n + 2, None, n % 2)})

        with m.block() as block:
            @block.sync
            def _(sp):
                def load_context(nb):
                    if not isinstance(nb, int) or nb > 0:
                        sp.wait_ge(ctx_split, nb)
                    sp.dma_start(ctx_raw[:, :], io["ctxT"][:, bass.ts(nb, S)]).then_inc(ctx_in, DMA)

                def stack(b, n_proj3, is_begin=False):
                    sp.wait_ge(work_free, n_proj3 + 1)
                    for j in range(4):
                        if not is_begin:
                            sp.wait_ge(scored, (b * 4 + j) * 2 + 2)
                        src = slice(32 * j, 32 * j + 32)
                        for r, (q, k) in enumerate(((qk_h, qk_h), (qk_l, qk_h), (qk_h, qk_l))):
                            dst = slice(32 * r, 32 * r + 32)
                            sp.dma_start(f32(q_stack[dst, j, :, :]), f32(q[src, 0, :, :])).then_inc(stacked[j], DMA)
                            sp.dma_start(f32(k_stack[dst, j, :, :]), f32(k[src, 1, :, :])).then_inc(stacked[j], DMA)

                def begin():
                    load_context(0)
                    stack(0, in_begin["proj3", 0][0], True)
                    load_context(1)

                def slots(b, steps, at):
                    if "lnt0" in at:
                        load_context(b + 2)
                    if "proj3" in at:
                        stack(b, at["proj3"][0])
                all_batches(sp, begin, slots, lambda at: None)

            @block.tensor
            def _(pe):
                def scores(b, i):
                    slot = b * 4 + i
                    pe.wait_ge(stacked[i], (b + 1) * 6 * DMA)
                    if not isinstance(slot, int) or slot > 0:
                        pe.wait_ge(exped, 2 * slot - 1)
                    for h in range(4):
                        pe.matmul(s_q0[:, h, :], q_stack[:, i, h, 0:P], k_stack[:, i, h, 0:P], start=True, stop=False)
                        last = pe.matmul(s_q0[:, h, :], identb[:, :], maskb[:, :], start=False, stop=True)
                    last.then_inc(scored, 1)
                    if not isinstance(slot, int) or slot > 0:
                        pe.wait_ge(exped, 2 * slot)
                    for h in range(4):
                        pe.matmul(s_q1[:, h, :], q_stack[:, i, h, P:S], k_stack[:, i, h, :], start=True, stop=False)
                        last = pe.matmul(s_q1[:, h, P:S], identb[:, :], maskb[:, :], start=False, stop=True)
                    last.then_inc(scored, 1)

                def transpose_probs(slot, i):
                    pe.wait_ge(normed, slot + 1)
                    pe.wait_ge(normed_pool, slot + 1)
                    if not isinstance(slot, int) or slot > 0:
                        pe.wait_ge(evac_act, slot)
                        pe.wait_ge(evac_dve, slot)
                    p0 = probs[i % 2][:, 0:4 * P].rearrange("p (h k) -> p h k", h=4)
                    p1 = probs[i % 2][:, 4 * P:12 * P].rearrange("p (h k) -> p h k", h=4)
                    for h in range(4):
                        pe.transpose(t_k0[:, h, 0:P], p0[:, h, :], ident[:, :])
                        last = pe.transpose(t_k0[:, h, P:S], p1[:, h, 0:P], ident[:, :])
                    last.then_inc(turned, 1)
                    for h in range(4):
                        last = pe.transpose(t_k1[:, h, :], p1[:, h, P:S], ident[:, :])
                    last.then_inc(turned, 1)

                def piece(step, n, bank, slot, nb, ready):
                    kind, i = kind_of(step), int(step.strip("'")[-1])
                    out = work[bank]
                    if not isinstance(n, int) or n >= 2:
                        pe.wait_ge(work_free, n - 1)
                    if kind == "lnt":
                        pe.wait_ge(y_ready, nb * TPB + i + 1)
                        for c in range(DC):
                            last = pe.transpose(out[:, c * P:(c + 1) * P], y[:, i, c * P:(c + 1) * P], ident[:, :])
                    elif kind == "proj":
                        if i == 0:
                            pe.wait_ge(work_free, ready)
                            pe.wait_ge(ctx_split, nb + 1)
                        cols = slice(i * P, (i + 1) * P)
                        products(pe, out[:, 0:S], [(wq_h[:, c, cols], wq_l[:, c, cols], yT_h[:, c, :], yT_l[:, c, :])
                                                   for c in range(DC)])
                        last = products(pe, out[:, S:2 * S], [(wkv_h[:, cols], wkv_l[:, cols], cT_h[:, :], cT_l[:, :])])
                    elif kind == "v":
                        tok = slice(i * P, (i + 1) * P)
                        last = products(pe, out[:, :], [(cT_h[:, tok], cT_l[:, tok], wkv_h[:, D:2 * D], wkv_l[:, D:2 * D])])
                    elif kind == "pv":
                        pe.wait_ge(evac_act, slot + 1)
                        if i == 0:
                            pe.wait_ge(v_moved, nb)
                        for h in range(4):
                            head = slice((4 * h + i) * HD0, (4 * h + i + 1) * HD0)
                            rows = slice(32 * h, 32 * h + 32)
                            pe.matmul(out[rows, 0:S], V[:, 0, head], pT[:, h, 0:S], start=True, stop=False,
                                      tile_position=(0, 32 * h))
                        pe.wait_ge(evac_dve, slot + 1)
                        for h in range(4):
                            head = slice((4 * h + i) * HD0, (4 * h + i + 1) * HD0)
                            rows = slice(32 * h, 32 * h + 32)
                            last = pe.matmul(out[rows, P:S], V[:, 1, head], pT[:, h, S:S + P], start=False, stop=True,
                                             tile_position=(0, 32 * h))
                    elif kind == "out":
                        if i == 0:
                            pe.wait_ge(work_free, ready)
                        tok = slice(i * P, (i + 1) * P)
                        last = products(pe, out[:, :], [(c_h[:, j, tok], c_l[:, j, tok], wo_h[:, j, :], wo_l[:, j, :])
                                                        for j in range(4)])
                    last.then_inc(worked, 1)

                def begin():
                    for n, x in enumerate(BEGIN0):
                        piece(x, n, n % 2, None, n // 8, in_begin["lnt1", 0][0] + 1)

                def slots(b, steps, at):
                    for i, slot_steps in enumerate(steps):
                        scores(b, i)
                        for x in slot_steps:
                            slot = b * 4 + i - 1
                            if x[0] == "T":
                                transpose_probs(slot, (i - 1) % 4)
                                continue
                            if kind_of(x) == "proj":
                                nb = b + 1
                                ready = in_begin["lnt1", 1][0] + 1 if isinstance(b, int) and b == 0 else (
                                    next(iter(at.values()))[0] - 1)
                            elif kind_of(x) == "lnt":
                                nb, ready = b + 2, None
                            elif kind_of(x) == "out":
                                nb, ready = b - 1, at["pv3'"][0] + 1
                            else:
                                nb, ready = b + 1, None
                            piece(x, at[x][0], at[x][2], slot, nb, ready)

                def end(at):
                    transpose_probs(B * 4 - 1, 3)
                    for x in at:
                        piece(x, at[x][0], at[x][2], B * 4 - 1, B, at["pv3'"][0] + 1)
                all_batches(pe, begin, slots, end)

            @block.scalar
            def _(act):
                act.dma_start(w1_raw, io["w1"].rearrange("(c p) n -> p c n", p=P)).then_inc(w1_in, DMA)

                def split_context(nb, n_v1):
                    act.wait_ge(ctx_in, (nb + 1) * DMA)
                    if n_v1 is not None:
                        act.wait_ge(worked, n_v1 + 1)
                    act.activation(cT_h[:, :], ctx_raw[:, :], ACT.Copy).then_inc(ctx_hi, 1)

                def exponentials(slot, i, part):
                    act.wait_ge(maxed, 2 * slot + part + 1)
                    if part == 0 and (not isinstance(slot, int) or slot >= 2):
                        act.wait_ge(turned, 2 * slot - 2)
                    src, width = ((s_q0, P), (s_q1, S))[part]
                    for h in range(4):
                        at = part * 4 * P + h * width
                        m_at = part * 4 + h
                        last = act.activation(probs[i % 2][:, at:at + width], src[:, h, :], ACT.Exp,
                                              bias=neg_max[:, m_at:m_at + 1], scale=SCALE,
                                              accum_out=sums[:, m_at:m_at + 1])
                    last.then_inc(exped, 1)

                def copy_probs(slot):
                    act.wait_ge(turned, 2 * slot + 1)
                    act.activation(pT[:, :, 0:S], t_k0[:, :, :], ACT.Copy).then_inc(evac_act, 1)

                def split(step, n, bank, nb):
                    kind, i, out = kind_of(step), int(step.strip("'")[-1]), work[bank]
                    act.wait_ge(worked, n + 1)
                    if kind == "lnt":
                        hi = act.activation(yT_h[:, :, i * P:(i + 1) * P], out[:, :].rearrange("p (c t) -> p c t", c=DC),
                                            ACT.Copy)
                    elif kind == "proj":
                        if i == 0 and nb is not None:
                            for s in stacked:
                                act.wait_ge(s, nb * 6 * DMA)
                        hi = act.activation(qk_h[:, :, i, :], out[:, :].rearrange("p (a t) -> p a t", a=2), ACT.Copy)
                    else:
                        hi = act.activation(c_h[:, i, :], out[:, 0:S], ACT.Copy)
                    hi.then_inc(work_hi, 1)

                def move_values(nb):
                    act.wait_ge(v_ready, 2 * (nb + 1))
                    act.activation(V[:], next_V[:], ACT.Copy).then_inc(v_moved, 1)

                def begin():
                    split_context(0, None)
                    for n, x in enumerate(BEGIN0):
                        if n == 8:
                            split_context(1, in_begin["v1", 0][0])
                        if kind_of(x) in SPLIT0:
                            split(x, n, n % 2, None)

                def slots(b, steps, at):
                    for i, slot_steps in enumerate(steps):
                        slot = b * 4 + i
                        todo = [x for x in slot_steps if kind_of(x) in SPLIT0]
                        turned = any(x[0] == "T" for x in slot_steps)
                        early = [x for x in todo if not turned or slot_steps.index(x) == 0]
                        exponentials(slot, i, 0)
                        for x in early:
                            split(x, at[x][0], at[x][2], b + 1)
                        exponentials(slot, i, 1)
                        if turned:
                            copy_probs(slot - 1)
                        for x in todo[len(early):]:
                            split(x, at[x][0], at[x][2], b + 1)
                        if i == 0:
                            move_values(b)
                        if i == 3 and "lnt0" in at:
                            split_context(b + 2, at["v1"][0])

                def end(at):
                    copy_probs(B * 4 - 1)
                    split("pv3'", at["pv3'"][0], at["pv3'"][2], None)
                all_batches(act, begin, slots, end)

            @block.gpsimd
            def _(pool):
                def normalise(slot, i):
                    pool.wait_ge(inverted, slot + 1)
                    p0 = probs[i % 2][:, 0:4 * P].rearrange("p (h k) -> p h k", h=4)
                    pool.tensor_tensor(p0, p0, inv0[:, :].unsqueeze(2).broadcast_to([P, 4, P]), ALU.mult
                                       ).then_inc(normed_pool, 1)

                with pool.Fori(0, B) as b:
                    for i in range(4):
                        normalise(b * 4 + i, i)

            @block.vector
            def _(dve):
                def normalise_y(nb):
                    for t in range(TPB):
                        tile = nb * TPB + t
                        dve.tensor_scalar(y[:, t, :], X[:, bass.ds(tile, 1), :].rearrange("p a d -> p (a d)"),
                                          mv[:, bass.ds(tile, 1), 0:1].rearrange("p a d -> p (a d)"),
                                          rstd[:, bass.ds(tile, 1)], ALU.subtract, ALU.mult).then_inc(y_ready, 1)

                def split_context(nb):
                    dve.wait_ge(ctx_hi, nb + 1)
                    dve.tensor_tensor(cT_l[:, :], ctx_raw[:, :], f32(cT_h[:, :]), ALU.subtract).then_inc(ctx_split, 1)

                def maxima(slot):
                    for part, src in enumerate((s_q0, s_q1)):
                        cols = neg_max[:, 4 * part:4 * part + 4]
                        dve.wait_ge(scored, 2 * slot + part + 1)
                        dve.tensor_reduce(cols, src[:, :, :], AX.X, ALU.max, negate=True)
                        dve.drain()
                        dve.tensor_scalar(cols, cols, SCALE, None, ALU.mult).then_inc(maxed, 1)

                def invert(slot):
                    dve.wait_ge(exped, 2 * slot + 1)
                    if not isinstance(slot, int) or slot > 0:
                        dve.wait_ge(normed_pool, slot)
                    dve.reciprocal(inv0[:, :], sums[:, 0:4]).then_inc(inverted, 1)

                def normalise(slot, i):
                    dve.wait_ge(exped, 2 * slot + 2)
                    dve.reciprocal(inv1[:, :], sums[:, 4:8])
                    dve.drain()
                    p1 = probs[i % 2][:, 4 * P:12 * P].rearrange("p (h k) -> p h k", h=4)
                    for h in range(4):
                        last = dve.tensor_scalar(p1[:, h, :], p1[:, h, :], inv1[:, h:h + 1], None, ALU.mult)
                    last.then_inc(normed, 1)

                def copy_probs(slot):
                    dve.wait_ge(turned, 2 * slot + 2)
                    dve.tensor_copy(pT[:, :, S:S + P], t_k1[:, :, :]).then_inc(evac_dve, 1)

                def piece(step, n, n_hi, bank, nb):
                    kind, i, out = kind_of(step), int(step.strip("'")[-1]), work[bank]
                    if kind in SPLIT0:
                        dve.wait_ge(work_hi, n_hi + 1)
                        if kind == "lnt":
                            hi = yT_h[:, :, i * P:(i + 1) * P]
                            lo, src = yT_l[:, :, i * P:(i + 1) * P], out[:, :].rearrange("p (c t) -> p c t", c=DC)
                        elif kind == "proj":
                            hi, lo = qk_h[:, :, i, :], qk_l[:, :, i, :]
                            src = out[:, :].rearrange("p (a t) -> p a t", a=2)
                        else:
                            hi, lo, src = c_h[:, i, :], c_l[:, i, :], out[:, 0:S]
                        dve.tensor_tensor(lo, src, f32(hi), ALU.subtract).then_inc(work_free, 1)
                        return
                    dve.wait_ge(worked, n + 1)
                    if kind == "v":
                        if i == 0 and nb is not None:
                            dve.wait_ge(v_moved, nb)
                        dve.tensor_copy(next_V[:, i, :], out[:, :]).then_inc(work_free, 1)
                        dve.drain().then_inc(v_ready, 1)
                    else:
                        tile = nb * TPB + i
                        xt = X[:, bass.ds(tile, 1), :].rearrange("p a d -> p (a d)")
                        dve.tensor_tensor(xt, xt, out[:, :], ALU.add).then_inc(work_free, 1)

                def new_stats(nb):
                    for i in range(TPB):
                        xt = X[:, bass.ds(nb * TPB + i, 1), :].rearrange("p a d -> p (a d)")
                        dve.bn_stats(stats[:, i, :], xt)
                    dve.drain()
                    for i in range(TPB):
                        dve.bn_aggr(new_mv[:, i, :], stats[:, i, :])
                    dve.drain()
                    dve.tensor_copy(mv[:, bass.ds(nb * TPB, TPB), :], new_mv[:, :, :])

                def begin():
                    normalise_y(0)
                    split_context(0)
                    for n, x in enumerate(BEGIN0):
                        if n == 2:
                            normalise_y(1)
                        if n == 8:
                            split_context(1)
                        piece(x, n, in_begin[x, n // 8][1], n % 2, None)

                def slots(b, steps, at):
                    for i, slot_steps in enumerate(steps):
                        slot = b * 4 + i
                        maxima(slot)
                        invert(slot)
                        for n_step, x in enumerate(slot_steps):
                            if n_step == 2:
                                normalise(slot, i)
                            if i == 3 and n_step == len(slot_steps) - 1 and any("'" in x for x in at):
                                new_stats(b - 1)
                            if i == 1 and n_step == len(slot_steps) - 1 and "lnt0" in at:
                                normalise_y(b + 2)
                            if x[0] == "T":
                                copy_probs(slot - 1)
                            else:
                                piece(x, *at[x], b - 1 if "'" in x else b + 1)
                        if len(slot_steps) <= 2:
                            normalise(slot, i)
                        if i == 3 and "lnt0" in at:
                            split_context(b + 2)

                def end(at):
                    copy_probs(B * 4 - 1)
                    for x in at:
                        piece(x, *at[x], B - 1)
                    dve.drain()
                    new_stats(B - 1)
                all_batches(dve, begin, slots, end)



CH = 4


def quantise_weights(nc, w1_raw, w2_raw, w1, w2, mean, w1_in, w2_in):
    with Memory(nc, "bw") as w:
        raw, dst = ([a.rearrange("p c n -> p (c n)").rearrange("p (c n) -> p c n", c=CH) for a in pair]
                    for pair in ((w1_raw, w2_raw), (w1, w2)))
        part, total = w.sb("part", [P, 2, CH]), w.sb("total", [P, 2])
        ones, scale = w.sb("ones", [P, P]), w.sb("scale", [P, 2])
        all_sums = w.ps("all_sums", [P, 2])
        ones_ready = w.sem("ones_ready")
        act_summed, summed, crossed, rounded = w.sem("act_summed"), w.sem("summed"), w.sem("crossed"), w.sem("rounded")
        with w.block() as block:
            @block.gpsimd
            def _(pool):
                pool.memset(ones[:, :], 1.0).then_inc(ones_ready, 1)

            def arrived(eng, i):
                if i == 0:
                    eng.wait_ge(w1_in, DMA)
                else:
                    eng.wait_ge(w2_in, CH * DMA)

            @block.tensor
            def _(pe):
                pe.wait_ge(ones_ready, 1)
                for i in range(2):
                    pe.wait_ge(summed, i + 1)
                    pe.matmul(all_sums[:, i:i + 1], ones[:, :], total[:, i:i + 1], start=True, stop=True).then_inc(crossed, 1)

            @block.vector
            def _(dve):
                def sums(i):
                    arrived(dve, i)
                    for c in range(CH // 2):
                        dve.tensor_reduce(part[:, i, c:c + 1], raw[i][:, c, :], AX.X, ALU.add, apply_absolute_value=True)
                    dve.drain()
                    dve.wait_ge(act_summed, i + 1)
                    dve.tensor_reduce(total[:, i:i + 1], part[:, i, :], AX.X, ALU.add).then_inc(summed, 1)
                    dve.wait_ge(crossed, i + 1)
                    dve.tensor_scalar(mean[:, i:i + 1], all_sums[:, i:i + 1], 1.0 / (F * D), 1e-5, ALU.mult, ALU.max)
                    dve.drain()
                    dve.reciprocal(scale[:, i:i + 1], mean[:, i:i + 1])
                    dve.drain()

                for i in range(2):
                    sums(i)
                    for c in range(CH):
                        dve.tensor_scalar(raw[i][:, c, :], raw[i][:, c, :], scale[:, i:i + 1], 1.0, ALU.mult, ALU.min)
                        dve.drain()
                        dve.tensor_scalar(raw[i][:, c, :], raw[i][:, c, :], -1.0, MAGIC, ALU.max, ALU.add).then_inc(rounded, 1)

            @block.scalar
            def _(act):
                for i in range(2):
                    arrived(act, i)
                    for c in range(CH // 2, CH):
                        last = act.activation(dst[i][:, c, :], raw[i][:, c, :], ACT.Abs, accum_out=part[:, i, c:c + 1])
                    last.then_inc(act_summed, 1)
                    for c in range(CH):
                        act.wait_ge(rounded, i * CH + c + 1)
                        act.activation(dst[i][:, c, :], raw[i][:, c, :], ACT.Copy, bias=-MAGIC)


def layer0_feed_forward(nc, io, X, mv, rstd, identb, store, w1_raw, w1_in, ahead, ahead_in):
    with Memory(nc, "b") as m:
        w2_raw = store.place("w2_raw", 8, [P, FC, D])
        w1, w2 = store.place("w1", 18, [P, DC, F], BF16), store.place("w2", 22, [P, FC, D], BF16)
        mean = m.sb("mean", [P, 2])
        w2_in = m.sem("w2_in")
        w2_chunks = io["w2"].rearrange("(k c p) n -> k p c n", p=P, k=CH)
        inverse_deviations(nc, "bs", mv, rstd, [(w2_raw[:, c * FC // CH:(c + 1) * FC // CH, :], w2_chunks[c], w2_in)
                                                for c in range(CH)])
        quantise_weights(nc, w1_raw, w2_raw, w1, w2, mean, w1_in, w2_in)

        y, yr = m.sb("y", [P, D]), m.sb("yr", [P, D])
        xq = [m.sb(f"xq{i}", [P, D], BF16) for i in range(2)]
        xqT = m.sb("xqT", [P, DC, P], BF16)
        s1, s2 = m.sb("s1", [P, 2]), m.sb("s2", [P, 2])
        h = [m.sb(f"h{i}", [P, F]) for i in range(2)]
        hr, hq = m.sb("hr", [P, F]), m.sb("hq", [P, F], BF16)
        hqT = m.sb("hqT", [P, FC, P], BF16)
        amax, unit, q_scale = m.sb("amax", [P, 2]), m.sb("unit", [P, 2]), m.sb("q_scale", [P, 2])
        stats, new_mv = m.sb("stats", [P, 6]), m.sb("new_mv", [P, 2])
        up = m.ps("up", [P, F])
        xT = m.ps("xT", [P, DC, P], BF16)
        hT = m.ps("hT", [P, FC, P], BF16)
        down = m.ps("down", [P, D])
        x_quant, x_turned, x_copied = m.sem("x_quant"), m.sem("x_turned"), m.sem("x_copied")
        upped, silued = m.sem("upped"), m.sem("silued")
        h_scaled, h_rounded, h_quant = m.sem("h_scaled"), m.sem("h_rounded"), m.sem("h_quant")
        h_turned, h_copied, downed, added = m.sem("h_turned"), m.sem("h_copied"), m.sem("downed"), m.sem("added")
        HALF = FC // 2

        def all_steps(eng, step):
            for t in range(-3, 1):
                step(t, t % 2, t)
            with eng.Fori(0, (TILES - 4) // 2) as r:
                step(2 * r + 1, 1, None)
                step(2 * r + 2, 0, None)
            for t in range(TILES - 3, TILES):
                step(t, t % 2, t)

        def has(t, ahead):
            return t is None or 0 <= t + ahead < TILES

        def after(eng, sem, n):
            if not isinstance(n, int) or n > 0:
                eng.wait_ge(sem, n)

        with m.block() as block:
            @block.sync
            def _(sp):
                wq, kcq, wqr, kckv = ahead
                sp.dma_start(kcq, io["kcq"].rearrange("h (c p) k -> p h c k", p=P)).then_inc(ahead_in, DMA)
                sp.dma_start(wqr, io["wqr"].rearrange("h (c p) r -> p h c r", p=P)).then_inc(ahead_in, DMA)
                sp.dma_start(wq, io["wq1"].rearrange("(h k) d -> k h d", k=P)).then_inc(ahead_in, DMA)
                sp.dma_start(kckv, io["kckv"].rearrange("h k d -> k h d")).then_inc(ahead_in, DMA)

            @block.tensor
            def _(pe):
                def step(t, par, at):
                    if has(at, 0):
                        pe.wait_ge(h_quant, t + 1)
                        after(pe, h_copied, 2 * t)
                        for c in range(FC):
                            last = pe.transpose(hT[:, c, :], hq[:, c * P:(c + 1) * P], identb[:, :])
                            if c == HALF - 1:
                                last.then_inc(h_turned, 1)
                        last.then_inc(h_turned, 1)
                    if has(at, 2):
                        pe.wait_ge(x_copied, t + 3)
                        for n in range(4):
                            if n % 2 == 0:
                                after(pe, silued, 2 * t + 3 + n // 2)
                            for c in range(DC):
                                last = pe.matmul(up[:, n * D:(n + 1) * D], xqT[:, c, :], w1[:, c, n * D:(n + 1) * D],
                                                 start=c == 0, stop=c == DC - 1)
                            if n % 2:
                                last.then_inc(upped, 1)
                    if has(at, 0):
                        after(pe, added, t)
                        for c in range(FC):
                            if c % HALF == 0:
                                pe.wait_ge(h_copied, 2 * t + 1 + c // HALF)
                            last = pe.matmul(down[:, :], hqT[:, c, :], w2[:, c, :], start=c == 0, stop=c == FC - 1)
                        last.then_inc(downed, 1)
                    if has(at, 3):
                        pe.wait_ge(x_quant, t + 4)
                        after(pe, x_copied, t + 3)
                        for c in range(DC):
                            last = pe.transpose(xT[:, c, :], xq[1 - par][:, c * P:(c + 1) * P], identb[:, :])
                        last.then_inc(x_turned, 1)
                all_steps(pe, step)

            @block.scalar
            def _(act):
                def step(t, par, at):
                    if has(at, 0):
                        for i in range(2):
                            act.wait_ge(h_turned, 2 * t + i + 1)
                            act.activation(hqT[:, i * HALF:(i + 1) * HALF, :], hT[:, i * HALF:(i + 1) * HALF, :], ACT.Copy
                                           ).then_inc(h_copied, 1)
                    if has(at, 1):
                        act.wait_ge(h_scaled, t + 2)
                        after(act, h_quant, t + 1)
                        act.activation(hr[:, :], h[1 - par][:, :], ACT.Copy, scale=q_scale[:, 1:2], bias=MAGIC
                                       ).then_inc(h_rounded, 1)
                    if has(at, 2):
                        for n in range(2):
                            act.wait_ge(upped, 2 * t + n + 5)
                            cols = slice(n * F // 2, (n + 1) * F // 2)
                            act.activation(h[par][:, cols], up[:, cols], ACT.Silu, scale=s1[:, par:par + 1]
                                           ).then_inc(silued, 1)
                    if has(at, 3):
                        act.wait_ge(x_turned, t + 4)
                        act.activation(xqT[:], xT[:], ACT.Copy).then_inc(x_copied, 1)
                all_steps(act, step)

            @block.vector
            def _(dve):
                def scales(i):
                    dve.drain()
                    dve.tensor_scalar(unit[:, i:i + 1], amax[:, i:i + 1], 1e-5, 1.0 / 127.0, ALU.max, ALU.mult)
                    dve.drain()
                    return dve.reciprocal(q_scale[:, i:i + 1], unit[:, i:i + 1])

                def add_output(t, par):
                    dve.wait_ge(downed, t + 1)
                    xt = X[:, bass.ds(t, 1), :].rearrange("p a d -> p (a d)")
                    dve.scalar_tensor_tensor(xt, down[:, :], s2[:, par:par + 1], xt, ALU.mult, ALU.add
                                             ).then_inc(added, 1)

                def scale_hidden(t, par):
                    dve.wait_ge(silued, 2 * t + 2)
                    dve.tensor_reduce(amax[:, 1:2], h[par][:, :], AX.X, ALU.max, apply_absolute_value=True)
                    scales(1).then_inc(h_scaled, 1)
                    dve.tensor_scalar(s2[:, par:par + 1], unit[:, 1:2], mean[:, 1:2], None, ALU.mult)

                def quantise_tokens(t, par):
                    after(dve, x_turned, t - 1)
                    dve.tensor_scalar(y[:, :], X[:, bass.ds(t, 1), :].rearrange("p a d -> p (a d)"),
                                      mv[:, bass.ds(t, 1), 0:1].rearrange("p a d -> p (a d)"),
                                      rstd[:, bass.ds(t, 1)], ALU.subtract, ALU.mult)
                    dve.drain()
                    dve.tensor_reduce(amax[:, 0:1], y[:, :], AX.X, ALU.max, apply_absolute_value=True)
                    scales(0)
                    dve.tensor_scalar(s1[:, par:par + 1], unit[:, 0:1], mean[:, 0:1], None, ALU.mult)
                    dve.drain()
                    dve.tensor_scalar(yr[:, :], y[:, :], q_scale[:, 0:1], MAGIC, ALU.mult, ALU.add)
                    dve.drain()
                    dve.tensor_scalar(xq[par][:, :], yr[:, :], -MAGIC, 127.0, ALU.add, ALU.min).then_inc(x_quant, 1)

                def quantise_hidden(t):
                    dve.wait_ge(h_rounded, t + 1)
                    after(dve, h_turned, 2 * t)
                    dve.tensor_scalar(hq[:, :], hr[:, :], -MAGIC, 127.0, ALU.add, ALU.min).then_inc(h_quant, 1)

                def new_stats(t):
                    xt = X[:, bass.ds(t, 1), :].rearrange("p a d -> p (a d)")
                    tile_stats(dve, xt, stats[:, :], new_mv[:, :])
                    dve.drain()
                    dve.tensor_copy(mv[:, bass.ds(t, 1), :].rearrange("p a d -> p (a d)"), new_mv[:, :])

                def step(t, par, at):
                    if has(at, -1):
                        add_output(t - 1, 1 - par)
                    if has(at, 1):
                        scale_hidden(t + 1, 1 - par)
                    if has(at, 3):
                        quantise_tokens(t + 3, 1 - par)
                    if has(at, 1):
                        quantise_hidden(t + 1)
                    else:
                        dve.drain()
                    if has(at, -1):
                        new_stats(t - 1)
                all_steps(dve, step)
                add_output(TILES - 1, (TILES - 1) % 2)
                dve.drain()
                new_stats(TILES - 1)



def score_weights(nc, A_h, A_l, ahead, ahead_in, ident, loads):
    with Memory(nc, "cw") as w:
        wq, kcq, wqr, _ = ahead
        midT = w.sb("midT", [P, PAIRS, P])
        mid = w.sb("mid", [P, H1, R1])
        AT = w.sb("AT", [P, PAIRS, D])
        banks = [w.ps(f"bank{i}", [P, D]) for i in range(4)]
        turned = [w.ps(f"turned{i}", [P, D]) for i in range(4)]
        midT_made, midT_moved, mid_made, mid_moved = w.sem("midT_made"), w.sem("midT_moved"), w.sem("mid_made"), w.sem("mid_moved")
        AT_made, AT_moved, A_made, A_hi, A_lo = (
            w.sem("AT_made"), w.sem("AT_moved"), w.sem("A_made"), w.sem("A_hi"), w.sem("A_lo"))
        PB = D // P
        with w.block() as block:
            @block.sync
            def _(sp):
                for dst, src, arrived in loads[0]:
                    sp.dma_start(dst, src).then_inc(arrived, DMA)
                sp.wait_ge(midT_made, 2)
                for dst, src, arrived in loads[1]:
                    sp.dma_start(dst, src).then_inc(arrived, DMA)

            @block.tensor
            def _(pe):
                pe.wait_ge(ahead_in, 4 * DMA)
                for p in range(PAIRS):
                    out = banks[p // PB][:, p % PB * P:(p % PB + 1) * P]
                    for c in range(3):
                        for i in range(2):
                            last = pe.matmul(out[i * R1:(i + 1) * R1, :], wqr[:, 2 * p + i, c, :], kcq[:, 2 * p + i, c, :],
                                             start=c == 0, stop=c == 2, tile_position=(0, i * R1))
                    if p % PB == PB - 1:
                        last.then_inc(midT_made, 1)
                for g in range(2):
                    pe.wait_ge(midT_moved, g + 1)
                    for p in range(g * PB, (g + 1) * PB):
                        last = pe.transpose(turned[g][:, p % PB * P:(p % PB + 1) * P], midT[:, p, :], ident[:, :])
                    last.then_inc(mid_made, 1)
                for p in range(PAIRS):
                    pe.wait_ge(mid_moved, p // PB + 1)
                    if p >= 2:
                        pe.wait_ge(AT_moved, p - 1)
                    for i in range(2):
                        last = pe.matmul(banks[2 + p % 2][i * R1:(i + 1) * R1, :], mid[:, 2 * p + i, :], wq[:, 2 * p + i, :],
                                         start=True, stop=True, tile_position=(0, i * R1))
                    last.then_inc(AT_made, 1)
                for n in range(2 * DC):
                    g, c = n // DC, n % DC
                    pe.wait_ge(AT_moved, (g + 1) * PB)
                    if n >= 2:
                        pe.wait_ge(A_lo, n - 1)
                    for p in range(g * PB, (g + 1) * PB):
                        last = pe.transpose(turned[2 + n % 2][:, p % PB * P:(p % PB + 1) * P], AT[:, p, c * P:(c + 1) * P],
                                            ident[:, :])
                    last.then_inc(A_made, 1)

            @block.scalar
            def _(act):
                for g in range(2):
                    act.wait_ge(midT_made, g + 1)
                    act.activation(midT[:, g * PB:(g + 1) * PB, :], banks[g][:, :].rearrange("p (h r) -> p h r", h=PB),
                                   ACT.Copy).then_inc(midT_moved, 1)
                for g in range(2):
                    act.wait_ge(mid_made, g + 1)
                    act.activation(mid[:, 2 * g * PB:2 * (g + 1) * PB, :], turned[g][:, :].rearrange("p (h r) -> p h r", r=R1),
                                   ACT.Copy).then_inc(mid_moved, 1)
                for p in range(PAIRS):
                    act.wait_ge(AT_made, p + 1)
                    act.activation(AT[:, p, :], banks[2 + p % 2][:, :], ACT.Copy).then_inc(AT_moved, 1)
                for n in range(2 * DC):
                    act.wait_ge(A_made, n + 1)
                    act.activation(A_h[:, n % DC, n // DC * D:(n // DC + 1) * D], turned[2 + n % 2][:, :], ACT.Copy
                                   ).then_inc(A_hi, 1)

            @block.vector
            def _(dve):
                for n in range(2 * DC):
                    cols = slice(n // DC * D, (n // DC + 1) * D)
                    dve.wait_ge(A_hi, n + 1)
                    dve.tensor_tensor(A_l[:, n % DC, cols], turned[2 + n % 2][:, :], f32(A_h[:, n % DC, cols]),
                                      ALU.subtract).then_inc(A_lo, 1)


def value_weights(nc, io, kr_h, kr_l, VO_h, VO_l, kckv, wo, wo_in, rope_first):
    with Memory(nc, "cv") as w:
        kr = w.sb("kr", [P, H1 * R1])
        banks = [w.ps(f"bank{i}", [P, D]) for i in range(4)]
        kr_in, made, split_hi, split_lo, kr_hi = (
            w.sem("kr_in"), w.sem("made"), w.sem("split_hi"), w.sem("split_lo"), w.sem("kr_hi"))
        with w.block() as block:
            @block.sync
            def _(sp):
                sp.dma_start(kr[:], io["kr"]).then_inc(kr_in, DMA)

            @block.gpsimd
            def _(pool):
                rope_first(pool)

            @block.tensor
            def _(pe):
                pe.wait_ge(wo_in, DMA)
                for h in range(H1):
                    if h >= 4:
                        pe.wait_ge(split_lo, h - 3)
                    pe.matmul(banks[h % 4][:, :], kckv[:, h, :], wo[:, h, :], start=True, stop=True).then_inc(made, 1)

            @block.scalar
            def _(act):
                act.wait_ge(kr_in, DMA)
                act.activation(kr_h[:, :], kr[:, :], ACT.Copy).then_inc(kr_hi, 1)
                for h in range(H1):
                    act.wait_ge(made, h + 1)
                    act.activation(VO_h[:, h, :], banks[h % 4][:, :], ACT.Copy).then_inc(split_hi, 1)

            @block.vector
            def _(dve):
                dve.wait_ge(kr_hi, 1)
                dve.tensor_tensor(kr_l[:, :], kr[:, :], f32(kr_h[:, :]), ALU.subtract)
                for h in range(H1):
                    dve.wait_ge(split_hi, h + 1)
                    dve.tensor_tensor(VO_l[:, h, :], banks[h % 4][:, :], f32(VO_h[:, h, :]), ALU.subtract
                                      ).then_inc(split_lo, 1)


def layer1_attention(nc, io, X, mv, rstd, ident, store, ahead, ahead_in, expert_raw, expert_in):
    with Memory(nc, "c") as m:
        A_h, A_l = (store.place(name, at, [P, DC, H1 * R1], F32R) for name, at in (("A_h", 18), ("A_l", 22)))
        VO_h, VO_l = (store.place(name, at, [P, H1, D], F32R) for name, at in (("VO_h", 0), ("VO_l", 8)))
        wo, wo_in = store.place("wo1", 8, [P, H1, D]), m.sem("wo_in")
        kr_h, kr_l = m.sb("kr_h", [P, H1 * R1], F32R), m.sb("kr_l", [P, H1 * R1], F32R)

        table = m.sb("table", [P, 4, S])
        ctx_raw = m.sb("ctx_raw", [P, 4, S])
        ctx_sum = m.sb("ctx_sum", [P, 2, S])
        kv_h = [m.sb(f"kv_h{i}", [P, 2, S], F32R) for i in range(2)]
        kv_l = [m.sb(f"kv_l{i}", [P, 2, S], F32R) for i in range(2)]
        table_in, ctx_in, kv_ready = m.sem("table_in"), m.sem("ctx_in"), m.sem("kv_ready")

        def make_rope(pool, b, par):
            pool.wait_ge(ctx_in, (b + 1) * DMA)
            pool.tensor_tensor(ctx_raw[:], ctx_raw[:], table[:], ALU.mult)
            pool.drain()
            pool.tensor_tensor(ctx_sum[:], ctx_raw[:, 0:2, :], ctx_raw[:, 2:4, :], ALU.add)
            pool.drain()
            pool.tensor_copy(kv_h[par][:], ctx_sum[:])
            pool.drain()
            pool.tensor_tensor(kv_l[par][:], ctx_sum[:], f32(kv_h[par][:]), ALU.subtract).then_inc(kv_ready, 1)

        def rope_first(pool):
            pool.wait_ge(table_in, DMA)
            make_rope(pool, 0, 0)

        first_context = io["ctx1"][0:1, :, :, :].rearrange("b p a s -> p (b a) s")
        score_weights(nc, A_h, A_l, ahead, ahead_in, ident,
                      (((table[:], io["table"], table_in), (ctx_raw[:], first_context, ctx_in)),
                       ((wo, io["wo1"].rearrange("(h k) n -> k h n", k=P), wo_in),)))
        value_weights(nc, io, kr_h, kr_l, VO_h, VO_l, ahead[3], wo, wo_in, rope_first)
        inverse_deviations(nc, "cs", mv, rstd)

        y = m.sb("y", [P, TPB, D])
        yT_h, yT_l = m.sb("yT_h", [P, DC, S], F32R), m.sb("yT_l", [P, DC, S], F32R)
        qk = [m.sb(f"qk{i}", [P, 2 * S], F32R) for i in range(2)]
        k_lo = m.sb("k_lo", [P, S], F32R)
        own, other = (slice(0, R1), slice(R1, P)), (slice(R1, P), slice(0, R1))
        neg_max, sums, inv = m.sb("neg_max", [P, 4]), m.sb("sums", [P, 4]), m.sb("inv", [P, 4])
        probs = [store.place(f"probs1_{i}", 16 + i, [P, 4, S]) for i in range(2)]
        pT_h, pT_l = m.sb("pT_h", [P, 2, 2 * S], F32R), m.sb("pT_l", [P, 2, 2 * S], F32R)
        c_h, c_l = (store.place(name, at, [P, 2 * S], F32R) for name, at in (("c1_h", 26), ("c1_l", 27)))
        stats, new_mv = m.sb("stats", [P, TPB, 6]), m.sb("new_mv", [P, TPB, 2])

        score = [m.ps(f"score{i}", [P, 2, S]) for i in range(2)]
        turn = [m.ps(f"turn{i}", [P, 2 * S]) for i in range(2)]
        bank_a, bank_b = m.ps("bank_a", [P, D]), m.ps("bank_b", [P, D])
        acc = [m.ps(f"acc{i}", [P, D]) for i in range(TPB)]

        y_ready = m.sem("y_ready")
        a_made, a_hi, a_free, a_copied = m.sem("a_made"), m.sem("a_hi"), m.sem("a_free"), m.sem("a_copied")
        b_made, b_hi, b_free = m.sem("b_made"), m.sem("b_hi"), m.sem("b_free")
        scored, maxed, exped, normed = m.sem("scored"), m.sem("maxed"), m.sem("exped"), m.sem("normed")
        turned, turn_hi, turn_lo = m.sem("turned"), m.sem("turn_hi"), m.sem("turn_lo")
        outed, added = m.sem("outed"), m.sem("added")
        LASTP = PAIRS - 1

        def a_no(b, slot, what):
            if slot == -1:
                return ("lnt", "proj").index(what)
            return b * 9 + 2 + slot + (1 if slot == LASTP and what == "proj" else 0)

        def b_no(b, slot, what, last=False):
            if slot == -1:
                return 0
            return b * 9 + slot + (1 if slot == LASTP and what == "pv" and not last else 0)

        def first(n):
            return isinstance(n, int) and n <= 0

        def all_slots(slots):
            def run(eng):
                slots(0, 0, True, False)
                with eng.Fori(0, (B - 2) // 2) as r:
                    slots(2 * r + 1, 1, False, False)
                    slots(2 * r + 2, 0, False, False)
                slots(B - 1, (B - 1) % 2, False, True)
            return run

        with m.block() as block:
            @block.sync
            def _(sp):
                for dst, name in zip(expert_raw, ("wd", "wu", "iota")):
                    src = io[name].rearrange("(c p) n -> p c n", p=P) if name == "wd" else io[name]
                    sp.dma_start(dst[:], src).then_inc(expert_in, DMA)
                with sp.Fori(1, B) as b:
                    sp.wait_ge(kv_ready, b)
                    sp.dma_start(ctx_raw[:], io["ctx1"][bass.ds(b, 1), :, :, :].rearrange("b p a s -> p (b a) s")
                                 ).then_inc(ctx_in, DMA)

            @block.gpsimd
            def _(pool):
                def rope(b, par):
                    if not isinstance(b, int) or b >= 2:
                        pool.wait_ge(b_made, b_no(b - 1, 0, "pv") + 1)
                    make_rope(pool, b, par)

                rope(1, 1)
                with pool.Fori(1, B // 2) as r:
                    rope(2 * r, 0)
                    rope(2 * r + 1, 1)

            @block.tensor
            def _(pe):
                def transpose_y(b, t):
                    bank, made = ((bank_a, a_made), (bank_b, b_made))[t]
                    pe.wait_ge(y_ready, b * TPB + t + 1)
                    for c in range(DC):
                        last = pe.transpose(bank[:, c * P:(c + 1) * P], y[:, t, c * P:(c + 1) * P], ident[:, :])
                    last.then_inc(made, 1)

                def project(par, p, n):
                    pe.wait_ge(a_free, n)
                    cols = slice(p * P, (p + 1) * P)
                    products(pe, bank_a[:, 0:S], [(A_h[:, c, cols], A_l[:, c, cols], yT_h[:, c, :], yT_l[:, c, :])
                                                  for c in range(DC)])
                    products(pe, bank_a[:, S:2 * S], [(kr_h[:, cols], kr_l[:, cols], kv_h[par][:, 1, :], kv_l[par][:, 1, :])]
                             ).then_inc(a_made, 1)

                def scores(b, p, n_proj):
                    pe.wait_ge(a_free, n_proj + 1)
                    pe.wait_ge(a_copied, b * PAIRS + p + 1)
                    if not first(b * PAIRS + p):
                        pe.wait_ge(exped, b * PAIRS + p)
                    for h in range(2):
                        for t in range(TPB):
                            q = slice(t * P, (t + 1) * P)
                            pe.matmul(score[h][:, t, :], qk[h][:, q], qk[h][:, S:2 * S], start=True, stop=False)
                            pe.matmul(score[h][:, t, :], qk[h][own[h], q], k_lo[own[h], :], start=False, stop=True
                                      ).then_inc(scored, 1)

                def transpose_probs(s, p):
                    pe.wait_ge(normed, s + 1)
                    for k in range(2):
                        if not first(s):
                            pe.wait_ge(turn_lo, 2 * s - 1 + k)
                        for hq in range(4):
                            last = pe.transpose(turn[k][:, hq * P:(hq + 1) * P], probs[p % 2][:, hq, k * P:(k + 1) * P], ident[:, :])
                        last.then_inc(turned, 1)

                def attend(s, par, n):
                    pe.wait_ge(b_free, n)
                    for k in range(2):
                        pe.wait_ge(turn_lo, 2 * s + k + 1)
                        kv = slice(k * P, (k + 1) * P)
                        pe.matmul(bank_b[:, :], kv_l[par][:, 0, kv], pT_h[:, k, :], start=k == 0, stop=False)
                        pe.matmul(bank_b[:, :], kv_h[par][:, 0, kv], pT_l[:, k, :], start=False, stop=False)
                        last = pe.matmul(bank_b[:, :], kv_h[par][:, 0, kv], pT_h[:, k, :], start=False, stop=k == 1)
                    last.then_inc(b_made, 1)

                def project_out(b, p, n_pv, tiles=range(TPB)):
                    pe.wait_ge(b_free, n_pv + 1)
                    if p == 0 and not first(b):
                        pe.wait_ge(added, b * TPB)
                    for t in tiles:
                        last = products(pe, acc[t][:, :], [(c_h[:, h * S + t * P:h * S + (t + 1) * P],
                                                            c_l[:, h * S + t * P:h * S + (t + 1) * P],
                                                            VO_h[:, 2 * p + h, :], VO_l[:, 2 * p + h, :]) for h in range(2)],
                                        start=p == 0, stop=p == LASTP)
                        if p == LASTP:
                            last.then_inc(outed, 1)

                def slots(b, par, is_first, is_last):
                    for p in range(PAIRS):
                        s = b * PAIRS + p
                        n_proj = a_no(b, p - 1, "proj") if p > 0 else (1 if is_first else a_no(b - 1, LASTP, "proj"))
                        scores(b, p, n_proj)
                        if p == LASTP and not is_last:
                            pe.wait_ge(a_free, a_no(b, p, "lnt"))
                            transpose_y(b + 1, 0)
                            pe.wait_ge(b_free, b_no(b, p, "lnt"))
                            transpose_y(b + 1, 1)
                        if p > 0 or not is_first:
                            transpose_probs(s - 1, (p - 1) % 2)
                        if p < LASTP:
                            project(par, p + 1, a_no(b, p, "proj"))
                        if p >= 2:
                            project_out(b, p - 2, b_no(b, p - 1, "pv"), range(1 if p == LASTP and not is_last else TPB))
                        elif not is_first:
                            project_out(b - 1, PAIRS - 2 + p, b_no(b - 1, LASTP, "pv") if p == 0 else b_no(b, 0, "pv"))
                        if p == LASTP and not is_last:
                            pe.wait_ge(b_free, b_no(b, p, "lnt") + 1)
                            pe.wait_ge(kv_ready, b + 2)
                            project(1 - par, 0, a_no(b, p, "proj"))
                            project_out(b, p - 2, b_no(b, p - 1, "pv"), range(1, TPB))
                        if p > 0 or not is_first:
                            attend(s - 1, par if p > 0 else 1 - par, b_no(b, p, "pv", is_last))

                transpose_y(0, 0)
                transpose_y(0, 1)
                pe.wait_ge(b_free, 1)
                pe.wait_ge(kv_ready, 1)
                project(0, 0, 1)
                all_slots(slots)(pe)
                end = B - 1
                transpose_probs(B * PAIRS - 1, LASTP % 2)
                project_out(end, LASTP - 1, b_no(end, LASTP, "pv", True))
                attend(B * PAIRS - 1, end % 2, b_no(end, LASTP, "pv", True) + 1)
                project_out(end, LASTP, b_no(end, LASTP, "pv", True) + 1)

            @block.scalar
            def _(act):
                def split_y(t, n):
                    bank, made, hi = ((bank_a, a_made, a_hi), (bank_b, b_made, b_hi))[t]
                    act.wait_ge(made, n + 1)
                    act.activation(yT_h[:, :, t * P:(t + 1) * P], bank[:, :].rearrange("p (c t) -> p c t", c=DC), ACT.Copy
                                   ).then_inc(hi, 1)

                def split_proj(n):
                    act.wait_ge(a_made, n + 1)
                    for h in range(2):
                        last = act.activation(qk[h][own[h], :], bank_a[own[h], :], ACT.Copy)
                    last.then_inc(a_hi, 1)
                    act.drain()
                    for h in range(2):
                        last = act.activation(qk[h][other[h], S:2 * S], f32(qk[h][own[h], S:2 * S]), ACT.Copy)
                    last.then_inc(a_copied, 1)

                def split_context(n):
                    act.wait_ge(b_made, n + 1)
                    act.activation(c_h[:, :], bank_b[:, :], ACT.Copy).then_inc(b_hi, 1)

                def split_probs(s):
                    for k in range(2):
                        act.wait_ge(turned, 2 * s + k + 1)
                        act.activation(pT_h[:, k, :], turn[k][:, :], ACT.Copy).then_inc(turn_hi, 1)

                def exponentials(s, p, h):
                    if h == 0 and (not isinstance(s, int) or s >= 2):
                        act.wait_ge(turned, 2 * s - 2)
                    act.wait_ge(maxed, 2 * s + h + 1)
                    for t in range(TPB):
                        i = 2 * h + t
                        last = act.activation(probs[p % 2][:, i, :], score[h][:, t, :], ACT.Exp, bias=neg_max[:, i:i + 1],
                                              accum_out=sums[:, i:i + 1])
                    if h == 1:
                        last.then_inc(exped, 1)

                def slots(b, par, is_first, is_last):
                    for p in range(PAIRS):
                        s = b * PAIRS + p
                        if p == LASTP and not is_last:
                            split_y(0, a_no(b, p, "lnt"))
                            split_y(1, b_no(b, p, "lnt"))
                        if p > 0 or not is_first:
                            split_probs(s - 1)
                        exponentials(s, p, 0)
                        if p < LASTP:
                            split_proj(a_no(b, p, "proj"))
                        exponentials(s, p, 1)
                        if p == LASTP and not is_last:
                            split_proj(a_no(b, p, "proj"))
                        if p > 0 or not is_first:
                            split_context(b_no(b, p, "pv", is_last))

                split_y(0, 0)
                split_y(1, 0)
                split_proj(1)
                all_slots(slots)(act)
                split_probs(B * PAIRS - 1)
                split_context(b_no(B - 1, LASTP, "pv", True) + 1)

            @block.vector
            def _(dve):
                def normalise_y(b):
                    for t in range(TPB):
                        tile = b * TPB + t
                        dve.tensor_scalar(y[:, t, :], X[:, bass.ds(tile, 1), :].rearrange("p a d -> p (a d)"),
                                          mv[:, bass.ds(tile, 1), 0:1].rearrange("p a d -> p (a d)"),
                                          rstd[:, bass.ds(tile, 1)], ALU.subtract, ALU.mult).then_inc(y_ready, 1)

                def split_y(t, n):
                    bank, hi, free = ((bank_a, a_hi, a_free), (bank_b, b_hi, b_free))[t]
                    dve.wait_ge(hi, n + 1)
                    cols = slice(t * P, (t + 1) * P)
                    dve.tensor_tensor(yT_l[:, :, cols], bank[:, :].rearrange("p (c t) -> p c t", c=DC), f32(yT_h[:, :, cols]),
                                      ALU.subtract).then_inc(free, 1)

                def split_proj(n):
                    dve.wait_ge(a_hi, n + 1)
                    for h in range(2):
                        dve.tensor_tensor(qk[h][other[h], 0:S], bank_a[own[h], 0:S], f32(qk[h][own[h], 0:S]), ALU.subtract)
                    for h in range(2):
                        last = dve.tensor_tensor(k_lo[own[h], :], bank_a[own[h], S:2 * S], f32(qk[h][own[h], S:2 * S]),
                                                 ALU.subtract)
                    last.then_inc(a_free, 1)

                def split_context(n):
                    dve.wait_ge(b_hi, n + 1)
                    dve.tensor_tensor(c_l[:, :], bank_b[:, :], f32(c_h[:, :]), ALU.subtract).then_inc(b_free, 1)

                def split_probs(s):
                    for k in range(2):
                        dve.wait_ge(turn_hi, 2 * s + k + 1)
                        dve.tensor_tensor(pT_l[:, k, :], turn[k][:, :], f32(pT_h[:, k, :]), ALU.subtract).then_inc(turn_lo, 1)

                def maxima(s):
                    for h in range(2):
                        dve.wait_ge(scored, 4 * s + 2 * h + 2)
                        dve.tensor_reduce(neg_max[:, 2 * h:2 * h + 2], score[h][:, :, :], AX.X, ALU.max, negate=True
                                          ).then_inc(maxed, 1)

                def normalise(s, p):
                    dve.wait_ge(exped, s + 1)
                    dve.reciprocal(inv[:, :], sums[:, :])
                    dve.drain()
                    for i in range(4):
                        last = dve.tensor_scalar(probs[p % 2][:, i, :], probs[p % 2][:, i, :], inv[:, i:i + 1], None, ALU.mult)
                    last.then_inc(normed, 1)

                def add_output(b):
                    for t in range(TPB):
                        xt = X[:, bass.ds(b * TPB + t, 1), :].rearrange("p a d -> p (a d)")
                        dve.wait_ge(outed, b * TPB + t + 1)
                        dve.tensor_tensor(xt, xt, acc[t][:, :], ALU.add).then_inc(added, 1)

                def new_stats(b, t):
                    xt = X[:, bass.ds(b * TPB + t, 1), :].rearrange("p a d -> p (a d)")
                    tile_stats(dve, xt, stats[:, t, :], new_mv[:, t, :])
                    dve.drain()
                    dve.tensor_copy(mv[:, bass.ds(b * TPB + t, 1), :].rearrange("p a d -> p (a d)"), new_mv[:, t, :])

                def slots(b, par, is_first, is_last):
                    for p in range(PAIRS):
                        s = b * PAIRS + p
                        maxima(s)
                        if p == LASTP and not is_last:
                            split_y(0, a_no(b, p, "lnt"))
                            split_y(1, b_no(b, p, "lnt"))
                        if p > 0 or not is_first:
                            split_probs(s - 1)
                        if p < LASTP:
                            split_proj(a_no(b, p, "proj"))
                        normalise(s, p)
                        if p == LASTP and not is_last:
                            split_proj(a_no(b, p, "proj"))
                        if p == LASTP - 1 and not is_last:
                            normalise_y(b + 1)
                        if p > 0 or not is_first:
                            split_context(b_no(b, p, "pv", is_last))
                        if p == 1 and not is_first:
                            add_output(b - 1)
                        if p in (3, 4) and not is_first:
                            new_stats(b - 1, p - 3)

                normalise_y(0)
                split_y(0, 0)
                split_y(1, 0)
                split_proj(1)
                all_slots(slots)(dve)
                split_probs(B * PAIRS - 1)
                split_context(b_no(B - 1, LASTP, "pv", True) + 1)
                add_output(B - 1)
                dve.drain()
                for t in range(TPB):
                    new_stats(B - 1, t)



def layer1_experts(nc, out_dram, X, mv, rstd, ident, expert_raw, expert_in):
    GE, WIDTH = G + E, 256
    with Memory(nc, "d") as m:
        wd, wu, iota = expert_raw
        wd_h, wd_l = m.sb("wd_h", [P, DC, WIDTH], F32R), m.sb("wd_l", [P, DC, WIDTH], F32R)
        wu_h, wu_l = m.sb("wu_h", [P, D], F32R), m.sb("wu_l", [P, D], F32R)
        inverse_deviations(nc, "ds", mv, rstd)

        y = m.sb("y", [P, TPB, D])
        yT_h, yT_l = m.sb("yT_h", [P, TPB, DC, P], F32R), m.sb("yT_l", [P, TPB, DC, P], F32R)
        neg_max, sums = m.sb("neg_max", [P, TPB]), m.sb("sums", [P, TPB])
        weight, top, index = m.sb("weight", [P, TPB, E]), m.sb("top", [P, TPB, 8]), m.sb("index", [P, TPB, 8], U32)
        index_f, mask, gate = m.sb("index_f", [P, TPB, 8]), m.sb("mask", [P, TPB, E]), m.sb("gate", [P, TPB, E])
        act_h = m.sb("act_h", [P, TPB, G])
        g_h, g_l = m.sb("g_h", [P, TPB * P], F32R), m.sb("g_l", [P, TPB * P], F32R)
        turn = m.ps("turn", [P, TPB, DC, P])
        hidden = [m.ps(f"hidden{i}", [P, TPB, S]) for i in range(2)]
        turn_g = m.ps("turn_g", [P, 4 * P])
        up = m.ps("up", [P, TPB, D])
        y_ready, turned, y_hi, y_lo = m.sem("y_ready"), m.sem("turned"), m.sem("y_hi"), m.sem("y_lo")
        hid, acted, maxed, exped = m.sem("hid"), m.sem("acted"), m.sem("maxed"), m.sem("exped")
        g_ready, g_turned, g_hi, g_lo = m.sem("g_ready"), m.sem("g_turned"), m.sem("g_hi"), m.sem("g_lo")
        upped, added, stored = m.sem("upped"), m.sem("added"), m.sem("stored")
        w_hi, w_lo = m.sem("w_hi"), m.sem("w_lo")

        def after(eng, sem, n):
            if not isinstance(n, int) or n > 0:
                eng.wait_ge(sem, n)

        def all_steps(eng, step):
            for b in range(-3, 1):
                step(b, b % 2, b)
            with eng.Fori(0, (B - 4) // 2) as r:
                step(2 * r + 1, 1, None)
                step(2 * r + 2, 0, None)
            for b in range(B - 3, B + 1):
                step(b, b % 2, b)

        def has(at, ahead):
            return at is None or 0 <= at + ahead < B

        with m.block() as block:
            @block.sync
            def _(sp):
                dst = out_dram.rearrange("(t p) d -> p t d", p=P)
                with sp.Fori(0, B) as b:
                    sp.wait_ge(added, b * TPB + TPB)
                    sp.dma_start(dst[:, bass.ds(b * TPB, TPB), :], X[:, bass.ds(b * TPB, TPB), :]).then_inc(stored, DMA)
                sp.wait_ge(stored, B * DMA)

            @block.tensor
            def _(pe):
                def step(b, par, at):
                    if has(at, 1):
                        pe.wait_ge(y_lo, b + 2)
                        if isinstance(b, int) and b == -1:
                            pe.wait_ge(w_lo, 2)
                        after(pe, acted, b)
                        for t in range(TPB):
                            last = products(pe, hidden[1 - par][:, t, :], [(yT_h[:, t, c, :], yT_l[:, t, c, :], wd_h[:, c, :], wd_l[:, c, :])
                                                                     for c in range(DC)])
                        last.then_inc(hid, 1)
                    if has(at, 2):
                        pe.wait_ge(y_ready, b + 3)
                        for t in range(TPB):
                            for c in range(DC):
                                last = pe.transpose(turn[:, t, c, :], y[:, t, c * P:(c + 1) * P], ident[:, :])
                        last.then_inc(turned, 1)
                    if has(at, -1):
                        pe.wait_ge(g_lo, b)
                        after(pe, added, (b - 1) * TPB)
                        for t in range(TPB):
                            tok = slice(t * P, (t + 1) * P)
                            last = products(pe, up[:, t, :], [(g_h[:, tok], g_l[:, tok], wu_h[:, :], wu_l[:, :])])
                        last.then_inc(upped, 1)
                    if has(at, 0):
                        pe.wait_ge(g_ready, b + 1)
                        after(pe, g_lo, b)
                        for t in range(TPB):
                            last = pe.transpose(turn_g[:, t * P:(t + 1) * P], act_h[:, t, :], ident[:, :])
                        last.then_inc(g_turned, 1)
                all_steps(pe, step)

            @block.scalar
            def _(act):
                def step(b, par, at):
                    if has(at, 2):
                        act.wait_ge(turned, b + 3)
                        act.activation(yT_h[:], turn[:], ACT.Copy).then_inc(y_hi, 1)
                    if has(at, 0):
                        act.wait_ge(g_turned, b + 1)
                        act.activation(g_h[:, :], turn_g[:, 0:TPB * P], ACT.Copy).then_inc(g_hi, 1)
                    if has(at, 1):
                        act.wait_ge(maxed, b + 2)
                        for t in range(TPB):
                            act.activation(weight[:, t, :], hidden[1 - par][:, t, G:GE], ACT.Exp, bias=neg_max[:, t:t + 1],
                                           accum_out=sums[:, t:t + 1])
                        act.drain().then_inc(exped, 1)
                        act.activation(act_h[:], hidden[1 - par][:, :, 0:G], ACT.Silu).then_inc(acted, 1)
                act.wait_ge(expert_in, 3 * DMA)
                act.activation(wd_h[:, :, GE:WIDTH], wd[:, :, 0:WIDTH - GE], ACT.Copy)
                act.activation(wd_h[:, :, 0:GE], wd[:], ACT.Copy).then_inc(w_hi, 1)
                act.activation(wu_h[:], wu[:], ACT.Copy).then_inc(w_hi, 1)
                all_steps(act, step)

            @block.vector
            def _(dve):
                def normalise_y(b):
                    after(dve, turned, b)
                    for t in range(TPB):
                        tile = b * TPB + t
                        last = dve.tensor_scalar(y[:, t, :], X[:, bass.ds(tile, 1), :].rearrange("p a d -> p (a d)"),
                                                 mv[:, bass.ds(tile, 1), 0:1].rearrange("p a d -> p (a d)"),
                                                 rstd[:, bass.ds(tile, 1)], ALU.subtract, ALU.mult)
                    last.then_inc(y_ready, 1)

                def gates(b):
                    dve.wait_ge(exped, b + 1)
                    dve.reciprocal(sums[:, :], sums[:, :])
                    dve.drain()
                    for t in range(TPB):
                        dve.tensor_scalar(weight[:, t, :], weight[:, t, :], sums[:, t:t + 1], None, ALU.mult)
                    dve.drain()
                    for t in range(TPB):
                        dve.max(top[:, t, :], weight[:, t, :])
                    dve.drain()
                    for t in range(TPB):
                        dve.max_index(index[:, t, :], top[:, t, :], weight[:, t, :])
                    dve.drain()
                    dve.tensor_copy(index_f[:], index[:])
                    dve.drain()
                    for t in range(TPB):
                        dve.tensor_scalar(mask[:, t, :], iota[:, :], index_f[:, t, 0:1], None, ALU.is_equal)
                    dve.drain()
                    for t in range(TPB):
                        dve.scalar_tensor_tensor(mask[:, t, :], iota[:, :], index_f[:, t, 1:2], mask[:, t, :],
                                                 ALU.is_equal, ALU.add)
                    dve.drain()
                    dve.tensor_tensor(gate[:], mask[:], weight[:], ALU.mult)
                    dve.drain()
                    dve.wait_ge(acted, b + 1)
                    units = act_h[:].rearrange("p t (e i) -> p (t e) i", e=E)
                    dve.tensor_tensor(units, units, gate[:].rearrange("p t e -> p (t e)").unsqueeze(2).broadcast_to([P, TPB * E, EI]),
                                      ALU.mult).then_inc(g_ready, 1)

                def split_weights():
                    dve.wait_ge(w_hi, 1)
                    dve.tensor_tensor(wd_l[:, :, GE:WIDTH], wd[:, :, 0:WIDTH - GE], f32(wd_h[:, :, GE:WIDTH]), ALU.subtract)
                    for n, (lo, raw, hi) in enumerate(((wd_l[:, :, 0:GE], wd, wd_h[:, :, 0:GE]), (wu_l, wu, wu_h))):
                        dve.wait_ge(w_hi, n + 1)
                        dve.tensor_tensor(lo[:], raw[:], f32(hi[:]), ALU.subtract).then_inc(w_lo, 1)

                def step(b, par, at):
                    if isinstance(b, int) and b == -2:
                        split_weights()
                    if has(at, 1):
                        dve.wait_ge(hid, b + 2)
                        dve.tensor_reduce(neg_max[:, :], hidden[1 - par][:, :, G:GE], AX.X, ALU.max, negate=True).then_inc(maxed, 1)
                    if has(at, 2):
                        dve.wait_ge(y_hi, b + 3)
                        dve.tensor_tensor(yT_l[:], turn[:], f32(yT_h[:]), ALU.subtract).then_inc(y_lo, 1)
                    if has(at, 0):
                        dve.wait_ge(g_hi, b + 1)
                        dve.tensor_tensor(g_l[:, :], turn_g[:, 0:TPB * P], f32(g_h[:, :]), ALU.subtract).then_inc(g_lo, 1)
                    if has(at, 3):
                        normalise_y(b + 3)
                    if has(at, 1):
                        gates(b + 1)
                    if has(at, -1):
                        dve.wait_ge(upped, b)
                        for t in range(TPB):
                            xt = X[:, bass.ds((b - 1) * TPB + t, 1), :].rearrange("p a d -> p (a d)")
                            dve.tensor_tensor(xt, xt, up[:, t, :], ALU.add).then_inc(added, 1)
                all_steps(dve, step)


def program(nc, io, out):
    with Memory(nc, "g") as g:
        X = g.sb("x", [P, TILES, D])
        mv = g.sb("mean_var", [P, TILES, 2])
        rstd = g.sb("rstd", [P, TILES])
        ident = g.sb("ident", [P, P])
        identb = g.sb("identb", [P, P], BF16)
        store = Store(nc, g, 28)
        w1_raw = store.place("w1_raw", 0, [P, DC, F])
        ahead = (store.place("wq1", 0, [P, H1, D]), store.place("kcq", 8, [P, H1, 3, P]),
                 store.place("wqr", 14, [P, H1, 3, R1]), store.place("kckv", 26, [P, H1, CTX]))
        w1_in, ahead_in = g.sem("w1_in"), g.sem("ahead_in")
        expert_raw = (g.sb("wd", [P, DC, G + E]), g.sb("wu", [P, D]), g.sb("iota", [P, E]))
        expert_in = g.sem("expert_in")
        layer0_attention(nc, io, X, mv, rstd, ident, identb, store, w1_raw, w1_in)
        layer0_feed_forward(nc, io, X, mv, rstd, identb, store, w1_raw, w1_in, ahead, ahead_in)
        layer1_attention(nc, io, X, mv, rstd, ident, store, ahead, ahead_in, expert_raw, expert_in)
        layer1_experts(nc, out, X, mv, rstd, ident, expert_raw, expert_in)



def arrays(x, ctx_512, L0_xattn_Wq, L0_xattn_Wkv_expand, L0_xattn_Wout, L0_ffn_W1, L0_ffn_W2, L1_xattn_Wq, L1_xattn_w_kc_q,
           L1_xattn_w_kc_kv, L1_xattn_W_qr, L1_xattn_W_kr, L1_xattn_Wo, L1_ffn_router_w, L1_ffn_down_w, L1_ffn_up_w):
    import numpy as np

    c = np.ascontiguousarray
    x, ctx = np.asarray(x), np.asarray(ctx_512)

    def tokens(a):
        return a.reshape(TPB, P, CTX).transpose(1, 0, 2).reshape(P, S)

    wo0 = np.asarray(L0_xattn_Wout).T.reshape(GROUPS, 4, HD0, D).transpose(1, 0, 2, 3).reshape(D, D)
    swapped = np.concatenate([ctx[..., CTX // 2:], ctx[..., :CTX // 2]], -1)
    ctx1 = np.stack([np.stack([tokens(ctx[b]), ctx[b].T, tokens(swapped[b]), swapped[b].T], 1) for b in range(B)])
    inv_freq = np.float32(1.0) / np.float32(10000.0) ** (np.arange(0, CTX, 2, dtype=np.float32) / np.float32(CTX))
    freqs = np.arange(S, dtype=np.float32)[:, None] * inv_freq[None, :]
    sin, cos = np.repeat(np.sin(freqs), 2, axis=-1), np.repeat(np.cos(freqs), 2, axis=-1)
    sin = sin * np.where(np.arange(CTX) < CTX // 2, -1, 1).astype(np.float32)
    table = np.stack([tokens(cos), cos.T, tokens(sin), sin.T], 1).astype(np.float32)
    causal = np.arange(P)[None, :] <= np.arange(P)[:, None]
    return {
        "x": c(x.reshape(B * S, D)),
        "ctxT": c(ctx.reshape(B * S, CTX).T),
        "wq0": c(np.asarray(L0_xattn_Wq).T),
        "wkv0": c(np.asarray(L0_xattn_Wkv_expand).T),
        "wo0": c(wo0),
        "ident": np.eye(P, dtype=np.float32),
        "mask": np.where(causal, 0.0, -2.0 ** 127).astype(np.float32),
        "w1": c(np.asarray(L0_ffn_W1).T),
        "w2": c(np.asarray(L0_ffn_W2).T),
        "kcq": c(np.asarray(L1_xattn_w_kc_q).transpose(0, 2, 1)),
        "wqr": c(L1_xattn_W_qr),
        "wq1": c(L1_xattn_Wq),
        "kckv": c(L1_xattn_w_kc_kv),
        "wo1": c(np.asarray(L1_xattn_Wo).T),
        "kr": c(np.asarray(L1_xattn_W_kr).transpose(1, 0, 2).reshape(CTX, H1 * R1)),
        "table": c(table),
        "ctx1": c(ctx1),
        "wd": c(np.concatenate([np.asarray(L1_ffn_down_w).reshape(E * EI, D).T, np.asarray(L1_ffn_router_w).T], 1)),
        "wu": c(np.asarray(L1_ffn_up_w).transpose(0, 2, 1).reshape(E * EI, D)),
        "iota": np.tile(np.arange(E, dtype=np.float32), (P, 1)),
    }


def kernel(**inputs):
    import concourse.bacc as bacc
    import numpy as np
    from concourse.bass_utils import run_bass_kernel_spmd

    nc = bacc.Bacc("TRN2", target_bir_lowering=False, num_devices=1)
    placed = arrays(**inputs)
    io = {n: nc.dram_tensor(f"in_{n}", a.shape, mybir.dt.from_np(a.dtype), kind="ExternalInput").ap()
          for n, a in placed.items()}
    out = nc.dram_tensor("out", (B * S, D), F32, kind="ExternalOutput").ap()
    program(nc, io, out)
    r = run_bass_kernel_spmd(nc, [{f"in_{n}": a for n, a in placed.items()}], core_ids=[0])
    return np.asarray(r.results[0]["out"]).reshape(B, S, D)
```
